# Optimizing a Trainium2 kernel written in Bass

```python
import numpy as np
import jax
import jax.numpy as jnp

def _softmax(x, axis=-1):
    return jax.nn.softmax(x, axis=axis)

def _gelu(x):
    return jax.nn.gelu(x, approximate=True)

def _silu(x):
    return jax.nn.silu(x)

def _sigmoid(x):
    return jax.nn.sigmoid(x)

def _layernorm(x, axis=-1, eps=1e-05):
    m = jnp.mean(x, axis=axis, keepdims=True)
    v = jnp.var(x, axis=axis, keepdims=True)
    return (x - m) / jnp.sqrt(v + eps)

def _scatter_add(tgt, idx, src, axis=0):
    return tgt.at[idx].add(src)

def _segment_sum(src, seg, n):
    return jax.ops.segment_sum(src, seg, n)
kernel_name = 'mk_vit_tower_cls_d2_tok_img1024_r4_51289d'

def setup_inputs(seed: int=0):
    np.random.seed(seed)
    _w = jnp.asarray

    def _rec_inputs():
        import jax
        import jax.numpy as jnp
        _rk = jax.random.key(seed)
        x = 7.22013e-05 + 1.00017 * jax.random.normal(jax.random.fold_in(_rk, 1), (4, 1, 512, 256), jnp.float32)
        cls_tok = 0.02 * jax.random.normal(jax.random.fold_in(_rk, 5), (1, 1, 256), jnp.float32)
        return (x, cls_tok)
    x, cls_tok = _rec_inputs()

    def _L0_tok_setup():
        import jax, jax.numpy as jnp
        import numpy as np
        import math
        EMBED_DIM = 256
        NUM_HEADS = 16
        HEAD_DIM = EMBED_DIM // NUM_HEADS
        INPUT_DIM = 256
        key = jax.random.key(seed)
        k_x, k_wqkv, k_wout = jax.random.split(key, 3)
        x = jax.random.normal(k_x, (4, 1, 512, INPUT_DIM), dtype=jnp.float32)

        def xavier(k, shape):
            fan_out, fan_in = shape
            bound = math.sqrt(6.0 / (fan_in + fan_out))
            return jax.random.uniform(k, shape, jnp.float32, -bound, bound)
        w_qkv = xavier(k_wqkv, (3 * EMBED_DIM, INPUT_DIM))
        b_qkv = jnp.zeros((3 * EMBED_DIM,), jnp.float32)
        w_out = xavier(k_wout, (EMBED_DIM, EMBED_DIM))
        b_out = jnp.zeros((EMBED_DIM,), jnp.float32)
        return {'x': x, 'w_qkv': w_qkv, 'b_qkv': b_qkv, 'w_out': w_out, 'b_out': b_out}
    _L0_tok_all = _L0_tok_setup()
    _L0_tok_in = {k: v for k, v in _L0_tok_all.items() if k in ('w_qkv', 'b_qkv', 'w_out', 'b_out')}
    del _L0_tok_all

    def _L0_attn_setup():
        import jax, jax.numpy as jnp
        import numpy as np
        ROPE_BASE = 2500
        B, L, D, NH = (2, 512, 256, 16)
        HD = D // NH

        def apply_rope(inputs, positions, base_frequency):
            head_dim = inputs.shape[-1]
            fraction = 2 * jnp.arange(0, head_dim // 2) / head_dim
            timescale = base_frequency ** fraction
            sinusoid = positions[..., None] / timescale[None, None, :]
            sinusoid = sinusoid[..., None, :]
            sin, cos = (jnp.sin(sinusoid), jnp.cos(sinusoid))
            first, second = jnp.split(inputs, 2, axis=-1)
            out = jnp.concatenate([first * cos - second * sin, second * cos + first * sin], axis=-1)
            return out.astype(inputs.dtype)
        key = jax.random.key(seed)
        ks = jax.random.split(key, 5)
        s = 0.02
        return {'x': jax.random.normal(ks[0], (B, L, D), jnp.float32), 'wq_w': jax.random.normal(ks[1], (D, D), jnp.float32) * s, 'wq_b': jnp.zeros((D,), jnp.float32), 'wk_w': jax.random.normal(ks[2], (D, D), jnp.float32) * s, 'wk_b': jnp.zeros((D,), jnp.float32), 'wv_w': jax.random.normal(ks[3], (D, D), jnp.float32) * s, 'wv_b': jnp.zeros((D,), jnp.float32), 'wo_w': jax.random.normal(ks[4], (D, D), jnp.float32) * s, 'wo_b': jnp.zeros((D,), jnp.float32)}
    _L0_attn_all = _L0_attn_setup()
    _L0_attn_in = {k: v for k, v in _L0_attn_all.items() if k in ('wq_w', 'wq_b', 'wk_w', 'wk_b', 'wv_w', 'wv_b', 'wo_w', 'wo_b')}
    del _L0_attn_all

    def _L0_ffn_setup():
        import jax, jax.numpy as jnp
        import numpy as np
        NUM_EXPERTS = 8
        TOP_K = 2
        MOE_DIM = 512

        def _moe_forward(x, moe_router, moe_w13, moe_w2):
            b, s, d = x.shape
            x_flat = x.reshape(b * s, d)
            router_logits = jnp.einsum('td,de->te', x_flat, moe_router)
            topk_logits, topk_idx = jax.lax.top_k(router_logits, TOP_K)
            topk_weights = jax.nn.softmax(topk_logits, axis=-1).astype(x.dtype)
            tokens = x_flat.shape[0]
            expert_ids = topk_idx.reshape(tokens * TOP_K)
            dispatch_weights = topk_weights.reshape(tokens * TOP_K)
            sort_idx = jnp.argsort(expert_ids, axis=0)
            token_ids = jnp.arange(tokens * TOP_K, dtype=jnp.int32) // TOP_K
            token_ids_sort = token_ids[sort_idx]
            x_sort = x_flat[token_ids_sort]
            w_sort = dispatch_weights[sort_idx].astype(x_flat.dtype)
            group_sizes = jnp.bincount(expert_ids, length=NUM_EXPERTS).astype(jnp.int32)
            w13_out = jax.lax.ragged_dot(x_sort, moe_w13, group_sizes)
            gate, up = jnp.split(w13_out, [MOE_DIM], axis=-1)
            hidden = jax.nn.silu(gate) * up
            out_dispatch = jax.lax.ragged_dot(hidden, moe_w2, group_sizes)
            out_flat = jnp.zeros_like(x_flat).at[token_ids_sort].add(out_dispatch * w_sort[:, None], mode='drop')
            return out_flat.reshape(b, s, d)
        key = jax.random.key(seed)
        k1, k2, k3, k4 = jax.random.split(key, 4)
        B, S, D = (4, 512, 256)
        x = jax.random.normal(k1, (B, S, D), dtype=jnp.float32)
        moe_router = jax.random.normal(k2, (D, NUM_EXPERTS), dtype=jnp.float32) * 0.02
        moe_w13 = jax.random.normal(k3, (NUM_EXPERTS, D, 2 * MOE_DIM), dtype=jnp.float32) * 0.02
        moe_w2 = jax.random.normal(k4, (NUM_EXPERTS, MOE_DIM, D), dtype=jnp.float32) * 0.02
        return {'x': x, 'moe_router': moe_router, 'moe_w13': moe_w13, 'moe_w2': moe_w2}
    _L0_ffn_all = _L0_ffn_setup()
    _L0_ffn_in = {k: v for k, v in _L0_ffn_all.items() if k in ('moe_router', 'moe_w13', 'moe_w2')}
    del _L0_ffn_all

    def _L1_attn_setup():
        import math
        import jax, jax.numpy as jnp
        import numpy as np
        D_MODEL = 256
        NUM_HEADS = 16
        D_HEAD = D_MODEL // NUM_HEADS
        K_S = 32
        B, N = (2, 512)

        def _attn(x, Wq, bq, Wk, bk, Wv, bv, Wo, bo):
            b, n, _ = x.shape
            q = (x @ Wq.T + bq).reshape(b, n, NUM_HEADS, D_HEAD).transpose(0, 2, 1, 3)
            k = (x @ Wk.T + bk).reshape(b, n, NUM_HEADS, D_HEAD).transpose(0, 2, 1, 3)
            v = (x @ Wv.T + bv).reshape(b, n, NUM_HEADS, D_HEAD).transpose(0, 2, 1, 3)
            scores = jnp.einsum('bhqd,bhkd->bhqk', q, k) / math.sqrt(D_HEAD)
            causal = jnp.triu(jnp.ones((n, n), dtype=bool), k=1)
            neg_inf = jnp.array(-jnp.inf, dtype=scores.dtype)
            scores = jnp.where(causal, neg_inf, scores)
            vals, idx = jax.lax.top_k(scores, K_S)
            masked = jnp.full_like(scores, -jnp.inf)
            masked = jnp.put_along_axis(masked, idx, vals, axis=-1, inplace=False)
            attn = jax.nn.softmax(masked, axis=-1)
            out = jnp.einsum('bhqk,bhkd->bhqd', attn, v)
            out = out.transpose(0, 2, 1, 3).reshape(b, n, D_MODEL)
            y = out @ Wo.T + bo
            return (y, attn.mean(axis=1))

        def _reference_tuple_inner(x, Wq, bq, Wk, bk, Wv, bv, Wo, bo):
            return _attn(x, Wq, bq, Wk, bk, Wv, bv, Wo, bo)
        key = jax.random.key(seed)
        ks = jax.random.split(key, 9)
        s = 1.0 / math.sqrt(D_MODEL)
        return {'x': jax.random.normal(ks[0], (B, N, D_MODEL), dtype=jnp.float32), 'Wq': jax.random.normal(ks[1], (D_MODEL, D_MODEL), dtype=jnp.float32) * s, 'bq': jnp.zeros((D_MODEL,), dtype=jnp.float32), 'Wk': jax.random.normal(ks[2], (D_MODEL, D_MODEL), dtype=jnp.float32) * s, 'bk': jnp.zeros((D_MODEL,), dtype=jnp.float32), 'Wv': jax.random.normal(ks[3], (D_MODEL, D_MODEL), dtype=jnp.float32) * s, 'bv': jnp.zeros((D_MODEL,), dtype=jnp.float32), 'Wo': jax.random.normal(ks[4], (D_MODEL, D_MODEL), dtype=jnp.float32) * s, 'bo': jnp.zeros((D_MODEL,), dtype=jnp.float32)}
    _L1_attn_all = _L1_attn_setup()
    _L1_attn_in = {k: v for k, v in _L1_attn_all.items() if k in ('Wq', 'bq', 'Wk', 'bk', 'Wv', 'bv', 'Wo', 'bo')}
    del _L1_attn_all

    def _L1_ffn_setup():
        import jax, jax.numpy as jnp
        import numpy as np
        B, S, H, F, E, K = (2, 512, 256, 1024, 8, 2)

        def _init_w(key, shape, fan_in):
            return jax.random.normal(key, shape, jnp.float32) * fan_in ** (-0.5)

        def _ffn(x, wi, bi, wo, bo):
            return jax.nn.selu(x @ wi + bi) @ wo + bo
        key = jax.random.key(seed)
        ks = jax.random.split(key, 6)
        return {'x': jax.random.normal(ks[0], (B, S, H), jnp.float32), 'gate_wi': _init_w(ks[1], (H, F), H), 'gate_bi': jnp.zeros((F,), jnp.float32), 'gate_wo': _init_w(ks[2], (F, H), F), 'gate_bo': jnp.zeros((H,), jnp.float32), 'exp_wi': _init_w(ks[3], (E, H, F), H), 'exp_bi': jnp.zeros((E, F), jnp.float32), 'exp_wo': _init_w(ks[4], (E, F, H), F), 'exp_bo': jnp.zeros((E, H), jnp.float32)}
    _L1_ffn_all = _L1_ffn_setup()
    _L1_ffn_in = {k: v for k, v in _L1_ffn_all.items() if k in ('gate_wi', 'gate_bi', 'gate_wo', 'gate_bo', 'exp_wi', 'exp_bi', 'exp_wo', 'exp_bo')}
    del _L1_ffn_all
    return {'x': x, 'cls_tok': cls_tok, 'L0_tok_w_qkv': _L0_tok_in['w_qkv'], 'L0_tok_b_qkv': _L0_tok_in['b_qkv'], 'L0_tok_w_out': _L0_tok_in['w_out'], 'L0_tok_b_out': _L0_tok_in['b_out'], 'L0_attn_wq_w': _L0_attn_in['wq_w'], 'L0_attn_wq_b': _L0_attn_in['wq_b'], 'L0_attn_wk_w': _L0_attn_in['wk_w'], 'L0_attn_wk_b': _L0_attn_in['wk_b'], 'L0_attn_wv_w': _L0_attn_in['wv_w'], 'L0_attn_wv_b': _L0_attn_in['wv_b'], 'L0_attn_wo_w': _L0_attn_in['wo_w'], 'L0_attn_wo_b': _L0_attn_in['wo_b'], 'L0_ffn_moe_router': _L0_ffn_in['moe_router'], 'L0_ffn_moe_w13': _L0_ffn_in['moe_w13'], 'L0_ffn_moe_w2': _L0_ffn_in['moe_w2'], 'L1_attn_Wq': _L1_attn_in['Wq'], 'L1_attn_bq': _L1_attn_in['bq'], 'L1_attn_Wk': _L1_attn_in['Wk'], 'L1_attn_bk': _L1_attn_in['bk'], 'L1_attn_Wv': _L1_attn_in['Wv'], 'L1_attn_bv': _L1_attn_in['bv'], 'L1_attn_Wo': _L1_attn_in['Wo'], 'L1_attn_bo': _L1_attn_in['bo'], 'L1_ffn_gate_wi': _L1_ffn_in['gate_wi'], 'L1_ffn_gate_bi': _L1_ffn_in['gate_bi'], 'L1_ffn_gate_wo': _L1_ffn_in['gate_wo'], 'L1_ffn_gate_bo': _L1_ffn_in['gate_bo'], 'L1_ffn_exp_wi': _L1_ffn_in['exp_wi'], 'L1_ffn_exp_bi': _L1_ffn_in['exp_bi'], 'L1_ffn_exp_wo': _L1_ffn_in['exp_wo'], 'L1_ffn_exp_bo': _L1_ffn_in['exp_bo']}

def reference(x, cls_tok, L0_tok_w_qkv, L0_tok_b_qkv, L0_tok_w_out, L0_tok_b_out, L0_attn_wq_w, L0_attn_wq_b, L0_attn_wk_w, L0_attn_wk_b, L0_attn_wv_w, L0_attn_wv_b, L0_attn_wo_w, L0_attn_wo_b, L0_ffn_moe_router, L0_ffn_moe_w13, L0_ffn_moe_w2, L1_attn_Wq, L1_attn_bq, L1_attn_Wk, L1_attn_bk, L1_attn_Wv, L1_attn_bv, L1_attn_Wo, L1_attn_bo, L1_ffn_gate_wi, L1_ffn_gate_bi, L1_ffn_gate_wo, L1_ffn_gate_bo, L1_ffn_exp_wi, L1_ffn_exp_bi, L1_ffn_exp_wo, L1_ffn_exp_bo):
    import jax
    import jax.numpy as jnp

    def _L0_tok_ref(x, w_qkv, b_qkv, w_out, b_out):
        import jax, jax.numpy as jnp
        import numpy as np
        import math
        EMBED_DIM = 256
        NUM_HEADS = 16
        HEAD_DIM = EMBED_DIM // NUM_HEADS
        INPUT_DIM = 256
        B, y, S, _ = x.shape
        qkv = jnp.einsum('bysd,ed->byse', x, w_qkv) + b_qkv
        qkv = qkv.reshape(B, S, NUM_HEADS, 3 * HEAD_DIM).transpose(0, 2, 1, 3)
        q, k, v = jnp.split(qkv, 3, axis=-1)
        logits = jnp.einsum('bhqd,bhkd->bhqk', q, k) / math.sqrt(HEAD_DIM)
        attn = jax.nn.softmax(logits, axis=-1)
        vals = jnp.einsum('bhqk,bhkd->bhqd', attn, v)
        vals = vals.transpose(0, 2, 1, 3).reshape(B, S, EMBED_DIM)
        return jnp.einsum('bse,oe->bso', vals, w_out) + b_out

    def _L0_attn_ref(x, wq_w, wq_b, wk_w, wk_b, wv_w, wv_b, wo_w, wo_b):
        import jax, jax.numpy as jnp
        import numpy as np
        ROPE_BASE = 2500
        B, L, D, NH = (2, 512, 256, 16)
        HD = D // NH

        def apply_rope(inputs, positions, base_frequency):
            head_dim = inputs.shape[-1]
            fraction = 2 * jnp.arange(0, head_dim // 2) / head_dim
            timescale = base_frequency ** fraction
            sinusoid = positions[..., None] / timescale[None, None, :]
            sinusoid = sinusoid[..., None, :]
            sin, cos = (jnp.sin(sinusoid), jnp.cos(sinusoid))
            first, second = jnp.split(inputs, 2, axis=-1)
            out = jnp.concatenate([first * cos - second * sin, second * cos + first * sin], axis=-1)
            return out.astype(inputs.dtype)
        b, l, _ = x.shape
        q = (x @ wq_w + wq_b).reshape(b, l, NH, HD)
        k = (x @ wk_w + wk_b).reshape(b, l, NH, HD)
        v = (x @ wv_w + wv_b).reshape(b, l, NH, HD)
        pos = jnp.arange(l)
        q = apply_rope(q, pos, ROPE_BASE)
        k = apply_rope(k, pos, ROPE_BASE)
        q = q.transpose(0, 2, 1, 3)
        k = k.transpose(0, 2, 1, 3)
        v = v.transpose(0, 2, 1, 3)
        scale = jnp.sqrt(jnp.asarray(HD, q.dtype))
        scores = jnp.einsum('bnqh,bnkh->bnqk', q, k) / scale
        causal = jnp.tril(jnp.ones((l, l), bool))
        scores = jnp.where(causal, scores, jnp.finfo(scores.dtype).min)
        attn = jax.nn.softmax(scores, axis=-1)
        ctx = jnp.einsum('bnqk,bnkh->bnqh', attn, v)
        ctx = ctx.transpose(0, 2, 1, 3).reshape(b, l, D)
        return ctx @ wo_w + wo_b

    def _L0_ffn_ref(x, moe_router, moe_w13, moe_w2):
        import jax, jax.numpy as jnp
        import numpy as np
        NUM_EXPERTS = 8
        TOP_K = 2
        MOE_DIM = 512

        def _moe_forward(x, moe_router, moe_w13, moe_w2):
            b, s, d = x.shape
            x_flat = x.reshape(b * s, d)
            router_logits = jnp.einsum('td,de->te', x_flat, moe_router)
            topk_logits, topk_idx = jax.lax.top_k(router_logits, TOP_K)
            topk_weights = jax.nn.softmax(topk_logits, axis=-1).astype(x.dtype)
            tokens = x_flat.shape[0]
            expert_ids = topk_idx.reshape(tokens * TOP_K)
            dispatch_weights = topk_weights.reshape(tokens * TOP_K)
            sort_idx = jnp.argsort(expert_ids, axis=0)
            token_ids = jnp.arange(tokens * TOP_K, dtype=jnp.int32) // TOP_K
            token_ids_sort = token_ids[sort_idx]
            x_sort = x_flat[token_ids_sort]
            w_sort = dispatch_weights[sort_idx].astype(x_flat.dtype)
            group_sizes = jnp.bincount(expert_ids, length=NUM_EXPERTS).astype(jnp.int32)
            w13_out = jax.lax.ragged_dot(x_sort, moe_w13, group_sizes)
            gate, up = jnp.split(w13_out, [MOE_DIM], axis=-1)
            hidden = jax.nn.silu(gate) * up
            out_dispatch = jax.lax.ragged_dot(hidden, moe_w2, group_sizes)
            out_flat = jnp.zeros_like(x_flat).at[token_ids_sort].add(out_dispatch * w_sort[:, None], mode='drop')
            return out_flat.reshape(b, s, d)
        return _moe_forward(x, moe_router, moe_w13, moe_w2)

    def _L1_attn_ref(x, Wq, bq, Wk, bk, Wv, bv, Wo, bo):
        import math
        import jax, jax.numpy as jnp
        import numpy as np
        D_MODEL = 256
        NUM_HEADS = 16
        D_HEAD = D_MODEL // NUM_HEADS
        K_S = 32
        B, N = (2, 512)

        def _attn(x, Wq, bq, Wk, bk, Wv, bv, Wo, bo):
            b, n, _ = x.shape
            q = (x @ Wq.T + bq).reshape(b, n, NUM_HEADS, D_HEAD).transpose(0, 2, 1, 3)
            k = (x @ Wk.T + bk).reshape(b, n, NUM_HEADS, D_HEAD).transpose(0, 2, 1, 3)
            v = (x @ Wv.T + bv).reshape(b, n, NUM_HEADS, D_HEAD).transpose(0, 2, 1, 3)
            scores = jnp.einsum('bhqd,bhkd->bhqk', q, k) / math.sqrt(D_HEAD)
            causal = jnp.triu(jnp.ones((n, n), dtype=bool), k=1)
            neg_inf = jnp.array(-jnp.inf, dtype=scores.dtype)
            scores = jnp.where(causal, neg_inf, scores)
            vals, idx = jax.lax.top_k(scores, K_S)
            masked = jnp.full_like(scores, -jnp.inf)
            masked = jnp.put_along_axis(masked, idx, vals, axis=-1, inplace=False)
            attn = jax.nn.softmax(masked, axis=-1)
            out = jnp.einsum('bhqk,bhkd->bhqd', attn, v)
            out = out.transpose(0, 2, 1, 3).reshape(b, n, D_MODEL)
            y = out @ Wo.T + bo
            return (y, attn.mean(axis=1))

        def _reference_tuple_inner(x, Wq, bq, Wk, bk, Wv, bv, Wo, bo):
            return _attn(x, Wq, bq, Wk, bk, Wv, bv, Wo, bo)
        return _reference_tuple_inner(x, Wq, bq, Wk, bk, Wv, bv, Wo, bo)[0]

    def _L1_ffn_ref(x, gate_wi, gate_bi, gate_wo, gate_bo, exp_wi, exp_bi, exp_wo, exp_bo):
        import jax, jax.numpy as jnp
        import numpy as np
        B, S, H, F, E, K = (2, 512, 256, 1024, 8, 2)

        def _init_w(key, shape, fan_in):
            return jax.random.normal(key, shape, jnp.float32) * fan_in ** (-0.5)

        def _ffn(x, wi, bi, wo, bo):
            return jax.nn.selu(x @ wi + bi) @ wo + bo
        Bb, Ss, Hh = x.shape
        xf = x.reshape(-1, Hh)
        gate_logits = _ffn(xf, gate_wi, gate_bi, gate_wo, gate_bo)
        topv, topi = jax.lax.top_k(gate_logits, K)
        topv = topv / jnp.sum(topv, axis=-1, keepdims=True)
        onehot = (topi[..., None] == jnp.arange(E)).astype(x.dtype)
        w = jnp.einsum('nk,nke->ne', topv, onehot)
        h = jax.nn.selu(jnp.einsum('nh,ehf->enf', xf, exp_wi) + exp_bi[:, None, :])
        out_e = jnp.einsum('enf,efh->enh', h, exp_wo) + exp_bo[:, None, :]
        out = jnp.einsum('enh,ne->nh', out_e, w)
        return out.reshape(Bb, Ss, Hh)
    h = _L0_tok_ref(x, L0_tok_w_qkv, L0_tok_b_qkv, L0_tok_w_out, L0_tok_b_out)
    h = jnp.concatenate([jnp.broadcast_to(cls_tok, (h.shape[0], 1, h.shape[2])), h], axis=1)
    h = h + _L0_attn_ref(_layernorm(h, axis=-1), L0_attn_wq_w, L0_attn_wq_b, L0_attn_wk_w, L0_attn_wk_b, L0_attn_wv_w, L0_attn_wv_b, L0_attn_wo_w, L0_attn_wo_b)
    h = h + _L0_ffn_ref(_layernorm(h, axis=-1), L0_ffn_moe_router, L0_ffn_moe_w13, L0_ffn_moe_w2)
    h = h + _L1_attn_ref(_layernorm(h, axis=-1), L1_attn_Wq, L1_attn_bq, L1_attn_Wk, L1_attn_bk, L1_attn_Wv, L1_attn_bv, L1_attn_Wo, L1_attn_bo)
    h = h + _L1_ffn_ref(_layernorm(h, axis=-1), L1_ffn_gate_wi, L1_ffn_gate_bi, L1_ffn_gate_wo, L1_ffn_gate_bo, L1_ffn_exp_wi, L1_ffn_exp_bi, L1_ffn_exp_wo, L1_ffn_exp_bo)
    return h

_drawn_inputs = setup_inputs


def setup_inputs(seed=0):
    import zlib

    import numpy as np

    out = dict(_drawn_inputs(seed))
    spreads = {'L0_tok_b_qkv': (0.0, 0.1),
     'L0_tok_b_out': (0.0, 0.1),
     'L0_attn_wq_b': (0.0, 0.8),
     'L0_attn_wk_b': (0.0, 0.8),
     'L0_attn_wv_b': (0.0, 0.1),
     'L0_attn_wo_b': (0.0, 0.1),
     'L1_attn_bq': (0.0, 0.296),
     'L1_attn_bk': (0.0, 2.0),
     'L1_attn_bv': (0.0, 0.1),
     'L1_attn_bo': (0.0, 0.1),
     'L1_ffn_gate_bi': (0.0, 2.0),
     'L1_ffn_gate_bo': (0.0, 0.556),
     'L1_ffn_exp_bi': (0.0, 2.0),
     'L1_ffn_exp_bo': (0.0, 2.0)}
    factors = {'L0_attn_wq_w': 7.082,
     'L0_attn_wk_w': 7.902,
     'L0_ffn_moe_router': 2.772,
     'L1_ffn_gate_wi': 4.254,
     'L1_ffn_gate_wo': 4.254,
     'L1_ffn_exp_wi': 2.909,
     'L1_ffn_exp_wo': 3.029}
    for name, (base, spread) in spreads.items():
        noise = np.random.default_rng([zlib.crc32(name.encode()), seed]).standard_normal(out[name].shape)
        drawn = base * np.exp(spread * noise) if base else spread * noise
        out[name] = jnp.asarray(drawn.astype(out[name].dtype))
    for name, factor in factors.items():
        out[name] = (out[name] * factor).astype(out[name].dtype)
    return out
```

```python
from contextlib import ExitStack, contextmanager

import numpy as np

import concourse.bass as bass
from concourse import mybir

F32 = mybir.dt.float32
BF16 = mybir.dt.bfloat16
U32 = mybir.dt.uint32
I32 = mybir.dt.int32
ALU = mybir.AluOpType
ACT = mybir.ActivationFunctionType
AX_X = mybir.AxisListType.X

P = 128
B = 4
S = 512
D = 256
DC = D // P
NH = 16
HD = D // NH
NQ = S // P
NT = B * NQ
G = 4
HG = NH // G
STRIP = 32
PARTS = 6
E = 8
EPS = 1e-5
MASKED = -1e30
TAKEN = -3e38
K_TOP = 32
TILES = (2 * (NT * P + B) - E) // P + E
NOWHERE = 1 << 16
HIDDEN = 1024
SELU_ALPHA = 1.6732632423543772
SELU_SCALE = 1.0507009873554805
QSCALE = 1.0 / float(np.sqrt(HD))


class Chip:

    def __init__(self, nc, stack):
        self.nc, self.stack = nc, stack
        self.stage_sems = []

    @contextmanager
    def stage(self):
        with ExitStack() as st:
            yield st
        sems, self.stage_sems = self.stage_sems, []
        self.nc.clear_and_free_semaphores(sems)
        self.nc.all_engine_barrier()

    def sbuf(self, stack, name, shape, dt):
        return stack.enter_context(self.nc.sbuf_tensor(name, shape, dt))

    def psum(self, stack, name, shape, dt=F32):
        return stack.enter_context(self.nc.psum_tensor(name, shape, dt))

    def sem(self, stack, name):
        sem = self.nc.alloc_semaphore(name)
        if stack is not self.stack:
            self.stage_sems.append(sem)
        return sem


def constants(c):
    nc = c.nc
    c.ident = c.sbuf(c.stack, "ident", [P, P], F32)
    c.ident_bf = c.sbuf(c.stack, "ident_bf", [P, P], BF16)
    c.mask_qk = c.sbuf(c.stack, "mask_qk", [P, P], BF16)
    c.mask_kq = c.sbuf(c.stack, "mask_kq", [P, P], BF16)
    c.pick_cls = c.sbuf(c.stack, "pick_cls", [B, B, P], F32)
    c.before = c.sbuf(c.stack, "before", [P, P], BF16)
    c.ones_bf = c.sbuf(c.stack, "ones_bf", [P, P], BF16)
    c.iota_e = c.sbuf(c.stack, "iota_e", [P, E], F32)
    c.iota_t = c.sbuf(c.stack, "iota_t", [P, TILES], F32)
    c.steps = c.sbuf(c.stack, "steps", [P, NT + 1], F32)
    c.valid = c.sbuf(c.stack, "valid", [P, NT + 1], F32)
    zeros = c.sbuf(c.stack, "zeros", [P, 1, D], F32)
    c.xs_clear = c.sem(c.stack, "xs_clear")
    with c.stage() as st:
        filled = c.sem(st, "const_filled")
        with nc.Block() as block:
            @block.sync
            def _(sp):
                sp.wait_ge(filled, 17)
                for xs in c.xs.values():
                    sp.dma_start(xs.rearrange("(p r) d -> p (r d)", p=P).rearrange("p (n w) -> p n w", w=D),
                                 zeros[:, :, :].broadcast_to([P, TILES, D])).then_inc(c.xs_clear, 16)

            @block.gpsimd
            def _(pool):
                pool.memset(c.ident[:, :], 0.0).then_inc(filled, 1)
                pool.memset(c.ident_bf[:, :], 0.0).then_inc(filled, 1)
                pool.memset(c.mask_qk[:, :], 0.0).then_inc(filled, 1)
                pool.memset(c.mask_kq[:, :], 0.0).then_inc(filled, 1)
                pool.memset(c.pick_cls[:, :, :], 0.0).then_inc(filled, 1)
                pool.wait_ge(filled, 5)
                for ident in (c.ident, c.ident_bf):
                    pool.affine_select(out=ident[:, :], in_=ident[:, :], compare_op=ALU.not_equal, fill=1.0,
                                       base=0, pattern=[[-1, P]], channel_multiplier=1).then_inc(filled, 1)
                pool.affine_select(out=c.mask_qk[:, :], in_=c.mask_qk[:, :], compare_op=ALU.is_ge, fill=MASKED,
                                   base=0, pattern=[[-1, P]], channel_multiplier=1).then_inc(filled, 1)
                pool.affine_select(out=c.mask_kq[:, :], in_=c.mask_kq[:, :], compare_op=ALU.is_ge, fill=MASKED,
                                   base=0, pattern=[[1, P]], channel_multiplier=-1).then_inc(filled, 1)
                pool.affine_select(out=c.pick_cls[:, :, :], in_=c.pick_cls[:, :, :], compare_op=ALU.not_equal,
                                   fill=1.0, base=0, pattern=[[-1, B], [0, P]],
                                   channel_multiplier=1).then_inc(filled, 1)
                pool.wait_ge(filled, 10)
                pool.memset(zeros[:, :, :], 0.0).then_inc(filled, 1)
                pool.memset(c.before[:, :], 1.0).then_inc(filled, 1)
                pool.memset(c.ones_bf[:, :], 1.0).then_inc(filled, 1)
                pool.memset(c.valid[:, :], 1.0).then_inc(filled, 1)
                pool.iota(c.iota_e[:, :], pattern=[[1, E]], base=0, channel_multiplier=0,
                          allow_small_or_imprecise_dtypes=True).then_inc(filled, 1)
                pool.iota(c.iota_t[:, :], pattern=[[1, TILES]], base=0, channel_multiplier=0,
                          allow_small_or_imprecise_dtypes=True).then_inc(filled, 1)
                pool.iota(c.steps[:, :], pattern=[[P, NT + 1]], base=0, channel_multiplier=0,
                          allow_small_or_imprecise_dtypes=True).then_inc(filled, 1)
                pool.wait_ge(filled, 17)
                pool.affine_select(out=c.before[:, :], in_=c.before[:, :], compare_op=ALU.is_gt, fill=0.0,
                                   base=0, pattern=[[1, P]], channel_multiplier=-1).then_inc(filled, 1)
                pool.affine_select(out=c.valid[:, NT:NT + 1], in_=c.valid[:, NT:NT + 1], compare_op=ALU.is_ge,
                                   fill=0.0, base=B - 1, pattern=[[0, 1]], channel_multiplier=-1).then_inc(filled, 1)
                pool.wait_ge(filled, 19)


def project(c, tag, w_dram, qkb_dram, vb_dram, cls, rope=None):
    nc = c.nc
    cols = (5 if rope else 3) * D
    turns = 2 if rope else 0
    with c.stage() as st:
        w = c.sbuf(st, f"{tag}_w", [P, DC, cols], F32)
        qkb = c.sbuf(st, f"{tag}_qkb", [P, DC, 4 if rope else 2], F32)
        vb = c.sbuf(st, f"{tag}_vb", [P, D], F32)
        full = c.sbuf(st, f"{tag}_full", [P, 2, S + 1], F32)
        rest = c.sbuf(st, f"{tag}_rest", [P, 2, S + 1], F32)
        hi = c.sbuf(st, f"{tag}_hi", [P, 2, S + 1], BF16)
        mid = c.sbuf(st, f"{tag}_mid", [P, 2, S + 1], BF16)
        lo = c.sbuf(st, f"{tag}_lo", [P, 2, S + 1], BF16)
        kcls = c.sbuf(st, f"{tag}_kcls", [P, DC, B], F32)
        va = c.sbuf(st, f"{tag}_va", [P, NQ, NH, STRIP], F32)
        if rope:
            cos = c.sbuf(st, f"{tag}_cos", [P, 2, S], F32)
            sin = c.sbuf(st, f"{tag}_sin", [P, 2, S], F32)
            turned = c.sbuf(st, f"{tag}_turned", [P, 2, S], F32)
            plain = c.sbuf(st, f"{tag}_plain", [P, 2, S], F32)
        ps = c.psum(st, f"{tag}_ps", [P, 2, S])
        ps_rot = c.psum(st, f"{tag}_ps_rot", [P, 2, S])
        ps_v = c.psum(st, f"{tag}_ps_v", [P, 2, S])
        ps_c = c.psum(st, f"{tag}_ps_c", [P, 2, S])
        w_in = c.sem(st, f"{tag}_w_in")
        cls_mm = c.sem(st, f"{tag}_cls_mm")
        cls_done = c.sem(st, f"{tag}_cls_done")
        tables = c.sem(st, f"{tag}_tables")
        qk_mm = c.sem(st, f"{tag}_qk_mm")
        full_ok = c.sem(st, f"{tag}_full_ok")
        turn_ok = c.sem(st, f"{tag}_turn_ok")
        hi_ok = c.sem(st, f"{tag}_hi_ok")
        rest_ok = c.sem(st, f"{tag}_rest_ok")
        mid_ok = c.sem(st, f"{tag}_mid_ok")
        lo_ok = c.sem(st, f"{tag}_lo_ok")
        stored = [c.sem(st, f"{tag}_stored{i}") for i in range(2)]
        v_mm = c.sem(st, f"{tag}_v_mm")
        v_ok = c.sem(st, f"{tag}_v_ok")
        v_ones = c.sem(st, f"{tag}_v_ones")
        v_out = c.sem(st, f"{tag}_v_out")
        n_in = 3 + (4 if rope else 0)
        step_stores = 16 * PARTS
        block = st.enter_context(nc.Block())

        def span(k):
            return slice(0 if cls and k // 2 == 1 else 1, S + 1)

        @block.sync
        def _(sp):
            for i in range(2):
                sp.sem_inc(stored[i], 16)
            sp.dma_start(w[:, :, :], w_dram).then_inc(w_in, 16)
            sp.dma_start(qkb[:, :, :], qkb_dram).then_inc(w_in, 16)
            sp.dma_start(vb[:, :], vb_dram.partition_broadcast(P)).then_inc(w_in, 16)
            if rope:
                for n, t in enumerate((cos, sin)):
                    for h in range(2):
                        sp.dma_start(t[:, h, :], rope[n]).then_inc(w_in, 16)
            for b in range(B):
                for k in range(4):
                    which, gg = k // 2, k % 2
                    order = ("hhhmml", "hmlhmh")[which]
                    dst = (c.qd, c.kd)[which]
                    for part, tile, ok in (("h", hi, hi_ok), ("m", mid, mid_ok), ("l", lo, lo_ok)):
                        sp.wait_ge(ok, b * 4 + k + 1)
                        for i in range(PARTS):
                            if order[i] == part:
                                at = 0 if which == 0 else span(k).start
                                sp.dma_start(dst[b, i, :, gg * 8:gg * 8 + 8, at:].rearrange("d h t -> h d t"),
                                             tile[:, k % 2, span(k)]).then_inc(stored[k % 2], 16)
            for i in range(2):
                sp.wait_ge(stored[i], 16 + B * 2 * step_stores)

        @block.tensor
        def _(pe):
            pe.wait_ge(w_in, 16 * n_in)
            if cls:
                for gg in range(DC):
                    for ch in range(DC):
                        pe.matmul(ps_c[:, 0, gg * B:gg * B + B], w[:, ch, D + gg * P:D + gg * P + P],
                                  c.xt[:, ch, :, 0], start=ch == 0, stop=ch == DC - 1)
                for ch in range(DC):
                    mm = pe.matmul(ps_c[0:B, 1, 0:D], c.xt[:, ch, :, 0], w[:, ch, 2 * D:3 * D],
                                   start=ch == 0, stop=ch == DC - 1)
                mm.then_inc(cls_mm, 1)
            with pe.Fori(0, B) as b:
                for k in range(4):
                    which, gg = k // 2, k % 2
                    pe.wait_ge(full_ok, b * 4 + (k + 1))
                    for ch in range(DC):
                        mm = pe.matmul(ps[:, k % 2, :], w[:, ch, which * D + gg * P:which * D + gg * P + P],
                                       c.xt[:, ch, b, 1:S + 1], start=ch == 0, stop=ch == DC - 1)
                    if rope:
                        at = (3 + which) * D + gg * P
                        for ch in range(DC):
                            mm = pe.matmul(ps_rot[:, k % 2, :], w[:, ch, at:at + P],
                                           c.xt[:, ch, b, 1:S + 1], start=ch == 0, stop=ch == DC - 1)
                    mm.then_inc(qk_mm, 1)
            for n in range(NT):
                b, t = n // NQ, n % NQ
                if n >= 2:
                    pe.wait_ge(v_ok, n - 1)
                for ch in range(DC):
                    mm = pe.matmul(ps_v[:, n % 2, 0:D], c.xt[:, ch, b, 1 + t * P:1 + t * P + P],
                                   w[:, ch, 2 * D:3 * D], start=ch == 0, stop=ch == DC - 1)
                mm.then_inc(v_mm, 1)

        @block.vector
        def _(dve):
            dve.sem_inc(full_ok, 2)
            dve.sem_inc(rest_ok, 2)
            dve.memset(va[:, :, :, :], 0.0).then_inc(v_ones, 1)
            dve.wait_ge(v_ones, 1)
            dve.memset(va[:, :, :, HD:HD + 1], 1.0).then_inc(v_ones, 1)
            dve.wait_ge(w_in, 16 * n_in)
            if cls:
                dve.wait_ge(cls_mm, 1)
                for gg in range(DC):
                    dve.tensor_scalar(kcls[:, gg, :], ps_c[:, 0, gg * B:gg * B + B], qkb[:, gg, 1:2], None,
                                      ALU.add).then_inc(cls_done, 1)
                dve.tensor_tensor(c.vcls[:, :], ps_c[0:B, 1, 0:D], vb[0:B, :], ALU.add).then_inc(cls_done, 1)
                dve.wait_ge(cls_done, DC + 1)
            if rope:
                dve.tensor_scalar(cos[:, 0, :], cos[:, 0, :], QSCALE, None, ALU.mult).then_inc(tables, 1)
                dve.tensor_scalar(sin[:, 0, :], sin[:, 0, :], QSCALE, None, ALU.mult).then_inc(tables, 1)
                dve.wait_ge(tables, 2)
            per_image = 4 * turns + (2 if cls else 0)
            with dve.Fori(0, B) as b:
                done = 0
                for k in range(4):
                    which, gg = k // 2, k % 2
                    dve.wait_ge(qk_mm, b * 4 + (k + 1))
                    dve.wait_ge(rest_ok, b * 4 + (k + 1))
                    dve.wait_ge(full_ok, b * 4 + (k + 1))
                    if cls and which == 1:
                        dve.tensor_copy(full[:, k % 2, 0:1], kcls[:, gg, bass.ds(b, 1)]).then_inc(turn_ok, 1)
                        done += 1
                    if rope:
                        dve.scalar_tensor_tensor(out=plain[:, k % 2, :], in0=ps[:, k % 2, :],
                                                 scalar=qkb[:, gg, which:which + 1], in1=cos[:, which, :],
                                                 op0=ALU.add, op1=ALU.mult).then_inc(turn_ok, 1)
                        dve.scalar_tensor_tensor(out=turned[:, k % 2, :], in0=ps_rot[:, k % 2, :],
                                                 scalar=qkb[:, gg, 2 + which:3 + which], in1=sin[:, which, :],
                                                 op0=ALU.add, op1=ALU.mult).then_inc(turn_ok, 1)
                        done += turns
                        dve.wait_ge(turn_ok, b * per_image + done)
                        dve.tensor_tensor(full[:, k % 2, 1:], plain[:, k % 2, :], turned[:, k % 2, :],
                                          ALU.add).then_inc(full_ok, 1)
                    else:
                        if cls and which == 1:
                            dve.wait_ge(turn_ok, b * per_image + done)
                        dve.tensor_scalar(full[:, k % 2, 1:], ps[:, k % 2, :], qkb[:, gg, which:which + 1],
                                          QSCALE if which == 0 else 1.0, ALU.add, ALU.mult).then_inc(full_ok, 1)
                    dve.wait_ge(full_ok, b * 4 + (k + 3))
                    dve.wait_ge(hi_ok, b * 4 + (k + 1))
                    dve.tensor_tensor(rest[:, k % 2, span(k)], full[:, k % 2, span(k)], hi[:, k % 2, span(k)],
                                      ALU.subtract).then_inc(rest_ok, 1)
            for n in range(NT):
                dve.wait_ge(v_mm, n + 1)
                if n == 0:
                    dve.wait_ge(v_ones, 2)
                if n % NQ == 0 and n:
                    dve.wait_ge(v_out, 16 * G * (n // NQ))
                dve.tensor_tensor(va[:, n % NQ, :, 0:HD],
                                  ps_v[:, n % 2, 0:D].rearrange("p (h d) -> p h d", d=HD),
                                  vb[:, :].rearrange("p (h d) -> p h d", d=HD), ALU.add).then_inc(v_ok, 1)

        @block.scalar
        def _(act):
            with act.Fori(0, B) as b:
                for k in range(4):
                    act.wait_ge(full_ok, b * 4 + (k + 3))
                    act.wait_ge(stored[k % 2], b * (2 * step_stores) + (16 + (k // 2) * step_stores))
                    act.activation(hi[:, k % 2, span(k)], full[:, k % 2, span(k)], ACT.Copy).then_inc(hi_ok, 1)
                    act.wait_ge(rest_ok, b * 4 + (k + 3))
                    act.activation(mid[:, k % 2, span(k)], rest[:, k % 2, span(k)], ACT.Copy).then_inc(mid_ok, 1)

        @block.gpsimd
        def _(pool):
            with pool.Fori(0, B) as b:
                for k in range(4):
                    pool.wait_ge(mid_ok, b * 4 + (k + 1))
                    pool.tensor_tensor(lo[:, k % 2, span(k)], rest[:, k % 2, span(k)], mid[:, k % 2, span(k)],
                                       ALU.subtract).then_inc(lo_ok, 1)
            for b in range(B):
                pool.wait_ge(v_ok, (b + 1) * NQ)
                for g in range(G):
                    pool.dma_start(c.vd[b, g], va[:, :, g * HG:g * HG + HG, :].rearrange("p n h s -> p n (h s)")
                                   ).then_inc(v_out, 16)
            pool.wait_ge(v_out, 16 * G * B)


def attend(c, tag, causal):
    nc = c.nc
    k0 = 1 if causal else 0
    dst_k = c.kd if causal else c.kd[:, :, :, :, 1:]
    units = NQ * HG
    with c.stage() as st:
        qs = [c.sbuf(st, f"{tag}_qs{i}", [P, HG, S], BF16) for i in range(2)]
        ks = [c.sbuf(st, f"{tag}_ks{i}", [P, HG, S + k0], BF16) for i in range(2)]
        vs = [c.sbuf(st, f"{tag}_vs{i}", [P, NQ, P], F32) for i in range(2)]
        et = c.sbuf(st, f"{tag}_et", [P, 2, HG, S], F32)
        pv_rows = c.sbuf(st, f"{tag}_pv_rows", [P, S], F32)
        rowmax = c.sbuf(st, f"{tag}_rowmax", [P, units], F32)
        top = c.sbuf(st, f"{tag}_top", [P, units], F32)
        neg = c.sbuf(st, f"{tag}_neg", [P, units, STRIP], BF16)
        neg_sum = c.sbuf(st, f"{tag}_neg_sum", [P, units], F32)
        cls_score = c.sbuf(st, f"{tag}_cls_score", [P, units], F32)
        p_cls = c.sbuf(st, f"{tag}_p_cls", [P, 2, units], F32)
        v_cls = c.sbuf(st, f"{tag}_v_cls", [P, B, D], F32)
        cls_part = c.sbuf(st, f"{tag}_cls_part", [P, NQ, HG, HD], F32)
        raw = c.sbuf(st, f"{tag}_raw", [P, NQ, HG, HD], F32)
        den = c.sbuf(st, f"{tag}_den", [P, units], F32)
        rden = c.sbuf(st, f"{tag}_rden", [P, units], F32)
        ps_st = c.psum(st, f"{tag}_ps_st", [P, HG, S])
        ps_s = c.psum(st, f"{tag}_ps_s", [P, 2, S])
        ps_pv = c.psum(st, f"{tag}_ps_pv", [P, S])
        ps_cls = c.psum(st, f"{tag}_ps_cls", [P, S])
        neg_t = ps_s[:, :, :].bitcast(BF16).rearrange("p a (h t) -> p (a h) t", t=S)
        ctx_t = ps_pv[:, :].rearrange("p (n h s) -> p n h s", h=HG, s=STRIP)

        loaded = [c.sem(st, f"{tag}_loaded{i}") for i in range(2)]
        ready = c.sem(st, f"{tag}_ready")
        vcls_mm = c.sem(st, f"{tag}_vcls_mm")
        cls_row = c.sem(st, f"{tag}_cls_row")
        s_mm = c.sem(st, f"{tag}_s_mm")
        max_ok = c.sem(st, f"{tag}_max_ok")
        chain = c.sem(st, f"{tag}_chain")
        neg_ok = c.sem(st, f"{tag}_neg_ok")
        sc_ok = c.sem(st, f"{tag}_sc_ok")
        nt_mm = c.sem(st, f"{tag}_nt_mm")
        nt_out = c.sem(st, f"{tag}_nt_out")
        pcls_ok = c.sem(st, f"{tag}_pcls_ok")
        st_mm = c.sem(st, f"{tag}_st_mm")
        exp_ok = c.sem(st, f"{tag}_exp_ok")
        pv_mm = c.sem(st, f"{tag}_pv_mm")
        pv_out = c.sem(st, f"{tag}_pv_out")
        bt_mm = c.sem(st, f"{tag}_bt_mm")
        fin_ok = c.sem(st, f"{tag}_fin_ok")
        block = st.enter_context(nc.Block())

        def keys(qt):
            return (qt + 1) * P if causal else S

        def q_from(kt):
            return kt * P if causal else 0

        @block.sync
        def _(sp):
            for s in range(B * G):
                b, g = s // G, s % G
                if s >= 2:
                    sp.wait_ge(pv_mm, 2 + NQ * (s - 1))
                heads = slice(g * HG, g * HG + HG)
                sp.dma_start(qs[s % 2][0:PARTS * HD, :, :],
                             c.qd[b, :, :, heads, :].rearrange("i d h t -> (i d) h t")).then_inc(loaded[s % 2], 16)
                sp.dma_start(ks[s % 2][0:PARTS * HD, :, :],
                             dst_k[b, :, :, heads, 0:S + k0].rearrange("i d h t -> (i d) h t")
                             ).then_inc(loaded[s % 2], 16)
                sp.dma_start(vs[s % 2][:, :, :], c.vd[b, g]).then_inc(loaded[s % 2], 16)

        @block.gpsimd
        def _(pool):
            pool.memset(neg[:, :, :], 0.0).then_inc(ready, 1)
            for i in range(2):
                pool.wait_ge(ready, 2 * i + 1)
                pool.memset(ks[i][PARTS * HD:P, :, :], 0.0).then_inc(ready, 1)
                pool.wait_ge(ready, 2 * i + 2)
                pool.memset(ks[i][PARTS * HD:PARTS * HD + 2, :, :], 1.0).then_inc(ready, 1)

        @block.tensor
        def _(pe):
            def score_units(b, g, qt):
                q, k = qs[g % 2], ks[g % 2]
                if qt == 0:
                    pe.wait_ge(loaded[g % 2], b * 96 + (48 * (g // 2) + 48))
                    pe.wait_ge(nt_out, b * 8 + (2 * g + 1))
                for h in range(HG):
                    u = qt * HG + h
                    pe.wait_ge(max_ok, b * (G * units) + (g * units + u + 1))
                    lhs = q[0:PARTS * HD, h, qt * P:qt * P + P]
                    if causal:
                        pe.matmul(ps_cls[:, u:u + 1], lhs, k[0:PARTS * HD, h, 0:1], start=True, stop=True)
                    mm = pe.matmul(ps_s[:, u % 2, 0:keys(qt)], lhs, k[0:PARTS * HD, h, k0:k0 + keys(qt)],
                                   start=True, stop=not causal)
                    if causal:
                        mm = pe.matmul(ps_s[:, u % 2, qt * P:qt * P + P], c.ident_bf[:, :], c.mask_qk[:, :],
                                       start=False, stop=True)
                    mm.then_inc(s_mm, 1)

            def turn_neg(b, g):
                pe.wait_ge(neg_ok, b * G + (g + 1))
                for u in range(units):
                    qt, h = u // HG, u % HG
                    mm = pe.transpose(neg_t[PARTS * HD:P, h, qt * P:qt * P + P], neg[:, u, :], c.ident_bf[:, :])
                mm.then_inc(nt_mm, 1)

            def second(b, g, kt):
                q, k = qs[g % 2], ks[g % 2]
                if kt == 0:
                    pe.wait_ge(nt_out, b * 8 + (2 * g + 3))
                for pr in range(2):
                    pe.wait_ge(exp_ok, b * (G * 8) + (g * 8 + 2 * kt + pr + 1))
                    for h in (2 * pr, 2 * pr + 1):
                        mm = pe.matmul(ps_st[:, h, q_from(kt):], k[:, h, k0 + kt * P:k0 + kt * P + P],
                                       q[:, h, q_from(kt):], start=True, stop=not causal)
                        if causal:
                            mm = pe.matmul(ps_st[:, h, kt * P:kt * P + P], c.ident_bf[:, :], c.mask_kq[:, :],
                                           start=False, stop=True)
                    mm.then_inc(st_mm, 1)

            def values(b, g, kt):
                pe.wait_ge(exp_ok, b * (G * 8) + (g * 8 + 2 * kt + 4))
                if kt == 0:
                    pe.wait_ge(fin_ok, b * G + (g + 1))
                for h in range(HG):
                    mm = pe.matmul(ps_pv[h * STRIP:h * STRIP + STRIP, q_from(kt):],
                                   vs[g % 2][:, kt, h * STRIP:h * STRIP + STRIP],
                                   et[:, kt % 2, h, q_from(kt):], start=kt == 0, stop=kt == NQ - 1)
                mm.then_inc(pv_mm, 1)

            def turn_back(b, g):
                pe.wait_ge(pv_out, b * G + (g + 1))
                for qt in range(NQ):
                    mm = pe.transpose(ps_pv[:, qt * P:qt * P + P], pv_rows[:, qt * P:qt * P + P], c.ident[:, :])
                mm.then_inc(bt_mm, 1)

            def step(b, g, more):
                nb, ng = (b, g + 1) if g + 1 < G else (b + 1, 0)
                second(b, g, 0)
                for kt in range(NQ):
                    if more:
                        score_units(nb, ng, kt)
                    if kt + 1 < NQ:
                        second(b, g, kt + 1)
                    values(b, g, kt)
                if more:
                    turn_neg(nb, ng)
                turn_back(b, g)

            pe.wait_ge(ready, 5)
            if causal:
                for b in range(B):
                    mm = pe.matmul(ps_st[:, b, 0:D], c.pick_cls[:, b, :], c.vcls[:, :], start=True, stop=True)
                mm.then_inc(vcls_mm, 1)
                pe.wait_ge(chain, 1)
            for qt in range(NQ):
                score_units(0, 0, qt)
            turn_neg(0, 0)
            with pe.Fori(0, B - 1) as b:
                for g in range(G):
                    step(b, g, True)
            for g in range(G):
                step(B - 1, g, g + 1 < G)

        @block.scalar
        def _(act):
            def cls_exp(b, g):
                act.wait_ge(sc_ok, b * G + (g + 1))
                if not (isinstance(b, int) and b == 0 and g == 0):
                    act.wait_ge(fin_ok, b * G + g)
                act.activation(p_cls[:, g % 2, :], cls_score[:, :], ACT.Exp).then_inc(pcls_ok, 1)

            def neg_copy(b, g):
                act.wait_ge(nt_mm, b * G + (g + 1))
                act.activation(qs[g % 2][PARTS * HD:P, 0:2, :], neg_t[PARTS * HD:P, 0:2, :], ACT.Copy
                               ).then_inc(nt_out, 1)

            def step(b, g, more):
                nb, ng = (b, g + 1) if g + 1 < G else (b + 1, 0)
                for kt in range(NQ):
                    act.wait_ge(pv_mm, b * (G * NQ) + (g * NQ + kt + 1))
                    for pr in range(2):
                        act.wait_ge(st_mm, b * (G * 8) + (g * 8 + 2 * kt + pr + 1))
                        act.activation(et[:, kt % 2, 2 * pr:2 * pr + 2, q_from(kt):],
                                       ps_st[:, 2 * pr:2 * pr + 2, q_from(kt):], ACT.Exp).then_inc(exp_ok, 1)
                if more and causal:
                    cls_exp(nb, ng)
                act.wait_ge(pv_mm, b * (G * NQ) + (g * NQ + NQ + 2))
                act.activation(pv_rows[:, :], ps_pv[:, :], ACT.Copy).then_inc(pv_out, 1)
                if more:
                    neg_copy(nb, ng)

            act.sem_inc(exp_ok, 2)
            if causal:
                cls_exp(0, 0)
            neg_copy(0, 0)
            with act.Fori(0, B - 1) as b:
                for g in range(G):
                    step(b, g, True)
            for g in range(G):
                step(B - 1, g, g + 1 < G)

        n_neg = 3 if causal else 1
        n_fin = 4 if causal else 1

        @block.vector
        def _(dve):
            def maxima(b, g, qt):
                if qt == 0 and not (isinstance(b, int) and b == 0 and g == 0):
                    dve.wait_ge(neg_ok, b * G + g)
                for h in range(HG):
                    u = qt * HG + h
                    dve.wait_ge(s_mm, b * (G * units) + (g * units + u + 1))
                    dve.tensor_reduce(rowmax[:, u:u + 1], ps_s[:, u % 2, 0:keys(qt)], AX_X, ALU.max
                                      ).then_inc(max_ok, 1)

            def negate(b, g, base):
                dve.wait_ge(max_ok, b * (G * units) + (g * units + units + 2))
                src = rowmax
                if causal:
                    dve.tensor_tensor(top[:, :], rowmax[:, :], ps_cls[:, 0:units], ALU.max).then_inc(chain, 1)
                    dve.wait_ge(chain, base + 1)
                    src = top
                dve.tensor_scalar(neg[:, :, 0], src[:, :], -1.0, None, ALU.mult).then_inc(chain, 1)
                dve.wait_ge(chain, base + (2 if causal else 1))
                dve.scalar_tensor_tensor(out=neg[:, :, 1], in0=src[:, :], scalar=-1.0, in1=neg[:, :, 0],
                                         op0=ALU.mult, op1=ALU.subtract).then_inc(neg_ok, 1)
                if causal:
                    dve.wait_ge(neg_ok, b * G + (g + 1))
                    dve.tensor_tensor(neg_sum[:, :], neg[:, :, 0], neg[:, :, 1], ALU.add).then_inc(chain, 1)
                    dve.wait_ge(chain, base + 3)
                    dve.wait_ge(pcls_ok, b * G + (g + 1))
                    dve.tensor_tensor(cls_score[:, :], ps_cls[:, 0:units], neg_sum[:, :], ALU.add
                                      ).then_inc(sc_ok, 1)
                dve.wait_ge(nt_mm, b * G + (g + 1))
                dve.tensor_copy(qs[g % 2][PARTS * HD:P, 2:4, :], neg_t[PARTS * HD:P, 2:4, :]).then_inc(nt_out, 1)

            def finish(b, g, base):
                dve.wait_ge(bt_mm, b * G + (g + 1))
                dve.wait_ge(fin_ok, b * G + (g + 1))
                pc = p_cls[:, g % 2, :]
                if causal:
                    dve.wait_ge(pcls_ok, b * G + (g + 2))
                    dve.tensor_tensor(cls_part[:, :, :, :],
                                      pc.rearrange("p (n h a) -> p n h a", n=NQ, a=1).broadcast_to([P, NQ, HG, HD]),
                                      v_cls[:, bass.ds(b, 1), g * HG * HD:(g + 1) * HG * HD].rearrange(
                                          "p a (h d) -> p a h d", d=HD).broadcast_to([P, NQ, HG, HD]),
                                      ALU.mult).then_inc(chain, 1)
                    dve.tensor_tensor(den[:, :].rearrange("p (n h) -> p n h", n=NQ), ctx_t[:, :, :, HD],
                                      pc.rearrange("p (n h) -> p n h", n=NQ), ALU.add).then_inc(chain, 1)
                    dve.wait_ge(chain, base + 2)
                    dve.reciprocal(rden[:, :], den[:, :]).then_inc(chain, 1)
                    dve.tensor_tensor(raw[:, :, :, :], ctx_t[:, :, :, 0:HD], cls_part[:, :, :, :], ALU.add
                                      ).then_inc(chain, 1)
                    dve.wait_ge(chain, base + 4)
                    src = raw[:, :, :, :]
                else:
                    dve.reciprocal(rden[:, :].rearrange("p (n h) -> p n h", n=NQ), ctx_t[:, :, :, HD]
                                   ).then_inc(chain, 1)
                    dve.wait_ge(chain, base + 1)
                    src = ctx_t[:, :, :, 0:HD]
                dve.tensor_tensor(
                    c.ctx[:, bass.ds(b * NQ, NQ), g * HG * HD:(g + 1) * HG * HD].rearrange("p n (h d) -> p n h d", d=HD),
                    src, rden[:, :].rearrange("p (n h a) -> p n h a", n=NQ, a=1).broadcast_to([P, NQ, HG, HD]),
                    ALU.mult).then_inc(fin_ok, 1)

            first = 1 if causal else 0
            per_step = n_neg + n_fin

            def step(b, g, more):
                nb, ng = (b, g + 1) if g + 1 < G else (b + 1, 0)
                at = b * (G * per_step) + (first + n_neg + g * per_step)
                if more:
                    for qt in range(NQ):
                        maxima(nb, ng, qt)
                    negate(nb, ng, at)
                    finish(b, g, at + n_neg)
                else:
                    finish(b, g, at)

            dve.sem_inc(max_ok, 2)
            dve.sem_inc(pv_mm, 2)
            dve.sem_inc(fin_ok, 1)
            dve.sem_inc(nt_out, 1)
            dve.sem_inc(pcls_ok, 1)
            if causal:
                dve.wait_ge(vcls_mm, 1)
                dve.tensor_copy(v_cls[:, :, :], ps_st[:, :, 0:D]).then_inc(chain, 1)
                dve.tensor_copy(c.ctx[0:B, NT, :], c.vcls[:, :]).then_inc(cls_row, 1)
            for qt in range(NQ):
                maxima(0, 0, qt)
            negate(0, 0, first)
            with dve.Fori(0, B - 1) as b:
                for g in range(G):
                    step(b, g, True)
            for g in range(G):
                step(B - 1, g, g + 1 < G)


def attend_top(c, tag):
    nc = c.nc
    units = NQ * HG
    pairs = units // 2
    rounds = K_TOP // 8
    ops = 2 * rounds
    WIDE = S + 1
    with c.stage() as st:
        qs = [c.sbuf(st, f"{tag}_qs{i}", [P, HG, S], BF16) for i in range(2)]
        ks = [c.sbuf(st, f"{tag}_ks{i}", [P, HG, WIDE], BF16) for i in range(2)]
        vs = [c.sbuf(st, f"{tag}_vs{i}", [P, NQ, P], F32) for i in range(2)]
        largest = c.sbuf(st, f"{tag}_largest", [P, 2, rounds, 8], F32)
        raw = c.sbuf(st, f"{tag}_raw", [P, 4, WIDE], F32)
        left = c.sbuf(st, f"{tag}_left", [P, 2, WIDE], F32)
        neg_max = c.sbuf(st, f"{tag}_neg_max", [P, 2], F32)
        e_all = c.sbuf(st, f"{tag}_e_all", [P, 2, WIDE], F32)
        e_left = c.sbuf(st, f"{tag}_e_left", [P, 2, WIDE], F32)
        prob = c.sbuf(st, f"{tag}_prob", [P, 2, HG, WIDE], F32)
        prob_t = c.sbuf(st, f"{tag}_prob_t", [P, 2, HG, S], F32)
        pv_rows = c.sbuf(st, f"{tag}_pv_rows", [P, P], F32)
        back = c.sbuf(st, f"{tag}_back", [P, HG, STRIP], F32)
        v_cls = c.sbuf(st, f"{tag}_v_cls", [P, B, D], F32)
        cls_part = c.sbuf(st, f"{tag}_cls_part", [P, HG, HD], F32)
        den = c.sbuf(st, f"{tag}_den", [P, NT, NH], F32)
        rden = c.sbuf(st, f"{tag}_rden", [P, NT, NH], F32)
        ps_s = c.psum(st, f"{tag}_ps_s", [P, 2, 2 * S])
        ps_t = c.psum(st, f"{tag}_ps_pt", [P, 2, S])
        ps_pv = c.psum(st, f"{tag}_ps_pv", [P, S])
        ps_back = c.psum(st, f"{tag}_ps_back", [P, S])

        loaded = [c.sem(st, f"{tag}_loaded{i}") for i in range(2)]
        vcls_mm = c.sem(st, f"{tag}_vcls_mm")
        vcls_ok = c.sem(st, f"{tag}_vcls_ok")
        s_mm = c.sem(st, f"{tag}_s_mm")
        raw_ok = c.sem(st, f"{tag}_raw_ok")
        pick = c.sem(st, f"{tag}_pick")
        neg_ok = c.sem(st, f"{tag}_neg_ok")
        all_ok = c.sem(st, f"{tag}_all_ok")
        left_ok = c.sem(st, f"{tag}_left_ok")
        prob_ok = c.sem(st, f"{tag}_prob_ok")
        t_mm = c.sem(st, f"{tag}_pt_mm")
        t_out = c.sem(st, f"{tag}_pt_out")
        pv_mm = c.sem(st, f"{tag}_pv_mm")
        pv_out = c.sem(st, f"{tag}_pv_out")
        bt_mm = c.sem(st, f"{tag}_bt_mm")
        back_ok = c.sem(st, f"{tag}_back_ok")
        part_ok = c.sem(st, f"{tag}_part_ok")
        fin_ok = c.sem(st, f"{tag}_fin_ok")
        scale_ok = c.sem(st, f"{tag}_scale_ok")
        block = st.enter_context(nc.Block())

        def keys(qt):
            return (qt + 1) * P

        def row(i, qt):
            return ps_s[:, i, S - 1:S + keys(qt)]

        def unit(b, g, u):
            return b * (G * units) + (g * units + u)

        def group(b, g, qt):
            return b * (G * NQ) + (g * NQ + qt)

        def picked(b, g, k, j, i):
            return b * (G * pairs * 2 * ops) + ((g * pairs + k) * 2 * ops + 2 * j + i + 1 + 4 * ops)

        @block.sync
        def _(sp):
            for s in range(B * G):
                b, g = s // G, s % G
                if s >= 2:
                    sp.wait_ge(pv_mm, 2 + NQ * (s - 1))
                heads = slice(g * HG, g * HG + HG)
                sp.dma_start(qs[s % 2][0:PARTS * HD, :, :],
                             c.qd[b, :, :, heads, :].rearrange("i d h t -> (i d) h t")).then_inc(loaded[s % 2], 16)
                sp.dma_start(ks[s % 2][0:PARTS * HD, :, :],
                             c.kd[b, :, :, heads, :].rearrange("i d h t -> (i d) h t")).then_inc(loaded[s % 2], 16)
                sp.dma_start(vs[s % 2][:, :, :], c.vd[b, g]).then_inc(loaded[s % 2], 16)

        @block.tensor
        def _(pe):
            def score_pair(b, g, k):
                q, kk = qs[g % 2], ks[g % 2]
                qt = 2 * k // HG
                if k == 0:
                    pe.wait_ge(loaded[g % 2], b * 96 + (48 * (g // 2) + 48))
                for i in range(2):
                    h = (2 * k + i) % HG
                    pe.wait_ge(raw_ok, unit(b, g, 2 * k + i + 1))
                    lhs = q[0:PARTS * HD, h, qt * P:qt * P + P]
                    pe.matmul(ps_s[:, i, S - 1:S], lhs, kk[0:PARTS * HD, h, 0:1], start=True, stop=True)
                    pe.matmul(ps_s[:, i, S:S + keys(qt)], lhs, kk[0:PARTS * HD, h, 1:1 + keys(qt)],
                              start=True, stop=False)
                    pe.matmul(ps_s[:, i, S + qt * P:S + qt * P + P], c.ident_bf[:, :], c.mask_qk[:, :],
                              start=False, stop=True).then_inc(s_mm, 1)

            def turn_pair(b, g, k):
                qt = 2 * k // HG
                for i in range(2):
                    u = 2 * k + i
                    pe.wait_ge(prob_ok, unit(b, g, u + 3))
                    pe.wait_ge(t_out, unit(b, g, u + 1))
                    for ch in range(qt + 1):
                        mm = pe.transpose(ps_t[:, i, ch * P:ch * P + P],
                                          prob[:, qt % 2, u % HG, 1 + ch * P:1 + ch * P + P], c.ident[:, :])
                    mm.then_inc(t_mm, 1)

            def values(b, g, qt):
                pe.wait_ge(t_out, unit(b, g, qt * HG + HG + 2))
                for ch in range(qt + 1):
                    for h in range(HG):
                        mm = pe.matmul(ps_pv[h * STRIP:h * STRIP + STRIP, 0:P],
                                       vs[g % 2][:, ch, h * STRIP:h * STRIP + STRIP],
                                       prob_t[:, qt % 2, h, ch * P:ch * P + P], start=ch == 0, stop=ch == qt)
                mm.then_inc(pv_mm, 1)
                pe.wait_ge(pv_out, group(b, g, qt + 1))
                pe.transpose(ps_back[:, 0:P], pv_rows[:, :], c.ident[:, :]).then_inc(bt_mm, 1)

            def step(b, g, more):
                for k in range(pairs):
                    if k + 1 < pairs:
                        score_pair(b, g, k + 1)
                    elif more:
                        score_pair(*((b, g + 1) if g + 1 < G else (b + 1, 0)), 0)
                    turn_pair(b, g, k)
                    if 2 * k % HG == HG - 2:
                        values(b, g, 2 * k // HG)

            for b in range(B):
                mm = pe.matmul(ps_s[:, b // 2, b % 2 * S:b % 2 * S + D], c.pick_cls[:, b, :], c.vcls[:, :],
                               start=True, stop=True)
            mm.then_inc(vcls_mm, 1)
            pe.wait_ge(vcls_ok, 2)
            score_pair(0, 0, 0)
            with pe.Fori(0, B - 1) as b:
                for g in range(G):
                    step(b, g, True)
            for g in range(G):
                step(B - 1, g, g + 1 < G)

        @block.scalar
        def _(act):
            def copy_pair(b, g, k):
                qt = 2 * k // HG
                for i in range(2):
                    act.wait_ge(s_mm, unit(b, g, 2 * k + i + 1))
                    act.wait_ge(pick, picked(b, g, k, 1, i) - 4 * ops)
                    act.wait_ge(all_ok, unit(b, g, 2 * k + i + 1))
                    act.activation(raw[:, 2 * (k % 2) + i, 0:1 + keys(qt)], row(i, qt), ACT.Copy
                                   ).then_inc(raw_ok, 1)

            def step(b, g, more):
                for k in range(pairs):
                    if k + 1 < pairs:
                        copy_pair(b, g, k + 1)
                    elif more:
                        copy_pair(*((b, g + 1) if g + 1 < G else (b + 1, 0)), 0)
                    qt = 2 * k // HG
                    w = 1 + keys(qt)
                    for i in range(2):
                        u = 2 * k + i
                        act.wait_ge(neg_ok, unit(b, g, u + 3))
                        act.wait_ge(prob_ok, unit(b, g, u + 1))
                        act.activation(e_all[:, i, 0:w], raw[:, 2 * (k % 2) + i, 0:w], ACT.Exp, bias=neg_max[:, i:i + 1]
                                       ).then_inc(all_ok, 1)
                    for i in range(2):
                        act.wait_ge(pick, picked(b, g, k, ops - 1, i))
                        act.activation(e_left[:, i, 0:w], left[:, i, 0:w], ACT.Exp, bias=neg_max[:, i:i + 1]
                                       ).then_inc(left_ok, 1)
                    for i in range(2):
                        u = 2 * k + i
                        act.wait_ge(t_mm, unit(b, g, u + 9))
                        act.wait_ge(pv_mm, group(b, g, qt + 1))
                        act.activation(prob_t[:, qt % 2, u % HG, 0:w - 1], ps_t[:, i, 0:w - 1], ACT.Copy
                                       ).then_inc(t_out, 1)
                    if 2 * k % HG == HG - 2:
                        act.wait_ge(pv_mm, group(b, g, qt + 3))
                        act.activation(pv_rows[:, :], ps_pv[:, 0:P], ACT.Copy).then_inc(pv_out, 1)
                        act.wait_ge(bt_mm, group(b, g, qt + 1))
                        act.wait_ge(fin_ok, group(b, g, qt + 1))
                        act.activation(back[:, :, :], ps_back[:, 0:P].rearrange("p (h s) -> p h s", s=STRIP),
                                       ACT.Copy).then_inc(back_ok, 1)

            act.sem_inc(raw_ok, 2)
            act.sem_inc(all_ok, 4)
            act.sem_inc(left_ok, 2)
            act.sem_inc(t_out, 2)
            act.wait_ge(vcls_ok, 2)
            copy_pair(0, 0, 0)
            with act.Fori(0, B - 1) as b:
                for g in range(G):
                    step(b, g, True)
            for g in range(G):
                step(B - 1, g, g + 1 < G)

        @block.gpsimd
        def _(pool):
            def step(b, g):
                for k in range(pairs):
                    qt = 2 * k // HG
                    w = 1 + keys(qt)
                    for i in range(2):
                        u = 2 * k + i
                        pool.wait_ge(pick, picked(b, g, k, 0, i))
                        pool.wait_ge(left_ok, unit(b, g, u + 1))
                        pool.nop(nofuse=True)
                        pool.tensor_scalar(neg_max[:, i:i + 1], largest[:, i, 0, 0:1], -1.0, None, ALU.mult
                                           ).then_inc(neg_ok, 1)
                    for i in range(2):
                        u = 2 * k + i
                        pool.wait_ge(left_ok, unit(b, g, u + 3))
                        pool.wait_ge(t_mm, unit(b, g, u + 1))
                        pool.wait_ge(fin_ok, group(b, g, qt + 1))
                        pool.tensor_tensor(prob[:, qt % 2, u % HG, 0:w], e_all[:, i, 0:w], e_left[:, i, 0:w],
                                           ALU.subtract).then_inc(prob_ok, 1)
                    if 2 * k % HG == HG - 2:
                        p_cls = prob[:, qt % 2, :, 0:1]
                        n = b * NQ + qt
                        pool.wait_ge(prob_ok, unit(b, g, qt * HG + HG + 2))
                        pool.nop(nofuse=True)
                        pool.tensor_tensor(cls_part[:, :, :], p_cls.broadcast_to([P, HG, HD]),
                                           v_cls[:, bass.ds(b, 1), g * HG * HD:(g + 1) * HG * HD].rearrange(
                                               "p a (h d) -> p (a h) d", d=HD), ALU.mult).then_inc(part_ok, 1)
                        pool.wait_ge(back_ok, group(b, g, qt + 1))
                        pool.wait_ge(part_ok, 2 * group(b, g, qt) + 1)
                        pool.nop(nofuse=True)
                        pool.tensor_tensor(den[:, bass.ds(n, 1), g * HG:g * HG + HG].rearrange("p a h -> p (a h)"),
                                           back[:, :, HD], prob[:, qt % 2, :, 0], ALU.add).then_inc(part_ok, 1)
                        pool.wait_ge(part_ok, 2 * group(b, g, qt) + 2)
                        pool.nop(nofuse=True)
                        pool.tensor_tensor(
                            c.ctx[:, bass.ds(n, 1), g * HG * HD:(g + 1) * HG * HD].rearrange("p a (h d) -> p (a h) d", d=HD),
                            back[:, :, 0:HD], cls_part[:, :, :], ALU.add).then_inc(fin_ok, 1)

            pool.sem_inc(prob_ok, 2)
            pool.sem_inc(fin_ok, 1)
            pool.wait_ge(vcls_ok, 2)
            with pool.Fori(0, B) as b:
                for g in range(G):
                    step(b, g)

        @block.vector
        def _(dve):
            def step(b, g):
                for k in range(pairs):
                    qt = 2 * k // HG
                    w = 1 + keys(qt)
                    for j in range(ops):
                        for i in range(2):
                            u = 2 * k + i
                            src = raw[:, 2 * (k % 2) + i, 0:w] if j < 2 else left[:, i, 0:w]
                            if j == 0:
                                dve.wait_ge(raw_ok, unit(b, g, u + 3))
                                dve.wait_ge(pick, picked(b, g, k, ops - 1, i) - 2 * ops)
                                dve.wait_ge(neg_ok, unit(b, g, u + 1))
                            else:
                                dve.wait_ge(pick, picked(b, g, k, j - 1, i))
                            if j == 1:
                                dve.wait_ge(left_ok, unit(b, g, u + 1))
                            dve.nop(nofuse=True)
                            if j % 2 == 0:
                                ins = dve.max(largest[:, i, j // 2, :], src)
                            else:
                                ins = dve.match_replace(left[:, i, 0:w], largest[:, i, j // 2, :], src, TAKEN)
                            ins.then_inc(pick, 1)

            dve.sem_inc(pick, 4 * ops)
            dve.sem_inc(neg_ok, 2)
            dve.sem_inc(t_mm, 8)
            dve.sem_inc(pv_mm, 2)
            dve.wait_ge(vcls_mm, 1)
            for i in range(2):
                dve.tensor_copy(v_cls[:, 2 * i:2 * i + 2, :], ps_s[:, i, :].rearrange("p (a n) -> p a n", a=2)[:, :, 0:D]
                                ).then_inc(vcls_ok, 1)
            dve.tensor_copy(c.ctx[0:B, NT, :], c.vcls[:, :]).then_inc(scale_ok, 1)
            with dve.Fori(0, B) as b:
                for g in range(G):
                    step(b, g)
            dve.wait_ge(fin_ok, 1 + B * G * NQ)
            dve.reciprocal(rden[:, :, :], den[:, :, :]).then_inc(scale_ok, 1)
            dve.wait_ge(scale_ok, 2)
            for n in range(NT):
                ctx_n = c.ctx[:, n, :].rearrange("p (h d) -> p h d", d=HD)
                dve.tensor_tensor(ctx_n, ctx_n,
                                  rden[:, n, :].rearrange("p (h a) -> p h a", a=1).broadcast_to([P, NH, HD]),
                                  ALU.mult).then_inc(scale_ok, 1)


def attend_out(c, tag, wo_dram, bo_dram, residual, cls):
    nc = c.nc
    tiles = NT + (1 if cls else 0)
    with c.stage() as st:
        wo = c.sbuf(st, f"{tag}_wo", [P, DC, D], F32)
        bo = c.sbuf(st, f"{tag}_bo", [P, D], F32)
        ctx_t = c.sbuf(st, f"{tag}_ctx_t", [P, 2, DC, P], F32)
        summed = c.sbuf(st, f"{tag}_summed", [P, 2, D], F32)
        ps_t = c.psum(st, f"{tag}_ps_t", [P, 2, S])
        ps_o = c.psum(st, f"{tag}_ps_o", [P, 2, S])
        w_in = c.sem(st, f"{tag}_wo_in")
        t_mm = c.sem(st, f"{tag}_t_mm")
        t_out = c.sem(st, f"{tag}_t_out")
        o_mm = c.sem(st, f"{tag}_o_mm")
        sum_ok = c.sem(st, f"{tag}_sum_ok")
        h_ok = c.sem(st, f"{tag}_h_ok")
        block = st.enter_context(nc.Block())

        def rows(n):
            return P if n < NT else B

        @block.sync
        def _(sp):
            sp.dma_start(wo[:, :, :], wo_dram).then_inc(w_in, 16)
            sp.dma_start(bo[:, :], bo_dram.partition_broadcast(P)).then_inc(w_in, 16)

        @block.tensor
        def _(pe):
            def turn(n):
                r = rows(n)
                if n >= 2:
                    pe.wait_ge(t_out, n - 1)
                for ch in range(DC):
                    mm = pe.transpose(ps_t[:, n % 2, ch * P:ch * P + r], c.ctx[0:r, n, ch * P:ch * P + P],
                                      c.ident[0:r, 0:r])
                mm.then_inc(t_mm, 1)

            turn(0)
            pe.wait_ge(w_in, 32)
            for n in range(tiles):
                if n + 1 < tiles:
                    turn(n + 1)
                pe.wait_ge(t_out, n + 1)
                if n >= 2:
                    pe.wait_ge(sum_ok, n - 1)
                for ch in range(DC):
                    mm = pe.matmul(ps_o[0:rows(n), n % 2, 0:D], ctx_t[:, n % 2, ch, 0:rows(n)], wo[:, ch, :],
                                   start=ch == 0, stop=ch == DC - 1)
                mm.then_inc(o_mm, 1)

        @block.scalar
        def _(act):
            for n in range(tiles):
                act.wait_ge(t_mm, n + 1)
                if n >= 2:
                    act.wait_ge(o_mm, n - 1)
                r = rows(n)
                act.activation(ctx_t[:, n % 2, :, 0:r],
                               ps_t[:, n % 2, 0:DC * P].rearrange("p (c t) -> p c t", c=DC)[:, :, 0:r],
                               ACT.Copy).then_inc(t_out, 1)

        @block.vector
        def _(dve):
            dve.wait_ge(w_in, 32)
            for n in range(tiles):
                r = rows(n)
                dve.wait_ge(o_mm, n + 1)
                if residual:
                    if n >= 2:
                        dve.wait_ge(h_ok, n - 1)
                    dve.tensor_tensor(summed[0:r, n % 2, :], ps_o[0:r, n % 2, 0:D], bo[0:r, :], ALU.add
                                      ).then_inc(sum_ok, 1)
                    dve.wait_ge(sum_ok, n + 1)
                    dve.tensor_tensor(c.h[0:r, n, :], c.h[0:r, n, :], summed[0:r, n % 2, :], ALU.add
                                      ).then_inc(h_ok, 1)
                else:
                    dve.tensor_tensor(c.h[0:r, n, :], ps_o[0:r, n % 2, 0:D], bo[0:r, :], ALU.add
                                      ).then_inc(sum_ok, 1)


def dispatch(c, tag, xn, idx):
    nc = c.nc
    n_all = NT + 1
    with c.stage() as st:
        chosen = c.sbuf(st, f"{tag}_chosen", [P, 2, n_all, E], F32)
        both = c.sbuf(st, f"{tag}_both", [P, n_all, E], BF16)
        base = c.sbuf(st, f"{tag}_base", [P, n_all + 1, E], F32)
        begin = c.sbuf(st, f"{tag}_begin", [P, E + 1], F32)
        tiles = c.sbuf(st, f"{tag}_tiles", [P, E], F32)
        over = c.sbuf(st, f"{tag}_over", [P, E, n_all], F32)
        slot = c.sbuf(st, f"{tag}_slot", [P, n_all, E], F32)
        slot_in = c.sbuf(st, f"{tag}_slot_in", [P, n_all, E], F32)
        mine = c.sbuf(st, f"{tag}_mine", [P, 2, n_all, E], F32)
        at = c.sbuf(st, f"{tag}_at", [P, 2, n_all], F32)
        has = c.sbuf(st, f"{tag}_has", [P, 2, n_all], F32)
        past = c.sbuf(st, f"{tag}_past", [P, TILES, E - 1], F32)
        owner_f = c.sbuf(st, f"{tag}_owner_f", [P, TILES], F32)
        ps_rank = c.psum(st, f"{tag}_ps_rank", [P, S])
        ps_total = c.psum(st, f"{tag}_ps_total", [P, S])
        both_ok = c.sem(st, f"{tag}_both_ok")
        rank_mm = c.sem(st, f"{tag}_rank_mm")
        chain = c.sem(st, f"{tag}_d_chain")
        row_ok = c.sem(st, f"{tag}_row_ok")
        sent = c.sem(st, f"{tag}_sent")
        block = st.enter_context(nc.Block())
        rank = ps_rank[:, 0:n_all * E].rearrange("p (n e) -> p n e", e=E)
        total = ps_total[:, 0:n_all * E].rearrange("p (n e) -> p n e", e=E)

        @block.vector
        def _(dve):
            done = [0]

            def then(ins):
                done[0] += 1
                ins.then_inc(chain, 1)
                dve.wait_ge(chain, done[0])

            for k in range(2):
                then(dve.tensor_tensor(chosen[:, k, :, :],
                                       c.iota_e[:, :].rearrange("p (a e) -> p a e", a=1).broadcast_to([P, n_all, E]),
                                       idx[:, :, k:k + 1].broadcast_to([P, n_all, E]), ALU.is_equal))
                then(dve.tensor_tensor(chosen[:, k, :, :], chosen[:, k, :, :],
                                       c.valid[:, :].rearrange("p (n a) -> p n a", a=1).broadcast_to([P, n_all, E]),
                                       ALU.mult))
            dve.tensor_tensor(both[:, :, :], chosen[:, 0, :, :], chosen[:, 1, :, :], ALU.add).then_inc(both_ok, 1)
            then(dve.memset(base[:, 0, :], 0.0))
            dve.wait_ge(rank_mm, 2)
            for n in range(n_all):
                then(dve.tensor_tensor(base[:, n + 1, :], base[:, n, :], total[:, n, :], ALU.add))
            then(dve.tensor_tensor(over[:, :, :],
                                   base[:, n_all, :].rearrange("p (e a) -> p e a", a=1).broadcast_to([P, E, n_all]),
                                   c.steps[:, :].rearrange("p (a n) -> p a n", a=1).broadcast_to([P, E, n_all]),
                                   ALU.is_gt))
            then(dve.tensor_reduce(tiles[:, :], over[:, :, :], AX_X, ALU.add))
            then(dve.memset(begin[:, 0:1], 0.0))
            for e in range(E):
                then(dve.tensor_tensor(begin[:, e + 1:e + 2], begin[:, e:e + 1], tiles[:, e:e + 1], ALU.add))
            then(dve.scalar_tensor_tensor(
                out=slot_in[:, :, :], in0=begin[:, 0:E].rearrange("p (a e) -> p a e", a=1).broadcast_to([P, n_all, E]),
                scalar=float(P), in1=base[:, 0:n_all, :], op0=ALU.mult, op1=ALU.add))
            then(dve.tensor_tensor(slot[:, :, :], slot_in[:, :, :], rank, ALU.add))
            for k in range(2):
                then(dve.tensor_tensor(mine[:, k, :, :], chosen[:, k, :, :], slot[:, :, :], ALU.mult))
            then(dve.tensor_reduce(at[:, :, :], mine[:, :, :, :], AX_X, ALU.add))
            then(dve.tensor_reduce(has[:, :, :], chosen[:, :, :, :], AX_X, ALU.add))
            then(dve.scalar_tensor_tensor(out=at[:, :, :], in0=has[:, :, :], scalar=-float(NOWHERE),
                                          in1=at[:, :, :], op0=ALU.mult, op1=ALU.add))
            dve.tensor_scalar(c.row[:, :, :], at[:, :, :], float(NOWHERE), None, ALU.add).then_inc(row_ok, 1)
            then(dve.tensor_tensor(past[:, :, :],
                                   c.iota_t[:, :].rearrange("p (t a) -> p t a", a=1).broadcast_to([P, TILES, E - 1]),
                                   begin[:, 1:E].rearrange("p (a e) -> p a e", a=1).broadcast_to([P, TILES, E - 1]),
                                   ALU.is_ge))
            then(dve.tensor_reduce(owner_f[:, :], past[:, :, :], AX_X, ALU.add))
            dve.tensor_copy(c.owner[:, :], owner_f[:, :]).then_inc(row_ok, 1)

        @block.tensor
        def _(pe):
            pe.wait_ge(both_ok, 1)
            pe.matmul(ps_rank[:, 0:n_all * E], c.before[:, :], both[:, :, :], start=True, stop=True
                      ).then_inc(rank_mm, 1)
            pe.matmul(ps_total[:, 0:n_all * E], c.ones_bf[:, :], both[:, :, :], start=True, stop=True
                      ).then_inc(rank_mm, 1)

        @block.gpsimd
        def _(pool):
            pool.wait_ge(row_ok, 1)
            pool.wait_ge(c.xs_clear, 16 * len(c.xs))
            for n in range(n_all):
                for k in range(2):
                    pool.indirect_dma_start(
                        out=c.xs[tag][:, :], out_offset=bass.IndirectOffsetOnAxis(ap=c.row[:, k, n:n + 1], axis=0),
                        in_=xn[:, n, :], in_offset=None, bounds_check=TILES * P - 1, oob_is_err=False
                    ).then_inc(sent, 16)
            pool.wait_ge(sent, 16 * 2 * n_all)


def run_gated_experts(c, tag, w_in_dram, w_out_dram, hidden):
    nc = c.nc
    wide = 2 * hidden
    HC = hidden // P
    with c.stage() as st:
        w1 = c.sbuf(st, f"{tag}_w1", [P, DC, E, wide], F32)
        w2 = c.sbuf(st, f"{tag}_w2", [P, HC, E, D], F32)
        rows = c.sbuf(st, f"{tag}_rows", [P, 2, D], F32)
        rows_t = c.sbuf(st, f"{tag}_rows_t", [P, 2, DC, P], F32)
        hid = c.sbuf(st, f"{tag}_hid", [P, 2, hidden], F32)
        hid_t = c.sbuf(st, f"{tag}_hid_t", [P, 2, HC, P], F32)
        y = c.sbuf(st, f"{tag}_y", [P, 2, D], F32)
        act_gate = c.sbuf(st, f"{tag}_act_gate", [P, 2, hidden], F32)
        ps_x = c.psum(st, f"{tag}_ps_x", [P, S])
        ps_h = c.psum(st, f"{tag}_ps_h", [P, 2, 2, S])
        ps_ht = c.psum(st, f"{tag}_ps_ht", [P, S])
        ps_y = c.psum(st, f"{tag}_ps_y", [P, S])
        w_in = c.sem(st, f"{tag}_ew_in")
        rows_in = [c.sem(st, f"{tag}_rows_in{i}") for i in range(2)]
        x_mm = c.sem(st, f"{tag}_x_mm")
        x_out = c.sem(st, f"{tag}_x_out")
        h_mm = c.sem(st, f"{tag}_h_mm")
        gate_ok = c.sem(st, f"{tag}_gate_ok")
        hid_ok = c.sem(st, f"{tag}_hid_ok")
        ht_mm = c.sem(st, f"{tag}_ht_mm")
        ht_out = c.sem(st, f"{tag}_ht_out")
        y_mm = c.sem(st, f"{tag}_y_mm")
        y_ok = c.sem(st, f"{tag}_y_ok")
        y_sent = [c.sem(st, f"{tag}_y_sent{i}") for i in range(2)]
        block = st.enter_context(nc.Block())

        @block.sync
        def _(sp):
            for i in range(2):
                sp.sem_inc(y_sent[i], 16)
            sp.dma_start(w1[:, :, :, :], w_in_dram).then_inc(w_in, 16)
            sp.dma_start(w2[:, :, :, :], w_out_dram).then_inc(w_in, 16)
            lag = 3
            for i in range(TILES + lag):
                if i < TILES:
                    if i >= 2:
                        sp.wait_ge(x_mm, i - 1)
                    sp.dma_start(rows[:, i % 2, :], c.xs[tag][i * P:(i + 1) * P, :]).then_inc(rows_in[i % 2], 16)
                j = i - lag
                if j >= 0:
                    sp.wait_ge(y_ok, j + 2)
                    sp.dma_start(c.ys[tag][j * P:(j + 1) * P, :], y[:, j % 2, :]).then_inc(y_sent[j % 2], 16)
            for i in range(2):
                sp.wait_ge(y_sent[i], 16 + 16 * (TILES // 2))

        @block.tensor
        def _(pe):
            def turn_rows(it, k):
                pe.wait_ge(rows_in[k % 2], it * 16 + 16 * (k // 2 + 1))
                pe.wait_ge(x_out, it * 2 + (k + 1))
                for ch in range(DC):
                    mm = pe.transpose(ps_x[:, ch * P:ch * P + P], rows[:, k % 2, ch * P:ch * P + P], c.ident[:, :])
                mm.then_inc(x_mm, 1)

            def first(it, k):
                e = pe.value_load(c.owner[0:1, bass.ds(it * 2 + k, 1)], min_val=0, max_val=E - 1)
                pe.wait_ge(x_out, it * 2 + (k + 2))
                pe.wait_ge(hid_ok, it * 2 + (k + 1))
                for half in range(2):
                    for ch in range(DC):
                        mm = pe.matmul(ps_h[:, k % 2, half, :], rows_t[:, k % 2, ch, :],
                                       w1[:, ch, bass.ds(e, 1), half * S:half * S + S].rearrange("p a n -> p (a n)"),
                                       start=ch == 0, stop=ch == DC - 1)
                mm.then_inc(h_mm, 1)

            def turn_hidden(it, k):
                pe.wait_ge(hid_ok, it * 2 + (k + 3))
                for j in range(HC):
                    mm = pe.transpose(ps_ht[:, j * P:j * P + P], hid[:, k % 2, j * P:(j + 1) * P], c.ident[:, :])
                mm.then_inc(ht_mm, 1)

            def second(it, k, e):
                pe.wait_ge(ht_out, it * 2 + (k + 1))
                pe.wait_ge(y_ok, it * 2 + (k + 1))
                for j in range(HC):
                    mm = pe.matmul(ps_y[:, 0:D], hid_t[:, k % 2, j, :],
                                   w2[:, j, bass.ds(e, 1), :].rearrange("p a n -> p (a n)"),
                                   start=j == 0, stop=j == HC - 1)
                mm.then_inc(y_mm, 1)

            def slot(it, k, more, more2):
                e = pe.value_load(c.owner[0:1, bass.ds(it * 2 + k, 1)], min_val=0, max_val=E - 1)
                if more:
                    first(it, k + 1)
                turn_hidden(it, k)
                if more2:
                    turn_rows(it, k + 2)
                second(it, k, e)

            turn_rows(0, 0)
            turn_rows(0, 1)
            pe.wait_ge(w_in, 32)
            first(0, 0)
            with pe.Fori(0, TILES // 2 - 1) as it:
                for k in range(2):
                    slot(it, k, True, True)
            slot(TILES // 2 - 1, 0, True, False)
            slot(TILES // 2 - 1, 1, False, False)

        @block.scalar
        def _(act):
            def rows_copy(it, k):
                act.wait_ge(x_mm, it * 2 + (k + 1))
                if not (isinstance(it, int) and it * 2 + k < 2):
                    act.wait_ge(h_mm, it * 2 + (k - 1))
                act.activation(rows_t[:, k % 2, :, :], ps_x[:, 0:DC * P].rearrange("p (c t) -> p c t", c=DC),
                               ACT.Copy).then_inc(x_out, 1)

            def gate(it, k):
                act.wait_ge(h_mm, it * 2 + (k + 1))
                act.wait_ge(hid_ok, it * 2 + (k + 1))
                act.activation(act_gate[:, k % 2, :], ps_h[:, k % 2, 0, :], ACT.Silu).then_inc(gate_ok, 1)

            def hidden_copy(it, k):
                act.wait_ge(ht_mm, it * 2 + (k + 1))
                act.wait_ge(y_mm, it * 2 + (k + 1))
                act.activation(hid_t[:, k % 2, :, :], ps_ht[:, :].rearrange("p (c t) -> p c t", c=HC),
                               ACT.Copy).then_inc(ht_out, 1)

            def slot(it, k, more, more2):
                if more:
                    gate(it, k + 1)
                hidden_copy(it, k)
                if more2:
                    rows_copy(it, k + 2)

            act.sem_inc(x_out, 1)
            act.sem_inc(y_mm, 2)
            rows_copy(0, 0)
            rows_copy(0, 1)
            gate(0, 0)
            with act.Fori(0, TILES // 2 - 1) as it:
                for k in range(2):
                    slot(it, k, True, True)
            slot(TILES // 2 - 1, 0, True, False)
            slot(TILES // 2 - 1, 1, False, False)

        @block.vector
        def _(dve):
            def combine(it, k):
                dve.wait_ge(h_mm, it * 2 + (k + 1))
                dve.wait_ge(gate_ok, it * 2 + (k + 1))
                if not (isinstance(it, int) and it * 2 + k < 2):
                    dve.wait_ge(ht_mm, it * 2 + (k - 1))
                dve.tensor_tensor(hid[:, k % 2, :], act_gate[:, k % 2, :], ps_h[:, k % 2, 1, :], ALU.mult
                                  ).then_inc(hid_ok, 1)

            def y_copy(it, k):
                dve.wait_ge(y_mm, it * 2 + (k + 3))
                dve.wait_ge(y_sent[k % 2], it * 16 + 16 * (k // 2 + 1))
                dve.tensor_copy(y[:, k % 2, :], ps_y[:, 0:D]).then_inc(y_ok, 1)

            def slot(it, k, more):
                if more:
                    combine(it, k + 1)
                y_copy(it, k)

            dve.sem_inc(hid_ok, 2)
            dve.sem_inc(y_ok, 1)
            combine(0, 0)
            with dve.Fori(0, TILES // 2 - 1) as it:
                for k in range(2):
                    slot(it, k, True)
            slot(TILES // 2 - 1, 0, True)
            slot(TILES // 2 - 1, 1, False)


def run_selu_experts(c, tag, w_in_dram, b_in_dram, w_out_dram, b_out_dram):
    nc = c.nc
    HC = HIDDEN // P
    with c.stage() as st:
        w1 = c.sbuf(st, f"{tag}_w1", [P, DC, E, HIDDEN], F32)
        w2 = c.sbuf(st, f"{tag}_w2", [P, HC, E, D], F32)
        b1 = c.sbuf(st, f"{tag}_b1", [P, HC, E], F32)
        b2 = c.sbuf(st, f"{tag}_b2", [P, E, D], F32)
        shift = c.sbuf(st, f"{tag}_shift", [P, 1], F32)
        rows = c.sbuf(st, f"{tag}_rows", [P, 2, D], F32)
        rows_t = c.sbuf(st, f"{tag}_rows_t", [P, 2, DC, P], F32)
        hid = c.sbuf(st, f"{tag}_hid", [P, 2, S], F32)
        pre = c.sbuf(st, f"{tag}_pre", [P, 2, S], F32)
        low = c.sbuf(st, f"{tag}_low", [P, 2, S], F32)
        grown = c.sbuf(st, f"{tag}_grown", [P, 2, S], F32)
        high = c.sbuf(st, f"{tag}_high", [P, 2, S], F32)
        hid_t = c.sbuf(st, f"{tag}_hid_t", [P, 2, S], F32)
        y = c.sbuf(st, f"{tag}_y", [P, 2, D], F32)
        ps_x = c.psum(st, f"{tag}_ps_x", [P, S])
        ps_h = c.psum(st, f"{tag}_ps_h", [P, 2, S])
        ps_ht = c.psum(st, f"{tag}_ps_ht", [P, 2, S])
        ps_y = c.psum(st, f"{tag}_ps_y", [P, S])
        w_in = c.sem(st, f"{tag}_ew_in")
        rows_in = [c.sem(st, f"{tag}_rows_in{i}") for i in range(2)]
        x_mm = c.sem(st, f"{tag}_x_mm")
        x_out = c.sem(st, f"{tag}_x_out")
        h_mm = c.sem(st, f"{tag}_h_mm")
        hid_ok = c.sem(st, f"{tag}_hid_ok")
        ht_mm = c.sem(st, f"{tag}_ht_mm")
        pre_ok = c.sem(st, f"{tag}_pre_ok")
        low_ok = c.sem(st, f"{tag}_low_ok")
        grown_ok = c.sem(st, f"{tag}_grown_ok")
        high_ok = c.sem(st, f"{tag}_high_ok")
        shift_ok = c.sem(st, f"{tag}_shift_ok")
        selu_ok = c.sem(st, f"{tag}_selu_ok")
        y_mm = c.sem(st, f"{tag}_y_mm")
        y_ok = c.sem(st, f"{tag}_y_ok")
        y_sent = [c.sem(st, f"{tag}_y_sent{i}") for i in range(2)]
        block = st.enter_context(nc.Block())

        def parts(it, k, part, more):
            return it * 4 + (2 * k + part + more)

        @block.sync
        def _(sp):
            for i in range(2):
                sp.sem_inc(y_sent[i], 16)
            for ch in range(DC):
                sp.dma_start(w1[:, ch, :, :], w_in_dram[:, ch]).then_inc(w_in, 16)
            sp.dma_start(w2[:, :, :, :], w_out_dram).then_inc(w_in, 16)
            sp.dma_start(b1[:, :, :], b_in_dram).then_inc(w_in, 16)
            sp.dma_start(b2[:, :, :], b_out_dram.partition_broadcast(P)).then_inc(w_in, 16)
            lag = 3
            for i in range(TILES + lag):
                if i < TILES:
                    if i >= 2:
                        sp.wait_ge(x_mm, i - 1)
                    sp.dma_start(rows[:, i % 2, :], c.xs[tag][i * P:(i + 1) * P, :]).then_inc(rows_in[i % 2], 16)
                j = i - lag
                if j >= 0:
                    sp.wait_ge(y_ok, j + 2)
                    sp.dma_start(c.ys[tag][j * P:(j + 1) * P, :], y[:, j % 2, :]).then_inc(y_sent[j % 2], 16)
            for i in range(2):
                sp.wait_ge(y_sent[i], 16 + 16 * (TILES // 2))

        @block.tensor
        def _(pe):
            def turn_rows(it, k):
                pe.wait_ge(rows_in[k % 2], it * 16 + 16 * (k // 2 + 1))
                pe.wait_ge(x_out, it * 2 + (k + 1))
                for ch in range(DC):
                    mm = pe.transpose(ps_x[:, ch * P:ch * P + P], rows[:, k % 2, ch * P:ch * P + P], c.ident[:, :])
                mm.then_inc(x_mm, 1)

            def first(it, k):
                e = pe.value_load(c.owner[0:1, bass.ds(it * 2 + k, 1)], min_val=0, max_val=E - 1)
                pe.wait_ge(x_out, it * 2 + (k + 2))
                for part in range(2):
                    pe.wait_ge(hid_ok, parts(it, k, part, 1))
                    for ch in range(DC):
                        mm = pe.matmul(ps_h[:, part, :], rows_t[:, k % 2, ch, :],
                                       w1[:, ch, bass.ds(e, 1), part * S:part * S + S].rearrange("p a n -> p (a n)"),
                                       start=ch == 0, stop=ch == DC - 1)
                    mm.then_inc(h_mm, 1)

            def turn_hidden(it, k):
                for part in range(2):
                    pe.wait_ge(hid_ok, parts(it, k, part, 3))
                    pe.wait_ge(pre_ok, parts(it, k, part, 1))
                    for j in range(S // P):
                        mm = pe.transpose(ps_ht[:, part, j * P:j * P + P], hid[:, part, j * P:j * P + P],
                                          c.ident[:, :])
                    mm.then_inc(ht_mm, 1)

            def second(it, k):
                e = pe.value_load(c.owner[0:1, bass.ds(it * 2 + k, 1)], min_val=0, max_val=E - 1)
                pe.wait_ge(y_ok, it * 2 + (k + 1))
                for part in range(2):
                    pe.wait_ge(selu_ok, parts(it, k, part, 3))
                    for j in range(S // P):
                        kk = part * (S // P) + j
                        mm = pe.matmul(ps_y[:, 0:D], hid_t[:, part, j * P:j * P + P],
                                       w2[:, kk, bass.ds(e, 1), :].rearrange("p a n -> p (a n)"),
                                       start=kk == 0, stop=kk == HC - 1)
                mm.then_inc(y_mm, 1)

            def slot(it, k, more, more2):
                turn_hidden(it, k)
                if more:
                    first(it, k + 1)
                if more2:
                    turn_rows(it, k + 2)
                second(it, k)

            turn_rows(0, 0)
            turn_rows(0, 1)
            pe.wait_ge(w_in, 16 * (DC + 3))
            first(0, 0)
            with pe.Fori(0, TILES // 2 - 1) as it:
                for k in range(2):
                    slot(it, k, True, True)
            slot(TILES // 2 - 1, 0, True, False)
            slot(TILES // 2 - 1, 1, False, False)

        @block.scalar
        def _(act):
            def rows_copy(it, k):
                act.wait_ge(x_mm, it * 2 + (k + 1))
                if not (isinstance(it, int) and it * 2 + k < 2):
                    act.wait_ge(h_mm, it * 4 + (2 * k - 2))
                act.activation(rows_t[:, k % 2, :, :], ps_x[:, 0:DC * P].rearrange("p (c t) -> p c t", c=DC),
                               ACT.Copy).then_inc(x_out, 1)

            def hidden_copy(it, k):
                for part in range(2):
                    act.wait_ge(h_mm, parts(it, k, part, 1))
                    act.wait_ge(ht_mm, parts(it, k, part, 1))
                    act.activation(hid[:, part, :], ps_h[:, part, :], ACT.Copy).then_inc(hid_ok, 1)

            def grow(it, k):
                for part in range(2):
                    act.wait_ge(low_ok, parts(it, k, part, 3))
                    act.wait_ge(selu_ok, parts(it, k, part, 1))
                    act.activation(grown[:, part, :], low[:, part, :], ACT.Exp, bias=shift[:, 0:1]
                                   ).then_inc(grown_ok, 1)

            def slot(it, k, more, more2):
                grow(it, k)
                if more:
                    hidden_copy(it, k + 1)
                if more2:
                    rows_copy(it, k + 2)

            act.sem_inc(x_out, 1)
            act.sem_inc(hid_ok, 2)
            act.sem_inc(grown_ok, 2)
            rows_copy(0, 0)
            rows_copy(0, 1)
            hidden_copy(0, 0)
            with act.Fori(0, TILES // 2 - 1) as it:
                for k in range(2):
                    slot(it, k, True, True)
            slot(TILES // 2 - 1, 0, True, False)
            slot(TILES // 2 - 1, 1, False, False)

        @block.gpsimd
        def _(pool):
            pool.sem_inc(low_ok, 2)
            with pool.Fori(0, TILES // 2) as it:
                for k in range(2):
                    for part in range(2):
                        pool.wait_ge(pre_ok, parts(it, k, part, 3))
                        pool.wait_ge(grown_ok, parts(it, k, part, 1))
                        pool.nop(nofuse=True)
                        pool.tensor_scalar(low[:, part, :], pre[:, part, :], 0.0, None, ALU.min
                                           ).then_inc(low_ok, 1)

        @block.vector
        def _(dve):
            S_P = S // P

            def before_second(it, k):
                e = dve.value_load(c.owner[0:1, bass.ds(it * 2 + k, 1)], min_val=0, max_val=E - 1)
                for part in range(2):
                    dve.wait_ge(ht_mm, parts(it, k, part, 3))
                    dve.wait_ge(low_ok, parts(it, k, part, 1))
                    dve.wait_ge(high_ok, parts(it, k, part, 1))
                    dve.tensor_tensor(
                        pre[:, part, :].rearrange("p (j t) -> p j t", t=P),
                        ps_ht[:, part, :].rearrange("p (j t) -> p j t", t=P),
                        b1[:, part * S_P:part * S_P + S_P, bass.ds(e, 1)].broadcast_to([P, S_P, P]),
                        ALU.add).then_inc(pre_ok, 1)
                for part in range(2):
                    dve.wait_ge(pre_ok, parts(it, k, part, 3))
                    dve.wait_ge(selu_ok, parts(it, k, part, 1))
                    dve.tensor_scalar(high[:, part, :], pre[:, part, :], 0.0, -SELU_ALPHA, ALU.max, ALU.add
                                      ).then_inc(high_ok, 1)
                for part in range(2):
                    dve.wait_ge(grown_ok, parts(it, k, part, 3))
                    dve.wait_ge(high_ok, parts(it, k, part, 3))
                    dve.wait_ge(y_mm, it * 2 + (k + 1))
                    dve.tensor_tensor(hid_t[:, part, :], high[:, part, :], grown[:, part, :], ALU.add
                                      ).then_inc(selu_ok, 1)

            def y_copy(it, k):
                e = dve.value_load(c.owner[0:1, bass.ds(it * 2 + k, 1)], min_val=0, max_val=E - 1)
                dve.wait_ge(y_mm, it * 2 + (k + 2))
                dve.wait_ge(y_sent[k % 2], it * 16 + 16 * (k // 2 + 1))
                dve.scalar_tensor_tensor(out=y[:, k % 2, :], in0=ps_y[:, 0:D], scalar=SELU_SCALE,
                                         in1=b2[:, bass.ds(e, 1), :].rearrange("p a n -> p (a n)"),
                                         op0=ALU.mult, op1=ALU.add).then_inc(y_ok, 1)

            dve.sem_inc(ht_mm, 2)
            dve.sem_inc(pre_ok, 2)
            dve.sem_inc(high_ok, 2)
            dve.sem_inc(selu_ok, 2)
            dve.sem_inc(y_mm, 1)
            dve.sem_inc(y_ok, 1)
            dve.memset(shift[:, :], float(np.log(SELU_ALPHA))).then_inc(shift_ok, 1)
            dve.wait_ge(shift_ok, 1)
            dve.wait_ge(w_in, 16 * (DC + 3))
            with dve.Fori(0, TILES // 2) as it:
                for k in range(2):
                    before_second(it, k)
                    y_copy(it, k)


def gather_experts(c, tag, weight):
    nc = c.nc
    n_all = NT + 1
    with c.stage() as st:
        got = c.sbuf(st, f"{tag}_got", [P, n_all, 2, D], F32)
        clear = c.sem(st, f"{tag}_clear")
        got_in = c.sem(st, f"{tag}_got_in")
        added = c.sem(st, f"{tag}_added")
        block = st.enter_context(nc.Block())

        @block.gpsimd
        def _(pool):
            pool.wait_ge(clear, 1)
            for n in range(n_all):
                for k in range(2):
                    pool.indirect_dma_start(
                        out=got[:, n, k, :], out_offset=None, in_=c.ys[tag][:, :],
                        in_offset=bass.IndirectOffsetOnAxis(ap=c.row[:, k, n:n + 1], axis=0),
                        bounds_check=TILES * P - 1, oob_is_err=False).then_inc(got_in, 16)

        @block.vector
        def _(dve):
            dve.memset(got[:, :, :, :], 0.0).then_inc(clear, 1)
            dve.wait_ge(got_in, 16 * 2 * n_all)
            for k in range(2):
                if k:
                    dve.wait_ge(added, n_all)
                for n in range(n_all):
                    dve.scalar_tensor_tensor(out=c.h[:, n, :], in0=got[:, n, k, :], scalar=weight[:, k, n:n + 1],
                                             in1=c.h[:, n, :], op0=ALU.mult, op1=ALU.add).then_inc(added, 1)


def route_moe(c, tag, router_dram, idx, weight):
    nc = c.nc
    n_all = NT + 1
    with c.stage() as st:
        router = c.sbuf(st, f"{tag}_router", [P, DC, E], F32)
        logits = c.sbuf(st, f"{tag}_logits", [P, n_all, E], F32)
        top = c.sbuf(st, f"{tag}_top8", [P, n_all, 8], F32)
        top_at = c.sbuf(st, f"{tag}_top8_at", [P, n_all, 8], U32)
        gap = c.sbuf(st, f"{tag}_gap", [P, n_all], F32)
        ratio = c.sbuf(st, f"{tag}_ratio", [P, n_all], F32)
        one_more = c.sbuf(st, f"{tag}_one_more", [P, n_all], F32)
        ps_l = c.psum(st, f"{tag}_ps_l", [P, S])
        r_in = c.sem(st, f"{tag}_r_in")
        l_mm = c.sem(st, f"{tag}_l_mm")
        l_ok = c.sem(st, f"{tag}_l_ok")
        top_ok = c.sem(st, f"{tag}_top_ok")
        at_ok = c.sem(st, f"{tag}_at_ok")
        gap_ok = c.sem(st, f"{tag}_gap_ok")
        ratio_ok = c.sem(st, f"{tag}_ratio_ok")
        chain = c.sem(st, f"{tag}_r_chain")
        block = st.enter_context(nc.Block())

        @block.sync
        def _(sp):
            sp.dma_start(router[:, :, :], router_dram).then_inc(r_in, 16)

        @block.tensor
        def _(pe):
            pe.wait_ge(r_in, 16)
            for n in range(n_all):
                r = P if n < NT else B
                for ch in range(DC):
                    lhs = (c.xt[:, ch, n // NQ, 1 + n % NQ * P:1 + n % NQ * P + P] if n < NT else c.xt[:, ch, :, 0])
                    mm = pe.matmul(ps_l[0:r, n * E:n * E + E], lhs, router[:, ch, :], start=ch == 0, stop=ch == DC - 1)
            mm.then_inc(l_mm, 1)

        @block.vector
        def _(dve):
            dve.memset(logits[:, NT, :], 0.0).then_inc(l_ok, 1)
            dve.wait_ge(l_mm, 1)
            dve.wait_ge(l_ok, 1)
            dve.tensor_copy(logits[:, 0:NT, :], ps_l[:, 0:NT * E].rearrange("p (n e) -> p n e", e=E)).then_inc(l_ok, 1)
            dve.tensor_copy(logits[0:B, NT, :], ps_l[0:B, NT * E:n_all * E]).then_inc(l_ok, 1)
            dve.wait_ge(l_ok, 3)
            for n in range(n_all):
                dve.max(top[:, n, :], logits[:, n, :]).then_inc(top_ok, 1)
            for n in range(n_all):
                dve.wait_ge(top_ok, n + 1)
                dve.max_index(top_at[:, n, :], top[:, n, :], logits[:, n, :]).then_inc(at_ok, 1)
            dve.tensor_tensor(gap[:, :], top[:, :, 1], top[:, :, 0], ALU.subtract).then_inc(gap_ok, 1)
            dve.wait_ge(at_ok, n_all)
            dve.tensor_copy(idx[:, :, :], top_at[:, :, 0:2]).then_inc(chain, 1)
            dve.wait_ge(ratio_ok, 1)
            dve.tensor_scalar(one_more[:, :], ratio[:, :], 1.0, None, ALU.add).then_inc(chain, 1)
            dve.wait_ge(chain, 2)
            dve.reciprocal(weight[:, 0, :], one_more[:, :]).then_inc(chain, 1)
            dve.wait_ge(chain, 3)
            dve.tensor_tensor(weight[:, 1, :], ratio[:, :], weight[:, 0, :], ALU.mult).then_inc(chain, 1)

        @block.scalar
        def _(act):
            act.wait_ge(gap_ok, 1)
            act.activation(ratio[:, :], gap[:, :], ACT.Exp).then_inc(ratio_ok, 1)


def route_last(c, tag, wi_dram, bi_dram, wo_dram, bo_dram, idx, weight):
    nc = c.nc
    HC = HIDDEN // P
    n_all = NT + 1
    with c.stage() as st:
        wi = c.sbuf(st, f"{tag}_gwi", [P, DC, HIDDEN], F32)
        wo = c.sbuf(st, f"{tag}_gwo", [P, HC, D], F32)
        bi = c.sbuf(st, f"{tag}_gbi", [P, HC], F32)
        bo = c.sbuf(st, f"{tag}_gbo", [P, D], F32)
        shift = c.sbuf(st, f"{tag}_gshift", [P, 1], F32)
        low = c.sbuf(st, f"{tag}_glow", [P, 2, S], F32)
        grown = c.sbuf(st, f"{tag}_ggrown", [P, 2, S], F32)
        high = c.sbuf(st, f"{tag}_ghigh", [P, 2, S], F32)
        hid = c.sbuf(st, f"{tag}_ghid", [P, 2, S], F32)
        logits = c.sbuf(st, f"{tag}_glogits", [P, NQ, D], F32)
        top = c.sbuf(st, f"{tag}_gtop", [P, NQ, 8], F32)
        top_at = c.sbuf(st, f"{tag}_gtop_at", [P, NQ, 8], U32)
        two = c.sbuf(st, f"{tag}_gtwo", [P, 2, n_all], F32)
        sums = c.sbuf(st, f"{tag}_gsums", [P, n_all], F32)
        ps_h = c.psum(st, f"{tag}_gps_h", [P, 2, S])
        ps_l = c.psum(st, f"{tag}_gps_l", [P, NQ, S])
        w_in = c.sem(st, f"{tag}_gw_in")
        ready = c.sem(st, f"{tag}_gready")
        h_mm = c.sem(st, f"{tag}_gh_mm")
        low_ok = c.sem(st, f"{tag}_glow_ok")
        high_ok = c.sem(st, f"{tag}_ghigh_ok")
        grown_ok = c.sem(st, f"{tag}_ggrown_ok")
        hid_ok = c.sem(st, f"{tag}_ghid_ok")
        l_mm = c.sem(st, f"{tag}_gl_mm")
        l_ok = c.sem(st, f"{tag}_gl_ok")
        top_ok = c.sem(st, f"{tag}_gtop_ok")
        at_ok = c.sem(st, f"{tag}_gat_ok")
        kept = c.sem(st, f"{tag}_gkept")
        block = st.enter_context(nc.Block())

        @block.sync
        def _(sp):
            sp.dma_start(wi[:, :, :], wi_dram).then_inc(w_in, 16)
            sp.dma_start(bi[:, :], bi_dram).then_inc(w_in, 16)
            sp.dma_start(wo[:, :, :], wo_dram).then_inc(w_in, 16)
            sp.dma_start(bo[:, :], bo_dram.partition_broadcast(P)).then_inc(w_in, 16)

        @block.tensor
        def _(pe):
            def hidden(b, f, wide):
                pe.wait_ge(high_ok, b * HC + (f + 1))
                for ch in range(DC):
                    src = (c.xt[:, ch, bass.ds(b, 1), 1:].rearrange("p a t -> p (a t)") if wide == S
                           else c.xt[:, ch, :, 0])
                    mm = pe.matmul(ps_h[:, f % 2, 0:wide], wi[:, ch, f * P:f * P + P], src,
                                   start=ch == 0, stop=ch == DC - 1)
                mm.then_inc(h_mm, 1)

            def add_logits(b, f, wide):
                pe.wait_ge(hid_ok, b * HC + (f + 3))
                for n in range(NQ if wide == S else 1):
                    if f == 0:
                        pe.wait_ge(l_ok, b * NQ + (n + 1))
                    r = min(wide, P)
                    mm = pe.matmul(ps_l[0:r, n, 0:D], hid[:, f % 2, n * P:n * P + r], wo[:, f, :],
                                   start=f == 0, stop=f == HC - 1)
                mm.then_inc(l_mm, 1)

            def image(b, wide):
                hidden(b, 0, wide)
                for f in range(HC):
                    if f + 1 < HC:
                        hidden(b, f + 1, wide)
                    add_logits(b, f, wide)

            pe.wait_ge(w_in, 16 * 4)
            with pe.Fori(0, B) as b:
                image(b, S)
            image(B, B)

        @block.scalar
        def _(act):
            def image(b, wide):
                for f in range(HC):
                    act.wait_ge(low_ok, b * HC + (f + 1))
                    act.wait_ge(hid_ok, b * HC + (f + 1))
                    act.activation(high[:, f % 2, 0:wide], ps_h[:, f % 2, 0:wide], ACT.Relu, bias=bi[:, f:f + 1]
                                   ).then_inc(high_ok, 1)
                    act.activation(grown[:, f % 2, 0:wide], low[:, f % 2, 0:wide], ACT.Exp, bias=shift[:, 0:1]
                                   ).then_inc(grown_ok, 1)

            act.sem_inc(high_ok, 2)
            act.sem_inc(grown_ok, 2)
            with act.Fori(0, B) as b:
                image(b, S)
            image(B, B)

        @block.vector
        def _(dve):
            def image(b, wide):
                for f in range(HC):
                    dve.wait_ge(h_mm, b * HC + (f + 1))
                    dve.wait_ge(grown_ok, b * HC + (f + 1))
                    dve.tensor_scalar(low[:, f % 2, 0:wide], ps_h[:, f % 2, 0:wide], bi[:, f:f + 1], 0.0,
                                      ALU.add, ALU.min).then_inc(low_ok, 1)
                    dve.wait_ge(high_ok, b * HC + (f + 3))
                    dve.wait_ge(grown_ok, b * HC + (f + 3))
                    dve.wait_ge(l_mm, b * HC + (f + 1))
                    dve.scalar_tensor_tensor(out=hid[:, f % 2, 0:wide], in0=grown[:, f % 2, 0:wide],
                                             scalar=-SELU_ALPHA, in1=high[:, f % 2, 0:wide],
                                             op0=ALU.add, op1=ALU.add).then_inc(hid_ok, 1)
                tiles = NQ if wide == S else 1
                r = min(wide, P)
                dve.wait_ge(l_mm, b * HC + (HC + 2))
                dve.wait_ge(at_ok, b * NQ + NQ)
                for n in range(tiles):
                    dve.scalar_tensor_tensor(out=logits[0:r, n, :], in0=ps_l[0:r, n, 0:D], scalar=SELU_SCALE,
                                             in1=bo[0:r, :], op0=ALU.mult, op1=ALU.add).then_inc(l_ok, 1)
                dve.wait_ge(kept, 2 * b + 2)
                for n in range(tiles):
                    dve.wait_ge(l_ok, b * NQ + (NQ + n + 1))
                    dve.nop(nofuse=True)
                    dve.max(top[:, n, :], logits[:, n, :]).then_inc(top_ok, 1)
                for n in range(tiles):
                    dve.wait_ge(top_ok, b * NQ + (n + 1))
                    dve.nop(nofuse=True)
                    dve.max_index(top_at[:, n, :], top[:, n, :], logits[:, n, :]).then_inc(at_ok, 1)
                dve.wait_ge(at_ok, b * NQ + (NQ + tiles))
                where = bass.ds(b * NQ, tiles)
                dve.tensor_copy(two[:, :, where].rearrange("p k n -> p n k"), top[:, 0:tiles, 0:2]).then_inc(kept, 1)
                dve.tensor_copy(idx[:, where, :], top_at[:, 0:tiles, 0:2]).then_inc(kept, 1)

            dve.sem_inc(hid_ok, 2)
            dve.sem_inc(l_mm, 2)
            dve.sem_inc(l_ok, NQ)
            dve.sem_inc(at_ok, NQ)
            dve.sem_inc(kept, 2)
            dve.memset(shift[:, :], float(np.log(SELU_ALPHA))).then_inc(ready, 1)
            dve.wait_ge(ready, 1)
            dve.wait_ge(w_in, 16 * 4)
            with dve.Fori(0, B) as b:
                image(b, S)
            dve.wait_ge(at_ok, (B + 1) * NQ)
            dve.memset(logits[:, 0, :], 1.0).then_inc(ready, 1)
            dve.wait_ge(ready, 2)
            image(B, B)
            dve.wait_ge(kept, 2 * B + 4)
            dve.tensor_tensor(sums[:, :], two[:, 0, :], two[:, 1, :], ALU.add).then_inc(ready, 1)
            dve.wait_ge(ready, 3)
            dve.reciprocal(sums[:, :], sums[:, :]).then_inc(ready, 1)
            dve.wait_ge(ready, 4)
            dve.tensor_tensor(weight[:, :, :], two[:, :, :],
                              sums[:, :].rearrange("p (a n) -> p a n", a=1).broadcast_to([P, 2, n_all]), ALU.mult
                              ).then_inc(ready, 1)


def load_patches(c, x_t, cls):
    with c.stage() as st:
        x_in = c.sem(st, "x_in")
        cleared = c.sem(st, "cleared")
        with c.nc.Block() as block:
            @block.sync
            def _(sp):
                for ch in range(DC):
                    sp.dma_start(c.xt[:, ch, :, 1:], x_t[:, ch]).then_inc(x_in, 16)
                sp.wait_ge(cleared, 1)
                sp.dma_start(c.h[0:B, NT, :], cls.partition_broadcast(B)).then_inc(x_in, 16)
                sp.wait_ge(x_in, 16 * (DC + 1))

            @block.gpsimd
            def _(pool):
                pool.memset(c.h[:, NT, :], 0.0).then_inc(cleared, 1)


def norm(c, tag, keep=None):
    nc = c.nc
    with c.stage() as st:
        stats = c.sbuf(st, f"{tag}_stats", [P, NT + 1, 6], F32)
        mv = c.sbuf(st, f"{tag}_mv", [P, NT + 1, 2], F32)
        rstd = c.sbuf(st, f"{tag}_rstd", [P, NT + 1], F32)
        eps = c.sbuf(st, f"{tag}_eps", [P, 1], F32)
        xn = keep if keep is not None else c.sbuf(st, f"{tag}_xn", [P, NT + 1, D], F32)
        ps_t = c.psum(st, f"{tag}_ps_xt", [P, 2, S])
        stat_ok = c.sem(st, f"{tag}_stat_ok")
        aggr_ok = c.sem(st, f"{tag}_aggr_ok")
        eps_ok = c.sem(st, f"{tag}_eps_ok")
        std_ok = c.sem(st, f"{tag}_std_ok")
        rstd_ok = c.sem(st, f"{tag}_rstd_ok")
        xn_ok = c.sem(st, f"{tag}_xn_ok")
        t_mm = c.sem(st, f"{tag}_xt_mm")
        t_out = c.sem(st, f"{tag}_xt_out")
        block = st.enter_context(nc.Block())

        @block.vector
        def _(dve):
            dve.memset(eps[:, :], EPS).then_inc(eps_ok, 1)
            for n in range(NT + 1):
                dve.bn_stats(stats[:, n, :], c.h[:, n, :]).then_inc(stat_ok, 1)
            for n in range(NT + 1):
                dve.wait_ge(stat_ok, n + 1)
                dve.bn_aggr(mv[:, n, :], stats[:, n, :]).then_inc(aggr_ok, 1)
            dve.wait_ge(std_ok, 1)
            dve.reciprocal(rstd[:, :], rstd[:, :]).then_inc(rstd_ok, 1)
            dve.wait_ge(rstd_ok, 1)
            dve.wait_ge(aggr_ok, NT + 1)
            for n in range(NT + 1):
                dve.tensor_scalar(xn[:, n, :], c.h[:, n, :], mv[:, n, 0:1], rstd[:, n:n + 1],
                                  ALU.subtract, ALU.mult).then_inc(xn_ok, 1)

        @block.tensor
        def _(pe):
            for n in range(NT + 1):
                pe.wait_ge(xn_ok, n + 1)
                if n >= 2:
                    pe.wait_ge(t_out, n - 1)
                r = P if n < NT else B
                for ch in range(DC):
                    mm = pe.transpose(ps_t[:, n % 2, ch * P:ch * P + r], xn[0:r, n, ch * P:ch * P + P],
                                      c.ident[0:r, 0:r])
                mm.then_inc(t_mm, 1)

        @block.scalar
        def _(act):
            act.wait_ge(aggr_ok, NT + 1)
            act.wait_ge(eps_ok, 1)
            act.activation(rstd[:, :], mv[:, :, 1], ACT.Sqrt, bias=eps[:, 0:1]).then_inc(std_ok, 1)
            for n in range(NT + 1):
                act.wait_ge(t_mm, n + 1)
                src = ps_t[:, n % 2, 0:DC * P].rearrange("p (c t) -> p c t", c=DC)
                if n < NT:
                    at = 1 + (n % NQ) * P
                    act.activation(c.xt[:, :, n // NQ, at:at + P], src, ACT.Copy).then_inc(t_out, 1)
                else:
                    act.activation(c.xt[:, :, :, 0], src[:, :, 0:B], ACT.Copy).then_inc(t_out, 1)


def debug_dump(c, ap):
    with c.stage() as st:
        out_ok = c.sem(st, "out_ok")
        with c.nc.Block() as block:
            @block.sync
            def _(sp):
                for b in range(B):
                    sp.dma_start(ap[b, 1:, :].rearrange("(n p) d -> p n d", p=P),
                                 c.h[:, b * NQ:b * NQ + NQ, :]).then_inc(out_ok, 16)
                sp.dma_start(ap[:, 0, :], c.h[0:B, NT, :]).then_inc(out_ok, 16)
                sp.wait_ge(out_ok, 16 * (B + 1))


def program(nc, a, out, stop=9):
    with ExitStack() as stack:
        c = Chip(nc, stack)
        c.qd = nc.dram_tensor("q_parts", [B, PARTS, HD, NH, S], BF16, kind="Internal").ap()
        c.kd = nc.dram_tensor("k_parts", [B, PARTS, HD, NH, S + 1], BF16, kind="Internal").ap()
        c.vd = nc.dram_tensor("v_rows", [B, G, P, NQ, P], F32, kind="Internal").ap()
        c.xs = {t: nc.dram_tensor(f"{t}_xs", [TILES * P, D], F32, kind="Internal").ap() for t in ("moe", "last")}
        c.ys = {t: nc.dram_tensor(f"{t}_ys", [TILES * P, D], F32, kind="Internal").ap() for t in ("moe", "last")}
        constants(c)
        c.h = c.sbuf(stack, "h", [P, NT + 1, D], F32)
        c.vcls = c.sbuf(stack, "vcls", [B, D], F32)
        c.row = c.sbuf(stack, "row", [P, 2, NT + 1], U32)
        c.owner = c.sbuf(stack, "owner", [P, TILES], I32)
        idx = c.sbuf(stack, "idx", [P, NT + 1, 2], F32)
        weight = c.sbuf(stack, "weight", [P, 2, NT + 1], F32)
        c.ctx = c.sbuf(stack, "ctx", [P, NT + 1, D], F32)
        with ExitStack() as wide:
            c.xt = c.sbuf(wide, "xt", [P, DC, B, S + 1], F32)
            load_patches(c, a["x_t"], a["cls"])
            project(c, "tok", a["tok_w"], a["tok_qkb"], a["tok_vb"], cls=False)
            attend(c, "tok", causal=False)
            attend_out(c, "tok", a["tok_wo"], a["tok_bo"], residual=False, cls=False)
            if stop == 0: return debug_dump(c, out)
            norm(c, "rot")
            project(c, "rot", a["rot_w"], a["rot_qkb"], a["rot_vb"], cls=True, rope=(a["cos"], a["sin"]))
            attend(c, "rot", causal=True)
            attend_out(c, "rot", a["rot_wo"], a["rot_bo"], residual=True, cls=True)
            if stop == 1: return debug_dump(c, out)
            norm(c, "moe", keep=c.ctx)
            route_moe(c, "moe", a["router"], idx, weight)
        dispatch(c, "moe", c.ctx, idx)
        run_gated_experts(c, "moe", a["moe_w13"], a["moe_w2"], S)
        gather_experts(c, "moe", weight)
        if stop == 2: return debug_dump(c, out)
        with ExitStack() as wide:
            c.xt = c.sbuf(wide, "xt2", [P, DC, B, S + 1], F32)
            norm(c, "top")
            project(c, "top", a["top_w"], a["top_qkb"], a["top_vb"], cls=True)
            attend_top(c, "top")
            attend_out(c, "top", a["top_wo"], a["top_bo"], residual=True, cls=True)
            if stop == 3: return debug_dump(c, out)
            norm(c, "last", keep=c.ctx)
            route_last(c, "last", a["gate_wi"], a["gate_bi"], a["gate_wo"], a["gate_bo"], idx, weight)
        dispatch(c, "last", c.ctx, idx)
        run_selu_experts(c, "last", a["exp_wi"], a["exp_bi"], a["exp_wo"], a["exp_bo"])
        gather_experts(c, "last", weight)
        debug_dump(c, out)


_OUT = (B, S + 1, D)


def _split_rows(w):
    return np.ascontiguousarray(w.reshape(DC, P, -1).transpose(1, 0, 2))


def _columns(*vectors):
    return _split_rows(np.stack(vectors, axis=1))


def _swap_halves(w):
    return w.reshape(-1, NH, 2, HD // 2)[:, :, ::-1].reshape(w.shape)


def layout(inputs):
    i = {k: np.asarray(v) for k, v in inputs.items()}
    a = {}
    a["x_t"] = np.ascontiguousarray(i["x"].reshape(B, S, DC, P).transpose(3, 2, 0, 1))
    a["cls"] = i["cls_tok"].reshape(D)
    wt = i["L0_tok_w_qkv"].T.reshape(D, NH, 3, HD).transpose(0, 2, 1, 3).reshape(D, 3 * D)
    bt = i["L0_tok_b_qkv"].reshape(NH, 3, HD).transpose(1, 0, 2).reshape(3, D)
    a["tok_w"] = _split_rows(wt)
    a["tok_qkb"] = _columns(bt[0], bt[1])
    a["tok_vb"] = np.ascontiguousarray(bt[2])
    a["tok_wo"] = _split_rows(i["L0_tok_w_out"].T)
    a["tok_bo"] = i["L0_tok_b_out"]
    wq, wk, wv = (i[f"L0_attn_w{x}_w"] for x in "qkv")
    bq, bk = i["L0_attn_wq_b"], i["L0_attn_wk_b"]
    a["rot_w"] = _split_rows(np.concatenate([wq, wk, wv, _swap_halves(wq), _swap_halves(wk)], axis=1))
    a["rot_qkb"] = _columns(bq, bk, _swap_halves(bq[None])[0], _swap_halves(bk[None])[0])
    a["rot_vb"] = i["L0_attn_wv_b"]
    a["rot_wo"] = _split_rows(i["L0_attn_wo_w"])
    a["rot_bo"] = i["L0_attn_wo_b"]
    half = HD // 2
    scale = np.float32(2500.0) ** (np.float32(2.0) * np.arange(half, dtype=np.float32) / np.float32(HD))
    angle = np.arange(1, S + 1, dtype=np.float32)[None, :] / scale[:, None].astype(np.float32)
    cos, sin = np.cos(angle).astype(np.float32), np.sin(angle).astype(np.float32)
    a["cos"] = np.tile(np.concatenate([cos, cos]), (P // HD, 1))
    a["sin"] = np.tile(np.concatenate([-sin, sin]), (P // HD, 1))
    a["top_w"] = _split_rows(np.concatenate([i[f"L1_attn_W{x}"].T for x in "qkv"], axis=1))
    a["top_qkb"] = _columns(i["L1_attn_bq"], i["L1_attn_bk"])
    a["top_vb"] = i["L1_attn_bv"]
    a["top_wo"] = _split_rows(i["L1_attn_Wo"].T)
    a["top_bo"] = i["L1_attn_bo"]
    a["router"] = _split_rows(i["L0_ffn_moe_router"])
    a["moe_w13"] = i["L0_ffn_moe_w13"].reshape(E, DC, P, -1).transpose(2, 1, 0, 3)
    a["moe_w2"] = i["L0_ffn_moe_w2"].reshape(E, -1, P, D).transpose(2, 1, 0, 3)
    a["gate_wi"] = _split_rows(i["L1_ffn_gate_wi"])
    a["gate_bi"] = i["L1_ffn_gate_bi"].reshape(-1, P).T
    a["gate_wo"] = i["L1_ffn_gate_wo"].reshape(-1, P, D).transpose(1, 0, 2)
    a["gate_bo"] = i["L1_ffn_gate_bo"]
    a["exp_wi"] = i["L1_ffn_exp_wi"].reshape(E, DC, P, -1).transpose(2, 1, 0, 3)
    a["exp_bi"] = i["L1_ffn_exp_bi"].reshape(E, -1, P).transpose(2, 1, 0)
    a["exp_wo"] = i["L1_ffn_exp_wo"].reshape(E, -1, P, D).transpose(2, 1, 0, 3)
    a["exp_bo"] = i["L1_ffn_exp_bo"]
    return {k: np.ascontiguousarray(v) for k, v in a.items()}


def kernel(**inputs):
    import concourse.bacc as bacc
    from concourse.bass_utils import run_bass_kernel_spmd

    nc = bacc.Bacc("TRN2", target_bir_lowering=False, num_devices=1)
    arrays = layout(inputs)
    aps = {k: nc.dram_tensor(f"in_{k}", list(v.shape), mybir.dt.from_np(v.dtype), kind="ExternalInput").ap()
           for k, v in arrays.items()}
    out = nc.dram_tensor("out", list(_OUT), F32, kind="ExternalOutput").ap()
    program(nc, aps, out)
    r = run_bass_kernel_spmd(nc, [{f"in_{k}": v for k, v in arrays.items()}], core_ids=[0])
    return r.results[0]["out"]
```

```python
from contextlib import ExitStack, contextmanager
from itertools import groupby

import numpy as np

import concourse.bass as bass
from concourse import mybir

F32 = mybir.dt.float32
BF16 = mybir.dt.bfloat16
U32 = mybir.dt.uint32
I32 = mybir.dt.int32
ALU = mybir.AluOpType
ACT = mybir.ActivationFunctionType
AX_X = mybir.AxisListType.X

P = 128
B = 4
S = 512
D = 256
DC = D // P
NH = 16
HD = D // NH
NQ = S // P
NT = B * NQ
G = 4
HG = NH // G
STRIP = 32
SPLIT = 3
Q_ORDER = (2, 1, 0, 0, 0, 1)
K_ORDER = (0, 0, 0, 1, 2, 1)
PARTS = len(Q_ORDER)
NLOADS = len(list(groupby(Q_ORDER))) + len(list(groupby(K_ORDER))) + 1
E = 8
EPS = 1e-5
MASKED = -1e30
TAKEN = -3e38
K_TOP = 32
TILES = (2 * (NT * P + B) - E) // P + E
NOWHERE = 1 << 16
HIDDEN = 1024
SELU_ALPHA = 1.6732632423543772
SELU_SCALE = 1.0507009873554805
QSCALE = 1.0 / float(np.sqrt(HD))


FIRST_PASS = ((1, 1, 1, 1), (1, 1, 2, 1), (1, 1, 2, 1))
FIRST_UNITS = 2


class Chip:

    def __init__(self, nc, stack):
        self.nc, self.stack = nc, stack
        self.stage_sems = []

    @contextmanager
    def stage(self):
        with ExitStack() as st:
            yield st
        sems, self.stage_sems = self.stage_sems, []
        self.nc.clear_and_free_semaphores(sems)
        self.nc.all_engine_barrier()

    def sbuf(self, stack, name, shape, dt):
        return stack.enter_context(self.nc.sbuf_tensor(name, shape, dt))

    def psum(self, stack, name, shape, dt=F32):
        return stack.enter_context(self.nc.psum_tensor(name, shape, dt))

    def sem(self, stack, name):
        sem = self.nc.alloc_semaphore(name)
        if stack is not self.stack:
            self.stage_sems.append(sem)
        return sem


def constants(c):
    nc = c.nc
    c.ident = c.sbuf(c.stack, "ident", [P, P], F32)
    c.ident_bf = c.sbuf(c.stack, "ident_bf", [P, P], BF16)
    c.mask_qk = c.sbuf(c.stack, "mask_qk", [P, P], BF16)
    c.mask_kq = c.sbuf(c.stack, "mask_kq", [P, P], BF16)
    c.pick_cls = c.sbuf(c.stack, "pick_cls", [B, B, P], F32)
    c.before = c.sbuf(c.stack, "before", [P, P], BF16)
    c.ones_bf = c.sbuf(c.stack, "ones_bf", [P, P], BF16)
    c.iota_e = c.sbuf(c.stack, "iota_e", [P, E], F32)
    c.iota_t = c.sbuf(c.stack, "iota_t", [P, TILES], F32)
    c.steps = c.sbuf(c.stack, "steps", [P, NT + 1], F32)
    c.valid = c.sbuf(c.stack, "valid", [P, NT + 1], F32)
    c.zeros = zeros = c.sbuf(c.stack, "zeros", [P, 1, D], F32)
    c.xs_clear = c.sem(c.stack, "xs_clear")
    with c.stage() as st:
        filled = c.sem(st, "const_filled")
        with nc.Block() as block:
            @block.gpsimd
            def _(pool):
                pool.memset(c.ident[:, :], 0.0).then_inc(filled, 1)
                pool.memset(c.ident_bf[:, :], 0.0).then_inc(filled, 1)
                pool.memset(c.mask_qk[:, :], 0.0).then_inc(filled, 1)
                pool.memset(c.mask_kq[:, :], 0.0).then_inc(filled, 1)
                pool.memset(c.pick_cls[:, :, :], 0.0).then_inc(filled, 1)
                pool.wait_ge(filled, 5)
                for ident in (c.ident, c.ident_bf):
                    pool.affine_select(out=ident[:, :], in_=ident[:, :], compare_op=ALU.not_equal, fill=1.0,
                                       base=0, pattern=[[-1, P]], channel_multiplier=1).then_inc(filled, 1)
                pool.affine_select(out=c.mask_qk[:, :], in_=c.mask_qk[:, :], compare_op=ALU.is_ge, fill=MASKED,
                                   base=0, pattern=[[-1, P]], channel_multiplier=1).then_inc(filled, 1)
                pool.affine_select(out=c.mask_kq[:, :], in_=c.mask_kq[:, :], compare_op=ALU.is_ge, fill=MASKED,
                                   base=0, pattern=[[1, P]], channel_multiplier=-1).then_inc(filled, 1)
                pool.affine_select(out=c.pick_cls[:, :, :], in_=c.pick_cls[:, :, :], compare_op=ALU.not_equal,
                                   fill=1.0, base=0, pattern=[[-1, B], [0, P]],
                                   channel_multiplier=1).then_inc(filled, 1)
                pool.wait_ge(filled, 10)
                pool.memset(zeros[:, :, :], 0.0).then_inc(filled, 1)
                pool.memset(c.before[:, :], 1.0).then_inc(filled, 1)
                pool.memset(c.ones_bf[:, :], 1.0).then_inc(filled, 1)
                pool.memset(c.valid[:, :], 1.0).then_inc(filled, 1)
                pool.iota(c.iota_e[:, :], pattern=[[1, E]], base=0, channel_multiplier=0,
                          allow_small_or_imprecise_dtypes=True).then_inc(filled, 1)
                pool.iota(c.iota_t[:, :], pattern=[[1, TILES]], base=0, channel_multiplier=0,
                          allow_small_or_imprecise_dtypes=True).then_inc(filled, 1)
                pool.iota(c.steps[:, :], pattern=[[P, NT + 1]], base=0, channel_multiplier=0,
                          allow_small_or_imprecise_dtypes=True).then_inc(filled, 1)
                pool.wait_ge(filled, 17)
                pool.affine_select(out=c.before[:, :], in_=c.before[:, :], compare_op=ALU.is_gt, fill=0.0,
                                   base=0, pattern=[[1, P]], channel_multiplier=-1).then_inc(filled, 1)
                pool.affine_select(out=c.valid[:, NT:NT + 1], in_=c.valid[:, NT:NT + 1], compare_op=ALU.is_ge,
                                   fill=0.0, base=B - 1, pattern=[[0, 1]], channel_multiplier=-1).then_inc(filled, 1)
                pool.wait_ge(filled, 19)


def load_step(sp, c, b, g, q, k, v, loaded):
    heads = slice(g * HG, g * HG + HG)
    for dst, parts, order in ((q, c.qd[b], Q_ORDER), (k, c.kd[k.shape[2]][b], K_ORDER)):
        at = 0
        for part, run in groupby(order):
            n = len(list(run))
            src = parts[part:part + 1, :, heads, :]
            if n > 1:
                src = src.broadcast_to([n, HD, HG, dst.shape[2]])
            sp.dma_start(dst[at * HD:(at + n) * HD, :, :], src.rearrange("i d h t -> (i d) h t") if n == 1 else src
                         ).then_inc(loaded, 16)
            at += n
    sp.dma_start(v[:, :, :], c.vd[b, g]).then_inc(loaded, 16)


def project(c, tag, w_dram, qkb_dram, vb_dram, cls, rope=None):
    nc = c.nc
    cols = (5 if rope else 3) * D
    turns = 2 if rope else 0
    with c.stage() as st:
        w = c.sbuf(st, f"{tag}_w", [P, DC, cols], F32)
        qkb = c.sbuf(st, f"{tag}_qkb", [P, DC, 4 if rope else 2], F32)
        vb = c.sbuf(st, f"{tag}_vb", [P, D], F32)
        full = c.sbuf(st, f"{tag}_full", [P, 2, S + 1], F32)
        rest = c.sbuf(st, f"{tag}_rest", [P, 2, S + 1], F32)
        hi = c.sbuf(st, f"{tag}_hi", [P, 2, S + 1], BF16)
        mid = c.sbuf(st, f"{tag}_mid", [P, 2, S + 1], BF16)
        lo = c.sbuf(st, f"{tag}_lo", [P, 2, S + 1], BF16)
        kcls = c.sbuf(st, f"{tag}_kcls", [P, DC, B], F32)
        va = c.sbuf(st, f"{tag}_va", [P, NT, NH, STRIP], F32)
        if rope:
            cos = c.sbuf(st, f"{tag}_cos", [P, 2, S], F32)
            sin = c.sbuf(st, f"{tag}_sin", [P, 2, S], F32)
            turned = c.sbuf(st, f"{tag}_turned", [P, 2, S], F32)
            plain = c.sbuf(st, f"{tag}_plain", [P, 2, S], F32)
        ps = c.psum(st, f"{tag}_ps", [P, 2, S])
        ps_rot = c.psum(st, f"{tag}_ps_rot", [P, 2, S])
        ps_v = c.psum(st, f"{tag}_ps_v", [P, 2, S])
        ps_c = c.psum(st, f"{tag}_ps_c", [P, 2, S])
        w_in = c.sem(st, f"{tag}_w_in")
        cls_mm = c.sem(st, f"{tag}_cls_mm")
        cls_done = c.sem(st, f"{tag}_cls_done")
        tables = c.sem(st, f"{tag}_tables")
        qk_mm = c.sem(st, f"{tag}_qk_mm")
        full_ok = c.sem(st, f"{tag}_full_ok")
        turn_ok = c.sem(st, f"{tag}_turn_ok")
        hi_ok = c.sem(st, f"{tag}_hi_ok")
        rest_ok = c.sem(st, f"{tag}_rest_ok")
        mid_ok = c.sem(st, f"{tag}_mid_ok")
        lo_ok = c.sem(st, f"{tag}_lo_ok")
        stored = [c.sem(st, f"{tag}_stored{i}") for i in range(2)]
        v_mm = c.sem(st, f"{tag}_v_mm")
        v_ok = c.sem(st, f"{tag}_v_ok")
        v_ones = c.sem(st, f"{tag}_v_ones")
        v_out = c.sem(st, f"{tag}_v_out")
        n_in = 3 + (4 if rope else 0)
        step_stores = 16 * SPLIT
        block = st.enter_context(nc.Block())

        def span(k):
            return slice(0 if cls and k // 2 == 1 else 1, S + 1)

        @block.sync
        def _(sp):
            for i in range(2):
                sp.sem_inc(stored[i], 16)
            sp.dma_start(w[:, :, :], w_dram).then_inc(w_in, 16)
            sp.dma_start(qkb[:, :, :], qkb_dram).then_inc(w_in, 16)
            sp.dma_start(vb[:, :], vb_dram.partition_broadcast(P)).then_inc(w_in, 16)
            if rope:
                for n, t in enumerate((cos, sin)):
                    for h in range(2):
                        sp.dma_start(t[:, h, :], rope[n]).then_inc(w_in, 16)
            for b in range(B):
                for k in range(4):
                    which, gg = k // 2, k % 2
                    dst = (c.qd, c.kd[S + 1 if cls else S])[which]
                    for part, (tile, ok) in enumerate(((hi, hi_ok), (mid, mid_ok), (lo, lo_ok))):
                        sp.wait_ge(ok, b * 4 + k + 1)
                        sp.dma_start(dst[b, part, :, gg * 8:gg * 8 + 8, :].rearrange("d h t -> h d t"),
                                     tile[:, k % 2, span(k)]).then_inc(stored[k % 2], 16)
                sp.wait_ge(v_ok, 2 + (b + 1) * NQ)
                for g in range(G):
                    sp.dma_start(c.vd[b, g], va[:, b * NQ:b * NQ + NQ, g * HG:g * HG + HG, :].rearrange(
                        "p n h s -> p n (h s)")).then_inc(v_out, 16)
            sp.wait_ge(v_out, 16 * G * B)
            for i in range(2):
                sp.wait_ge(stored[i], 16 + B * 2 * step_stores)

        @block.tensor
        def _(pe):
            pe.wait_ge(w_in, 16 * n_in)
            if cls:
                for gg in range(DC):
                    for ch in range(DC):
                        pe.matmul(ps_c[:, 0, gg * B:gg * B + B], w[:, ch, D + gg * P:D + gg * P + P],
                                  c.xt[:, ch, :, 0], start=ch == 0, stop=ch == DC - 1)
                for ch in range(DC):
                    mm = pe.matmul(ps_c[0:B, 1, 0:D], c.xt[:, ch, :, 0], w[:, ch, 2 * D:3 * D],
                                   start=ch == 0, stop=ch == DC - 1)
                mm.then_inc(cls_mm, 1)
            for b in range(B):
                for k in range(4):
                    which, gg = k // 2, k % 2
                    pe.wait_ge(full_ok, b * 4 + (k + 1))
                    for ch in range(DC):
                        mm = pe.matmul(ps[:, k % 2, :], w[:, ch, which * D + gg * P:which * D + gg * P + P],
                                       c.xt[:, ch, b, 1:S + 1], start=ch == 0, stop=ch == DC - 1)
                    if rope:
                        at = (3 + which) * D + gg * P
                        for ch in range(DC):
                            mm = pe.matmul(ps_rot[:, k % 2, :], w[:, ch, at:at + P],
                                           c.xt[:, ch, b, 1:S + 1], start=ch == 0, stop=ch == DC - 1)
                    mm.then_inc(qk_mm, 1)
                    pe.wait_ge(v_ok, b * NQ + (k + 1))
                    for ch in range(DC):
                        mm = pe.matmul(ps_v[:, k % 2, 0:D], c.xt[:, ch, b, 1 + k * P:1 + k * P + P],
                                       w[:, ch, 2 * D:3 * D], start=ch == 0, stop=ch == DC - 1)
                    mm.then_inc(v_mm, 1)

        @block.vector
        def _(dve):
            dve.sem_inc(full_ok, 2)
            dve.sem_inc(rest_ok, 2)
            dve.sem_inc(v_ok, 2)
            dve.wait_ge(v_ones, 2)
            dve.wait_ge(w_in, 16 * n_in)
            if cls:
                dve.wait_ge(cls_mm, 1)
                for gg in range(DC):
                    dve.tensor_scalar(kcls[:, gg, :], ps_c[:, 0, gg * B:gg * B + B], qkb[:, gg, 1:2], None,
                                      ALU.add).then_inc(cls_done, 1)
                dve.tensor_tensor(c.vcls[:, :], ps_c[0:B, 1, 0:D], vb[0:B, :], ALU.add).then_inc(cls_done, 1)
                dve.wait_ge(cls_done, DC + 1)
            if rope:
                dve.tensor_scalar(cos[:, 0, :], cos[:, 0, :], QSCALE, None, ALU.mult).then_inc(tables, 1)
                dve.tensor_scalar(sin[:, 0, :], sin[:, 0, :], QSCALE, None, ALU.mult).then_inc(tables, 1)
                dve.wait_ge(tables, 2)
            per_image = 4 * turns + (2 if cls else 0)
            with dve.Fori(0, B) as b:
                done = 0
                for k in range(4):
                    which, gg = k // 2, k % 2
                    dve.wait_ge(qk_mm, b * 4 + (k + 1))
                    dve.wait_ge(rest_ok, b * 4 + (k + 1))
                    dve.wait_ge(full_ok, b * 4 + (k + 1))
                    if cls and which == 1:
                        dve.tensor_copy(full[:, k % 2, 0:1], kcls[:, gg, bass.ds(b, 1)]).then_inc(turn_ok, 1)
                        done += 1
                    if rope:
                        dve.scalar_tensor_tensor(out=plain[:, k % 2, :], in0=ps[:, k % 2, :],
                                                 scalar=qkb[:, gg, which:which + 1], in1=cos[:, which, :],
                                                 op0=ALU.add, op1=ALU.mult).then_inc(turn_ok, 1)
                        dve.scalar_tensor_tensor(out=turned[:, k % 2, :], in0=ps_rot[:, k % 2, :],
                                                 scalar=qkb[:, gg, 2 + which:3 + which], in1=sin[:, which, :],
                                                 op0=ALU.add, op1=ALU.mult).then_inc(turn_ok, 1)
                        done += turns
                        dve.wait_ge(turn_ok, b * per_image + done)
                        dve.tensor_tensor(full[:, k % 2, 1:], plain[:, k % 2, :], turned[:, k % 2, :],
                                          ALU.add).then_inc(full_ok, 1)
                    else:
                        if cls and which == 1:
                            dve.wait_ge(turn_ok, b * per_image + done)
                        dve.tensor_scalar(full[:, k % 2, 1:], ps[:, k % 2, :], qkb[:, gg, which:which + 1],
                                          QSCALE if which == 0 else 1.0, ALU.add, ALU.mult).then_inc(full_ok, 1)
                    dve.wait_ge(full_ok, b * 4 + (k + 3))
                    dve.wait_ge(hi_ok, b * 4 + (k + 1))
                    dve.tensor_tensor(rest[:, k % 2, span(k)], full[:, k % 2, span(k)], hi[:, k % 2, span(k)],
                                      ALU.subtract).then_inc(rest_ok, 1)
                    n = b * NQ + k
                    dve.wait_ge(v_mm, n + 1)
                    dve.tensor_tensor(va[:, bass.ds(n, 1), :, 0:HD].rearrange("p a h d -> p (a h) d"),
                                      ps_v[:, k % 2, 0:D].rearrange("p (h d) -> p h d", d=HD),
                                      vb[:, :].rearrange("p (h d) -> p h d", d=HD), ALU.add).then_inc(v_ok, 1)

        @block.scalar
        def _(act):
            with act.Fori(0, B) as b:
                for k in range(4):
                    act.wait_ge(full_ok, b * 4 + (k + 3))
                    act.wait_ge(stored[k % 2], b * (2 * step_stores) + (16 + (k // 2) * step_stores))
                    act.activation(hi[:, k % 2, span(k)], full[:, k % 2, span(k)], ACT.Copy).then_inc(hi_ok, 1)
                    act.wait_ge(rest_ok, b * 4 + (k + 3))
                    act.activation(mid[:, k % 2, span(k)], rest[:, k % 2, span(k)], ACT.Copy).then_inc(mid_ok, 1)

        @block.gpsimd
        def _(pool):
            pool.memset(va[:, :, :, :], 0.0).then_inc(v_ones, 1)
            pool.wait_ge(v_ones, 1)
            pool.memset(va[:, :, :, HD:HD + 1], 1.0).then_inc(v_ones, 1)
            with pool.Fori(0, B) as b:
                for k in range(4):
                    pool.wait_ge(mid_ok, b * 4 + (k + 1))
                    pool.tensor_tensor(lo[:, k % 2, span(k)], rest[:, k % 2, span(k)], mid[:, k % 2, span(k)],
                                       ALU.subtract).then_inc(lo_ok, 1)


def attend(c, tag, causal, clear=False):
    nc = c.nc
    k0 = 1 if causal else 0
    units = NQ * HG
    with c.stage() as st:
        qs = [c.sbuf(st, f"{tag}_qs{i}", [P, HG, S], BF16) for i in range(G)]
        ks = [c.sbuf(st, f"{tag}_ks{i}", [P, HG, S + k0], BF16) for i in range(G)]
        vs = [c.sbuf(st, f"{tag}_vs{i}", [P, NQ, P], F32) for i in range(G)]
        et = c.sbuf(st, f"{tag}_et", [P, 2, HG, S], F32)
        pv_rows = c.sbuf(st, f"{tag}_pv_rows", [P, S], F32)
        rowmax = c.sbuf(st, f"{tag}_rowmax", [P, units], F32)
        top = c.sbuf(st, f"{tag}_top", [P, units], F32)
        neg = c.sbuf(st, f"{tag}_neg", [P, units, STRIP], BF16)
        neg_sum = c.sbuf(st, f"{tag}_neg_sum", [P, units], F32)
        cls_score = c.sbuf(st, f"{tag}_cls_score", [P, units], F32)
        p_cls = c.sbuf(st, f"{tag}_p_cls", [P, 2, units], F32)
        v_cls = c.sbuf(st, f"{tag}_v_cls", [P, B, D], F32)
        cls_part = c.sbuf(st, f"{tag}_cls_part", [P, NQ, HG, HD], F32)
        raw = c.sbuf(st, f"{tag}_raw", [P, NQ, HG, HD], F32)
        den = c.sbuf(st, f"{tag}_den", [P, units], F32)
        rden = c.sbuf(st, f"{tag}_rden", [P, units], F32)
        ps_st = c.psum(st, f"{tag}_ps_st", [P, HG, S])
        ps_s = c.psum(st, f"{tag}_ps_s", [P, 2, S])
        ps_pv = c.psum(st, f"{tag}_ps_pv", [P, S])
        ps_cls = c.psum(st, f"{tag}_ps_cls", [P, S])
        neg_t = ps_s[:, :, :].bitcast(BF16).rearrange("p a (h t) -> p (a h) t", t=S)
        ctx_t = ps_pv[:, :].rearrange("p (n h s) -> p n h s", h=HG, s=STRIP)

        loaded = [c.sem(st, f"{tag}_loaded{i}") for i in range(G)]
        ready = c.sem(st, f"{tag}_ready")
        vcls_mm = c.sem(st, f"{tag}_vcls_mm")
        cls_row = c.sem(st, f"{tag}_cls_row")
        s_mm = c.sem(st, f"{tag}_s_mm")
        max_ok = c.sem(st, f"{tag}_max_ok")
        neg_chain = c.sem(st, f"{tag}_neg_chain")
        fin_chain = c.sem(st, f"{tag}_fin_chain")
        vcls_ok = c.sem(st, f"{tag}_vcls_ok")
        neg_ok = c.sem(st, f"{tag}_neg_ok")
        sc_ok = c.sem(st, f"{tag}_sc_ok")
        nt_mm = c.sem(st, f"{tag}_nt_mm")
        nt_out = c.sem(st, f"{tag}_nt_out")
        pcls_ok = c.sem(st, f"{tag}_pcls_ok")
        st_mm = c.sem(st, f"{tag}_st_mm")
        exp_ok = c.sem(st, f"{tag}_exp_ok")
        pv_mm = c.sem(st, f"{tag}_pv_mm")
        pv_out = c.sem(st, f"{tag}_pv_out")
        bt_mm = c.sem(st, f"{tag}_bt_mm")
        fin_ok = c.sem(st, f"{tag}_fin_ok")
        block = st.enter_context(nc.Block())

        def keys(qt):
            return (qt + 1) * P if causal else S

        def q_from(kt):
            return kt * P if causal else 0

        @block.sync
        def _(sp):
            for s in range(B * G):
                b, g = s // G, s % G
                if s >= G:
                    sp.wait_ge(pv_mm, 2 + NQ * (s - G + 1))
                load_step(sp, c, b, g, qs[g], ks[g], vs[g], loaded[g])
                if clear and s == G:
                    for xs in c.xs.values():
                        sp.dma_start(xs.rearrange("(p r) d -> p (r d)", p=P).rearrange("p (n w) -> p n w", w=D),
                                     c.zeros[:, :, :].broadcast_to([P, TILES, D])).then_inc(c.xs_clear, 16)

        @block.gpsimd
        def _(pool):
            for i in range(2, G):
                pool.memset(ks[i][PARTS * HD:P, :, :], 1.0).then_inc(ready, 1)

        @block.tensor
        def _(pe):
            def score_units(b, g, units_now):
                q, k = qs[g % G], ks[g % G]
                for u in units_now:
                    qt, h = u // HG, u % HG
                    if u == 0:
                        pe.wait_ge(loaded[g % G], b * (16 * NLOADS) + 16 * NLOADS * (g // G + 1))
                        pe.wait_ge(nt_out, b * 8 + (2 * g + 1))
                    pe.wait_ge(max_ok, b * (G * units) + (g * units + u + 1))
                    lhs = q[0:PARTS * HD, h, qt * P:qt * P + P]
                    if causal:
                        pe.matmul(ps_cls[:, u:u + 1], lhs, k[0:PARTS * HD, h, 0:1], start=True, stop=True)
                    mm = pe.matmul(ps_s[:, u % 2, 0:keys(qt)], lhs, k[0:PARTS * HD, h, k0:k0 + keys(qt)],
                                   start=True, stop=not causal)
                    if causal:
                        mm = pe.matmul(ps_s[:, u % 2, qt * P:qt * P + P], c.ident_bf[:, :], c.mask_qk[:, :],
                                       start=False, stop=True)
                    mm.then_inc(s_mm, 1)

            def turn_neg(b, g):
                pe.wait_ge(neg_ok, b * G + (g + 1))
                for u in range(units):
                    qt, h = u // HG, u % HG
                    mm = pe.transpose(neg_t[PARTS * HD:P, h, qt * P:qt * P + P], neg[:, u, :], c.ident_bf[:, :])
                mm.then_inc(nt_mm, 1)

            def second(b, g, kt, pr):
                q, k = qs[g % G], ks[g % G]
                if kt == 0 and pr == 0:
                    pe.wait_ge(nt_out, b * 8 + (2 * g + 3))
                pe.wait_ge(exp_ok, b * (G * 8) + (g * 8 + 2 * kt + pr + 1))
                for h in (2 * pr, 2 * pr + 1):
                    mm = pe.matmul(ps_st[:, h, q_from(kt):], k[:, h, k0 + kt * P:k0 + kt * P + P],
                                   q[:, h, q_from(kt):], start=True, stop=not causal)
                    if causal:
                        mm = pe.matmul(ps_st[:, h, kt * P:kt * P + P], c.ident_bf[:, :], c.mask_kq[:, :],
                                       start=False, stop=True)
                mm.then_inc(st_mm, 1)

            def values(b, g, kt):
                pe.wait_ge(exp_ok, b * (G * 8) + (g * 8 + 2 * kt + 4))
                if kt == 0:
                    pe.wait_ge(fin_ok, b * G + (g + 1))
                for h in range(HG):
                    mm = pe.matmul(ps_pv[h * STRIP:h * STRIP + STRIP, q_from(kt):],
                                   vs[g % G][:, kt, h * STRIP:h * STRIP + STRIP],
                                   et[:, kt % 2, h, q_from(kt):], start=kt == 0, stop=kt == NQ - 1)
                mm.then_inc(pv_mm, 1)

            def turn_back(b, g):
                pe.wait_ge(pv_out, b * G + (g + 1))
                for qt in range(NQ):
                    mm = pe.transpose(ps_pv[:, qt * P:qt * P + P], pv_rows[:, qt * P:qt * P + P], c.ident[:, :])
                mm.then_inc(bt_mm, 1)

            def step(b, g, before, more):
                ahead = [0]

                def scores(n):
                    if more:
                        score_units(b, g + 1, range(ahead[0], ahead[0] + n))
                    ahead[0] += n

                scores(FIRST_UNITS)
                if before:
                    turn_back(b, g - 1)
                for kt, (n0, n1, n2, n3) in enumerate(FIRST_PASS):
                    scores(n0)
                    second(b, g, kt + 1, 0)
                    scores(n1)
                    second(b, g, kt + 1, 1)
                    scores(n2)
                    values(b, g, kt)
                    scores(n3)
                values(b, g, NQ - 1)
                if more:
                    turn_neg(b, g + 1)
                    second(b, g + 1, 0, 0)
                    second(b, g + 1, 0, 1)

            pe.wait_ge(ready, G + 1)
            if causal:
                for b in range(B):
                    mm = pe.matmul(ps_st[:, b, 0:D], c.pick_cls[:, b, :], c.vcls[:, :], start=True, stop=True)
                mm.then_inc(vcls_mm, 1)
                pe.wait_ge(vcls_ok, 1)
            score_units(0, 0, range(units))
            turn_neg(0, 0)
            second(0, 0, 0, 0)
            second(0, 0, 0, 1)
            step(0, 0, False, True)
            with pe.Fori(0, B - 1) as b:
                for g in range(1, G + 1):
                    step(b, g, True, True)
            for g in range(1, G):
                step(B - 1, g, True, g + 1 < G)
            turn_back(B - 1, G - 1)

        @block.scalar
        def _(act):
            def cls_exp(b, g):
                act.wait_ge(sc_ok, b * G + (g + 1))
                if not (isinstance(b, int) and b == 0 and g == 0):
                    act.wait_ge(fin_ok, b * G + g)
                act.activation(p_cls[:, g % 2, :], cls_score[:, :], ACT.Exp).then_inc(pcls_ok, 1)

            def neg_copy(b, g):
                act.wait_ge(nt_mm, b * G + (g + 1))
                act.activation(qs[g % G][PARTS * HD:P, 0:2, :], neg_t[PARTS * HD:P, 0:2, :], ACT.Copy
                               ).then_inc(nt_out, 1)

            def step(b, g, more):
                for kt in range(NQ):
                    act.wait_ge(pv_mm, b * (G * NQ) + (g * NQ + kt + 1))
                    for pr in range(2):
                        act.wait_ge(st_mm, b * (G * 8) + (g * 8 + 2 * kt + pr + 1))
                        act.activation(et[:, kt % 2, 2 * pr:2 * pr + 2, q_from(kt):],
                                       ps_st[:, 2 * pr:2 * pr + 2, q_from(kt):], ACT.Exp).then_inc(exp_ok, 1)
                if more:
                    neg_copy(b, g + 1)
                act.wait_ge(pv_mm, b * (G * NQ) + (g * NQ + NQ + 2))
                act.activation(pv_rows[:, :], ps_pv[:, :], ACT.Copy).then_inc(pv_out, 1)
                if more and causal:
                    cls_exp(b, g + 1)

            act.sem_inc(exp_ok, 2)
            neg_copy(0, 0)
            if causal:
                cls_exp(0, 0)
            step(0, 0, True)
            with act.Fori(0, B - 1) as b:
                for g in range(1, G + 1):
                    step(b, g, True)
            for g in range(1, G):
                step(B - 1, g, g + 1 < G)

        n_neg = 3 if causal else 1
        n_fin = 4 if causal else 1

        @block.vector
        def _(dve):
            def maxima(b, g, units_now):
                for u in units_now:
                    qt = u // HG
                    if u == 0 and not (isinstance(b, int) and b == 0 and g == 0):
                        dve.wait_ge(neg_ok, b * G + g)
                    dve.wait_ge(s_mm, b * (G * units) + (g * units + u + 1))
                    dve.tensor_reduce(rowmax[:, u:u + 1], ps_s[:, u % 2, 0:keys(qt)], AX_X, ALU.max
                                      ).then_inc(max_ok, 1)

            def negate(b, g):
                base = b * (G * n_neg) + g * n_neg
                dve.wait_ge(max_ok, b * (G * units) + (g * units + units + 2))
                src = rowmax
                if causal:
                    dve.tensor_tensor(top[:, :], rowmax[:, :], ps_cls[:, 0:units], ALU.max).then_inc(neg_chain, 1)
                    dve.wait_ge(neg_chain, base + 1)
                    src = top
                dve.tensor_scalar(neg[:, :, 0], src[:, :], -1.0, None, ALU.mult).then_inc(neg_chain, 1)
                dve.wait_ge(neg_chain, base + (2 if causal else 1))
                dve.scalar_tensor_tensor(out=neg[:, :, 1], in0=src[:, :], scalar=-1.0, in1=neg[:, :, 0],
                                         op0=ALU.mult, op1=ALU.subtract).then_inc(neg_ok, 1)
                if causal:
                    dve.wait_ge(neg_ok, b * G + (g + 1))
                    dve.tensor_tensor(neg_sum[:, :], neg[:, :, 0], neg[:, :, 1], ALU.add).then_inc(neg_chain, 1)
                    dve.wait_ge(neg_chain, base + 3)
                    dve.wait_ge(pcls_ok, b * G + (g + 1))
                    dve.tensor_tensor(cls_score[:, :], ps_cls[:, 0:units], neg_sum[:, :], ALU.add
                                      ).then_inc(sc_ok, 1)
                dve.wait_ge(nt_mm, b * G + (g + 1))
                dve.tensor_copy(qs[g % G][PARTS * HD:P, 2:4, :], neg_t[PARTS * HD:P, 2:4, :]).then_inc(nt_out, 1)

            def finish(b, g):
                base = b * (G * n_fin) + g * n_fin
                image, columns = b + g // G, slice(g % G * HG * HD, (g % G + 1) * HG * HD)
                dve.wait_ge(bt_mm, b * G + (g + 1))
                dve.wait_ge(fin_ok, b * G + (g + 1))
                pc = p_cls[:, g % 2, :]
                if causal:
                    dve.wait_ge(pcls_ok, b * G + (g + 2))
                    dve.tensor_tensor(cls_part[:, :, :, :],
                                      pc.rearrange("p (n h a) -> p n h a", n=NQ, a=1).broadcast_to([P, NQ, HG, HD]),
                                      v_cls[:, bass.ds(image, 1), columns].rearrange(
                                          "p a (h d) -> p a h d", d=HD).broadcast_to([P, NQ, HG, HD]),
                                      ALU.mult).then_inc(fin_chain, 1)
                    dve.tensor_tensor(den[:, :].rearrange("p (n h) -> p n h", n=NQ), ctx_t[:, :, :, HD],
                                      pc.rearrange("p (n h) -> p n h", n=NQ), ALU.add).then_inc(fin_chain, 1)
                    dve.wait_ge(fin_chain, base + 2)
                    dve.reciprocal(rden[:, :], den[:, :]).then_inc(fin_chain, 1)
                    dve.tensor_tensor(raw[:, :, :, :], ctx_t[:, :, :, 0:HD], cls_part[:, :, :, :], ALU.add
                                      ).then_inc(fin_chain, 1)
                    dve.wait_ge(fin_chain, base + 4)
                    src = raw[:, :, :, :]
                else:
                    dve.reciprocal(rden[:, :].rearrange("p (n h) -> p n h", n=NQ), ctx_t[:, :, :, HD]
                                   ).then_inc(fin_chain, 1)
                    dve.wait_ge(fin_chain, base + 1)
                    src = ctx_t[:, :, :, 0:HD]
                dve.tensor_tensor(
                    c.ctx[:, bass.ds(image * NQ, NQ), columns].rearrange("p n (h d) -> p n h d", d=HD),
                    src, rden[:, :].rearrange("p (n h a) -> p n h a", n=NQ, a=1).broadcast_to([P, NQ, HG, HD]),
                    ALU.mult).then_inc(fin_ok, 1)

            def step(b, g, before, more):
                if more:
                    maxima(b, g + 1, range(FIRST_UNITS))
                if before:
                    finish(b, g - 1)
                if more:
                    maxima(b, g + 1, range(FIRST_UNITS, units))
                    negate(b, g + 1)

            dve.memset(neg[:, :, :], 0.0).then_inc(ready, 1)
            for i in range(2):
                dve.memset(ks[i][PARTS * HD:P, :, :], 1.0).then_inc(ready, 1)
            dve.wait_ge(ready, G + 1)
            dve.sem_inc(max_ok, 2)
            dve.sem_inc(pv_mm, 2)
            dve.sem_inc(fin_ok, 1)
            dve.sem_inc(nt_out, 1)
            dve.sem_inc(pcls_ok, 1)
            if causal:
                dve.wait_ge(vcls_mm, 1)
                dve.tensor_copy(v_cls[:, :, :], ps_st[:, :, 0:D]).then_inc(vcls_ok, 1)
                dve.tensor_copy(c.ctx[0:B, NT, :], c.vcls[:, :]).then_inc(cls_row, 1)
            maxima(0, 0, range(units))
            negate(0, 0)
            step(0, 0, False, True)
            with dve.Fori(0, B - 1) as b:
                for g in range(1, G + 1):
                    step(b, g, True, True)
            for g in range(1, G):
                step(B - 1, g, True, g + 1 < G)
            finish(B - 1, G - 1)


def attend_top(c, tag):
    nc = c.nc
    units = NQ * HG
    pairs = units // 2
    rounds = K_TOP // 8
    ops = 2 * rounds
    WIDE = S + 1
    with c.stage() as st:
        qs = [c.sbuf(st, f"{tag}_qs{i}", [P, HG, S], BF16) for i in range(2)]
        ks = [c.sbuf(st, f"{tag}_ks{i}", [P, HG, WIDE], BF16) for i in range(2)]
        vs = [c.sbuf(st, f"{tag}_vs{i}", [P, NQ, P], F32) for i in range(2)]
        largest = c.sbuf(st, f"{tag}_largest", [P, 4, rounds, 8], F32)
        raw = c.sbuf(st, f"{tag}_raw", [P, 4, WIDE], F32)
        left = c.sbuf(st, f"{tag}_left", [P, 4, WIDE], F32)
        neg_max = c.sbuf(st, f"{tag}_neg_max", [P, 4], F32)
        e_all = c.sbuf(st, f"{tag}_e_all", [P, 4, WIDE], F32)
        e_left = c.sbuf(st, f"{tag}_e_left", [P, 2, WIDE], F32)
        prob = c.sbuf(st, f"{tag}_prob", [P, 2, HG, WIDE], F32)
        prob_t = c.sbuf(st, f"{tag}_prob_t", [P, 2, HG, S], F32)
        pv_rows = c.sbuf(st, f"{tag}_pv_rows", [P, P], F32)
        back = c.sbuf(st, f"{tag}_back", [P, HG, STRIP], F32)
        v_cls = c.sbuf(st, f"{tag}_v_cls", [P, B, D], F32)
        cls_part = c.sbuf(st, f"{tag}_cls_part", [P, HG, HD], F32)
        den = c.sbuf(st, f"{tag}_den", [P, NT, NH], F32)
        rden = c.sbuf(st, f"{tag}_rden", [P, NT, NH], F32)
        ps_s = c.psum(st, f"{tag}_ps_s", [P, 2, 2 * S])
        ps_t = c.psum(st, f"{tag}_ps_pt", [P, 2, S])
        ps_pv = c.psum(st, f"{tag}_ps_pv", [P, S])
        ps_back = c.psum(st, f"{tag}_ps_back", [P, S])

        loaded = [c.sem(st, f"{tag}_loaded{i}") for i in range(2)]
        vcls_mm = c.sem(st, f"{tag}_vcls_mm")
        vcls_ok = c.sem(st, f"{tag}_vcls_ok")
        s_mm = c.sem(st, f"{tag}_s_mm")
        raw_ok = c.sem(st, f"{tag}_raw_ok")
        pick = c.sem(st, f"{tag}_pick")
        neg_ok = c.sem(st, f"{tag}_neg_ok")
        all_ok = c.sem(st, f"{tag}_all_ok")
        left_ok = c.sem(st, f"{tag}_left_ok")
        prob_ok = c.sem(st, f"{tag}_prob_ok")
        t_mm = c.sem(st, f"{tag}_pt_mm")
        t_out = c.sem(st, f"{tag}_pt_out")
        pv_mm = c.sem(st, f"{tag}_pv_mm")
        pv_out = c.sem(st, f"{tag}_pv_out")
        bt_mm = c.sem(st, f"{tag}_bt_mm")
        back_ok = c.sem(st, f"{tag}_back_ok")
        part_ok = c.sem(st, f"{tag}_part_ok")
        fin_ok = c.sem(st, f"{tag}_fin_ok")
        scale_ok = c.sem(st, f"{tag}_scale_ok")
        block = st.enter_context(nc.Block())

        def keys(qt):
            return (qt + 1) * P

        def row(i, qt):
            return ps_s[:, i, S - 1:S + keys(qt)]

        def unit(b, g, u):
            return b * (G * units) + (g * units + u)

        def group(b, g, qt):
            return b * (G * NQ) + (g * NQ + qt)

        def picked(b, g, k, j, i):
            return b * (G * pairs * 2 * ops) + ((g * pairs + k) * 2 * ops + 2 * j + i + 1 + 4 * ops)

        def ahead(do, b, g, k, more):
            if k + 2 < pairs:
                do(b, g, k + 2)
            elif more:
                do(b, g + 1, k + 2 - pairs)

        def with_before(b, g, before):
            for k in range(pairs):
                yield k, ((b, g, k - 1) if k else (b, g - 1, pairs - 1) if before else None)

        def over_steps(eng, step):
            step(0, 0, False, True)
            with eng.Fori(0, B - 1) as b:
                for g in range(1, G + 1):
                    step(b, g, True, True)
            for g in range(1, G):
                step(B - 1, g, True, g + 1 < G)

        @block.sync
        def _(sp):
            for s in range(B * G):
                b, g = s // G, s % G
                if s >= 2:
                    sp.wait_ge(pv_mm, 2 + NQ * (s - 1))
                load_step(sp, c, b, g, qs[s % 2], ks[s % 2], vs[s % 2], loaded[s % 2])

        @block.tensor
        def _(pe):
            def score_pair(b, g, k):
                q, kk = qs[g % 2], ks[g % 2]
                qt = 2 * k // HG
                if k == 0:
                    pe.wait_ge(loaded[g % 2], b * (32 * NLOADS) + 16 * NLOADS * (g // 2 + 1))
                for i in range(2):
                    h = (2 * k + i) % HG
                    pe.wait_ge(raw_ok, unit(b, g, 2 * k + i + 1))
                    lhs = q[0:PARTS * HD, h, qt * P:qt * P + P]
                    pe.matmul(ps_s[:, i, S - 1:S], lhs, kk[0:PARTS * HD, h, 0:1], start=True, stop=True)
                    pe.matmul(ps_s[:, i, S:S + keys(qt)], lhs, kk[0:PARTS * HD, h, 1:1 + keys(qt)],
                              start=True, stop=False)
                    pe.matmul(ps_s[:, i, S + qt * P:S + qt * P + P], c.ident_bf[:, :], c.mask_qk[:, :],
                              start=False, stop=True).then_inc(s_mm, 1)

            def turn_pair(b, g, k):
                qt = 2 * k // HG
                for i in range(2):
                    u = 2 * k + i
                    pe.wait_ge(prob_ok, unit(b, g, u + 5))
                    pe.wait_ge(t_out, unit(b, g, u + 1))
                    for ch in range(qt + 1):
                        mm = pe.transpose(ps_t[:, i, ch * P:ch * P + P],
                                          prob[:, qt % 2, u % HG, 1 + ch * P:1 + ch * P + P], c.ident[:, :])
                    mm.then_inc(t_mm, 1)

            def values(b, g, qt):
                pe.wait_ge(t_out, unit(b, g, qt * HG + HG + 2))
                for ch in range(qt + 1):
                    for h in range(HG):
                        mm = pe.matmul(ps_pv[h * STRIP:h * STRIP + STRIP, 0:P],
                                       vs[g % 2][:, ch, h * STRIP:h * STRIP + STRIP],
                                       prob_t[:, qt % 2, h, ch * P:ch * P + P], start=ch == 0, stop=ch == qt)
                mm.then_inc(pv_mm, 1)
                pe.wait_ge(pv_out, group(b, g, qt + 1))
                pe.transpose(ps_back[:, 0:P], pv_rows[:, :], c.ident[:, :]).then_inc(bt_mm, 1)

            def use(b, g, k):
                turn_pair(b, g, k)
                if 2 * k % HG == HG - 2:
                    values(b, g, 2 * k // HG)

            def step(b, g, before, more):
                for k, last in with_before(b, g, before):
                    ahead(score_pair, b, g, k, more)
                    if last:
                        use(*last)

            for b in range(B):
                mm = pe.matmul(ps_s[:, b // 2, b % 2 * S:b % 2 * S + D], c.pick_cls[:, b, :], c.vcls[:, :],
                               start=True, stop=True)
            mm.then_inc(vcls_mm, 1)
            pe.wait_ge(vcls_ok, 2)
            score_pair(0, 0, 0)
            score_pair(0, 0, 1)
            over_steps(pe, step)
            use(B - 1, G - 1, pairs - 1)

        @block.scalar
        def _(act):
            def copy_pair(b, g, k):
                qt = 2 * k // HG
                for i in range(2):
                    act.wait_ge(s_mm, unit(b, g, 2 * k + i + 1))
                    act.wait_ge(pick, picked(b, g, k, 1, i) - 4 * ops)
                    act.wait_ge(all_ok, unit(b, g, 2 * k + i + 1))
                    act.activation(raw[:, 2 * (k % 2) + i, 0:1 + keys(qt)], row(i, qt), ACT.Copy
                                   ).then_inc(raw_ok, 1)

            def use(b, g, k):
                qt = 2 * k // HG
                w = 1 + keys(qt)
                for i in range(2):
                    u = 2 * k + i
                    act.wait_ge(t_mm, unit(b, g, u + 9))
                    act.wait_ge(pv_mm, group(b, g, qt + 1))
                    act.activation(prob_t[:, qt % 2, u % HG, 0:w - 1], ps_t[:, i, 0:w - 1], ACT.Copy
                                   ).then_inc(t_out, 1)
                if 2 * k % HG == HG - 2:
                    act.wait_ge(pv_mm, group(b, g, qt + 3))
                    act.activation(pv_rows[:, :], ps_pv[:, 0:P], ACT.Copy).then_inc(pv_out, 1)
                    act.wait_ge(bt_mm, group(b, g, qt + 1))
                    act.wait_ge(fin_ok, group(b, g, qt + 1))
                    act.activation(back[:, :, :], ps_back[:, 0:P].rearrange("p (h s) -> p h s", s=STRIP),
                                   ACT.Copy).then_inc(back_ok, 1)

            def step(b, g, before, more):
                for k, last in with_before(b, g, before):
                    qt = 2 * k // HG
                    w = 1 + keys(qt)
                    for i in range(2):
                        u, j = 2 * k + i, 2 * (k % 2) + i
                        act.wait_ge(neg_ok, unit(b, g, u + 5))
                        act.wait_ge(prob_ok, unit(b, g, u + 1))
                        act.activation(e_all[:, j, 0:w], raw[:, j, 0:w], ACT.Exp, bias=neg_max[:, j:j + 1]
                                       ).then_inc(all_ok, 1)
                    ahead(copy_pair, b, g, k, more)
                    for i in range(2):
                        u, j = 2 * k + i, 2 * (k % 2) + i
                        act.wait_ge(pick, picked(b, g, k, ops - 1, i))
                        act.wait_ge(prob_ok, unit(b, g, u + 3))
                        act.activation(e_left[:, i, 0:w], left[:, j, 0:w], ACT.Exp, bias=neg_max[:, j:j + 1]
                                       ).then_inc(left_ok, 1)
                    if last:
                        use(*last)

            act.sem_inc(raw_ok, 2)
            act.sem_inc(all_ok, 4)
            act.sem_inc(left_ok, 4)
            act.sem_inc(t_out, 2)
            act.wait_ge(vcls_ok, 2)
            copy_pair(0, 0, 0)
            copy_pair(0, 0, 1)
            over_steps(act, step)
            use(B - 1, G - 1, pairs - 1)

        @block.gpsimd
        def _(pool):
            def use(b, g, k):
                qt = 2 * k // HG
                w = 1 + keys(qt)
                for i in range(2):
                    u = 2 * k + i
                    pool.wait_ge(left_ok, unit(b, g, u + 5))
                    pool.wait_ge(t_mm, unit(b, g, u + 1))
                    pool.wait_ge(fin_ok, group(b, g, qt + 1))
                    pool.tensor_tensor(prob[:, qt % 2, u % HG, 0:w], e_all[:, 2 * (k % 2) + i, 0:w],
                                       e_left[:, i, 0:w], ALU.subtract).then_inc(prob_ok, 1)

            def finish(b, g, qt):
                p_cls = prob[:, qt % 2, :, 0:1]
                image, columns = b + g // G, slice(g % G * HG * HD, (g % G + 1) * HG * HD)
                n = image * NQ + qt
                pool.wait_ge(prob_ok, unit(b, g, qt * HG + HG + 4))
                pool.nop(nofuse=True)
                pool.tensor_tensor(cls_part[:, :, :], p_cls.broadcast_to([P, HG, HD]),
                                   v_cls[:, bass.ds(image, 1), columns].rearrange("p a (h d) -> p (a h) d", d=HD),
                                   ALU.mult).then_inc(part_ok, 1)
                pool.wait_ge(back_ok, group(b, g, qt + 1))
                pool.wait_ge(part_ok, 2 * group(b, g, qt) + 1)
                pool.nop(nofuse=True)
                pool.tensor_tensor(den[:, bass.ds(n, 1), g % G * HG:g % G * HG + HG].rearrange("p a h -> p (a h)"),
                                   back[:, :, HD], prob[:, qt % 2, :, 0], ALU.add).then_inc(part_ok, 1)
                pool.wait_ge(part_ok, 2 * group(b, g, qt) + 2)
                pool.nop(nofuse=True)
                pool.tensor_tensor(c.ctx[:, bass.ds(n, 1), columns].rearrange("p a (h d) -> p (a h) d", d=HD),
                                   back[:, :, 0:HD], cls_part[:, :, :], ALU.add).then_inc(fin_ok, 1)

            def step(b, g, before, more):
                for k, last in with_before(b, g, before):
                    for i in range(2):
                        u, j = 2 * k + i, 2 * (k % 2) + i
                        pool.wait_ge(pick, picked(b, g, k, 0, i))
                        pool.wait_ge(left_ok, unit(b, g, u + 1))
                        pool.nop(nofuse=True)
                        pool.tensor_scalar(neg_max[:, j:j + 1], largest[:, j, 0, 0:1], -1.0, None, ALU.mult
                                           ).then_inc(neg_ok, 1)
                    if last:
                        if last[2] % 2 == 0 and (before or k > 1):
                            finish(*((last[0], last[1], last[2] // 2 - 1) if last[2] else
                                     (last[0], last[1] - 1, NQ - 1)))
                        use(*last)

            pool.sem_inc(prob_ok, 4)
            pool.sem_inc(fin_ok, 1)
            pool.wait_ge(vcls_ok, 2)
            over_steps(pool, step)
            use(B - 1, G - 1, pairs - 1)
            finish(B - 1, G - 1, NQ - 1)

        @block.vector
        def _(dve):
            def step(b, g):
                for k in range(pairs):
                    qt = 2 * k // HG
                    w = 1 + keys(qt)
                    for j in range(ops):
                        for i in range(2):
                            u, at = 2 * k + i, 2 * (k % 2) + i
                            src = raw[:, at, 0:w] if j < 2 else left[:, at, 0:w]
                            if j == 0:
                                dve.wait_ge(raw_ok, unit(b, g, u + 3))
                                dve.wait_ge(pick, picked(b, g, k, ops - 1, i) - 4 * ops)
                                dve.wait_ge(neg_ok, unit(b, g, u + 1))
                            else:
                                dve.wait_ge(pick, picked(b, g, k, j - 1, i))
                            if j == 1:
                                dve.wait_ge(left_ok, unit(b, g, u + 1))
                            dve.nop(nofuse=True)
                            if j % 2 == 0:
                                ins = dve.max(largest[:, at, j // 2, :], src)
                            else:
                                ins = dve.match_replace(left[:, at, 0:w], largest[:, at, j // 2, :], src, TAKEN)
                            ins.then_inc(pick, 1)

            dve.sem_inc(pick, 4 * ops)
            dve.sem_inc(neg_ok, 4)
            dve.sem_inc(t_mm, 8)
            dve.sem_inc(pv_mm, 2)
            dve.wait_ge(vcls_mm, 1)
            for i in range(2):
                dve.tensor_copy(v_cls[:, 2 * i:2 * i + 2, :], ps_s[:, i, :].rearrange("p (a n) -> p a n", a=2)[:, :, 0:D]
                                ).then_inc(vcls_ok, 1)
            dve.tensor_copy(c.ctx[0:B, NT, :], c.vcls[:, :]).then_inc(scale_ok, 1)
            with dve.Fori(0, B) as b:
                for g in range(G):
                    step(b, g)
            dve.wait_ge(fin_ok, 1 + B * G * NQ)
            dve.reciprocal(rden[:, :, :], den[:, :, :]).then_inc(scale_ok, 1)
            dve.wait_ge(scale_ok, 2)
            for n in range(NT):
                ctx_n = c.ctx[:, n, :].rearrange("p (h d) -> p h d", d=HD)
                dve.tensor_tensor(ctx_n, ctx_n,
                                  rden[:, n, :].rearrange("p (h a) -> p h a", a=1).broadcast_to([P, NH, HD]),
                                  ALU.mult).then_inc(scale_ok, 1)


def attend_out(c, tag, wo_dram, bo_dram, residual, cls):
    nc = c.nc
    tiles = NT + (1 if cls else 0)
    with c.stage() as st:
        wo = c.sbuf(st, f"{tag}_wo", [P, DC, D], F32)
        bo = c.sbuf(st, f"{tag}_bo", [P, D], F32)
        ctx_t = c.sbuf(st, f"{tag}_ctx_t", [P, 2, DC, P], F32)
        summed = c.sbuf(st, f"{tag}_summed", [P, 2, D], F32)
        ps_t = c.psum(st, f"{tag}_ps_t", [P, 2, S])
        ps_o = c.psum(st, f"{tag}_ps_o", [P, 2, S])
        w_in = c.sem(st, f"{tag}_wo_in")
        t_mm = c.sem(st, f"{tag}_t_mm")
        t_out = c.sem(st, f"{tag}_t_out")
        o_mm = c.sem(st, f"{tag}_o_mm")
        sum_ok = c.sem(st, f"{tag}_sum_ok")
        h_ok = c.sem(st, f"{tag}_h_ok")
        block = st.enter_context(nc.Block())

        def rows(n):
            return P if n < NT else B

        @block.sync
        def _(sp):
            sp.dma_start(wo[:, :, :], wo_dram).then_inc(w_in, 16)
            sp.dma_start(bo[:, :], bo_dram.partition_broadcast(P)).then_inc(w_in, 16)

        @block.tensor
        def _(pe):
            def turn(n):
                r = rows(n)
                if n >= 2:
                    pe.wait_ge(t_out, n - 1)
                for ch in range(DC):
                    mm = pe.transpose(ps_t[:, n % 2, ch * P:ch * P + r], c.ctx[0:r, n, ch * P:ch * P + P],
                                      c.ident[0:r, 0:r])
                mm.then_inc(t_mm, 1)

            turn(0)
            pe.wait_ge(w_in, 32)
            for n in range(tiles):
                if n + 1 < tiles:
                    turn(n + 1)
                pe.wait_ge(t_out, n + 1)
                if n >= 2:
                    pe.wait_ge(sum_ok, n - 1)
                for ch in range(DC):
                    mm = pe.matmul(ps_o[0:rows(n), n % 2, 0:D], ctx_t[:, n % 2, ch, 0:rows(n)], wo[:, ch, :],
                                   start=ch == 0, stop=ch == DC - 1)
                mm.then_inc(o_mm, 1)

        @block.scalar
        def _(act):
            for n in range(tiles):
                act.wait_ge(t_mm, n + 1)
                if n >= 2:
                    act.wait_ge(o_mm, n - 1)
                r = rows(n)
                act.activation(ctx_t[:, n % 2, :, 0:r],
                               ps_t[:, n % 2, 0:DC * P].rearrange("p (c t) -> p c t", c=DC)[:, :, 0:r],
                               ACT.Copy).then_inc(t_out, 1)

        @block.vector
        def _(dve):
            dve.wait_ge(w_in, 32)
            for n in range(tiles):
                r = rows(n)
                dve.wait_ge(o_mm, n + 1)
                if residual:
                    if n >= 2:
                        dve.wait_ge(h_ok, n - 1)
                    dve.tensor_tensor(summed[0:r, n % 2, :], ps_o[0:r, n % 2, 0:D], bo[0:r, :], ALU.add
                                      ).then_inc(sum_ok, 1)
                    dve.wait_ge(sum_ok, n + 1)
                    dve.tensor_tensor(c.h[0:r, n, :], c.h[0:r, n, :], summed[0:r, n % 2, :], ALU.add
                                      ).then_inc(h_ok, 1)
                else:
                    dve.tensor_tensor(c.h[0:r, n, :], ps_o[0:r, n % 2, 0:D], bo[0:r, :], ALU.add
                                      ).then_inc(sum_ok, 1)


def dispatch(c, tag, xn, idx):
    nc = c.nc
    n_all = NT + 1
    with c.stage() as st:
        chosen = c.sbuf(st, f"{tag}_chosen", [P, 2, n_all, E], F32)
        both = c.sbuf(st, f"{tag}_both", [P, n_all, E], BF16)
        base = c.sbuf(st, f"{tag}_base", [P, n_all + 1, E], F32)
        begin = c.sbuf(st, f"{tag}_begin", [P, E + 1], F32)
        tiles = c.sbuf(st, f"{tag}_tiles", [P, E], F32)
        over = c.sbuf(st, f"{tag}_over", [P, E, n_all], F32)
        slot = c.sbuf(st, f"{tag}_slot", [P, n_all, E], F32)
        slot_in = c.sbuf(st, f"{tag}_slot_in", [P, n_all, E], F32)
        mine = c.sbuf(st, f"{tag}_mine", [P, 2, n_all, E], F32)
        at = c.sbuf(st, f"{tag}_at", [P, 2, n_all], F32)
        has = c.sbuf(st, f"{tag}_has", [P, 2, n_all], F32)
        past = c.sbuf(st, f"{tag}_past", [P, TILES, E - 1], F32)
        owner_f = c.sbuf(st, f"{tag}_owner_f", [P, TILES], F32)
        ps_rank = c.psum(st, f"{tag}_ps_rank", [P, S])
        ps_total = c.psum(st, f"{tag}_ps_total", [P, S])
        both_ok = c.sem(st, f"{tag}_both_ok")
        rank_mm = c.sem(st, f"{tag}_rank_mm")
        chain = c.sem(st, f"{tag}_d_chain")
        row_ok = c.sem(st, f"{tag}_row_ok")
        sent = c.sem(st, f"{tag}_sent")
        block = st.enter_context(nc.Block())
        rank = ps_rank[:, 0:n_all * E].rearrange("p (n e) -> p n e", e=E)
        total = ps_total[:, 0:n_all * E].rearrange("p (n e) -> p n e", e=E)

        @block.vector
        def _(dve):
            done = [0]

            def then(ins):
                done[0] += 1
                ins.then_inc(chain, 1)
                dve.wait_ge(chain, done[0])

            for k in range(2):
                then(dve.tensor_tensor(chosen[:, k, :, :],
                                       c.iota_e[:, :].rearrange("p (a e) -> p a e", a=1).broadcast_to([P, n_all, E]),
                                       idx[:, :, k:k + 1].broadcast_to([P, n_all, E]), ALU.is_equal))
                then(dve.tensor_tensor(chosen[:, k, :, :], chosen[:, k, :, :],
                                       c.valid[:, :].rearrange("p (n a) -> p n a", a=1).broadcast_to([P, n_all, E]),
                                       ALU.mult))
            dve.tensor_tensor(both[:, :, :], chosen[:, 0, :, :], chosen[:, 1, :, :], ALU.add).then_inc(both_ok, 1)
            then(dve.memset(base[:, 0, :], 0.0))
            dve.wait_ge(rank_mm, 2)
            for n in range(n_all):
                then(dve.tensor_tensor(base[:, n + 1, :], base[:, n, :], total[:, n, :], ALU.add))
            then(dve.tensor_tensor(over[:, :, :],
                                   base[:, n_all, :].rearrange("p (e a) -> p e a", a=1).broadcast_to([P, E, n_all]),
                                   c.steps[:, :].rearrange("p (a n) -> p a n", a=1).broadcast_to([P, E, n_all]),
                                   ALU.is_gt))
            then(dve.tensor_reduce(tiles[:, :], over[:, :, :], AX_X, ALU.add))
            then(dve.memset(begin[:, 0:1], 0.0))
            for e in range(E):
                then(dve.tensor_tensor(begin[:, e + 1:e + 2], begin[:, e:e + 1], tiles[:, e:e + 1], ALU.add))
            then(dve.scalar_tensor_tensor(
                out=slot_in[:, :, :], in0=begin[:, 0:E].rearrange("p (a e) -> p a e", a=1).broadcast_to([P, n_all, E]),
                scalar=float(P), in1=base[:, 0:n_all, :], op0=ALU.mult, op1=ALU.add))
            then(dve.tensor_tensor(slot[:, :, :], slot_in[:, :, :], rank, ALU.add))
            for k in range(2):
                then(dve.tensor_tensor(mine[:, k, :, :], chosen[:, k, :, :], slot[:, :, :], ALU.mult))
            then(dve.tensor_reduce(at[:, :, :], mine[:, :, :, :], AX_X, ALU.add))
            then(dve.tensor_reduce(has[:, :, :], chosen[:, :, :, :], AX_X, ALU.add))
            then(dve.scalar_tensor_tensor(out=at[:, :, :], in0=has[:, :, :], scalar=-float(NOWHERE),
                                          in1=at[:, :, :], op0=ALU.mult, op1=ALU.add))
            dve.tensor_scalar(c.row[:, :, :], at[:, :, :], float(NOWHERE), None, ALU.add).then_inc(row_ok, 1)
            then(dve.tensor_tensor(past[:, :, :],
                                   c.iota_t[:, :].rearrange("p (t a) -> p t a", a=1).broadcast_to([P, TILES, E - 1]),
                                   begin[:, 1:E].rearrange("p (a e) -> p a e", a=1).broadcast_to([P, TILES, E - 1]),
                                   ALU.is_ge))
            then(dve.tensor_reduce(owner_f[:, :], past[:, :, :], AX_X, ALU.add))
            dve.tensor_copy(c.owner[:, :], owner_f[:, :]).then_inc(row_ok, 1)
            dve.tensor_copy(c.used[:, :], begin[:, E:E + 1]).then_inc(row_ok, 1)

        @block.tensor
        def _(pe):
            pe.wait_ge(both_ok, 1)
            pe.matmul(ps_rank[:, 0:n_all * E], c.before[:, :], both[:, :, :], start=True, stop=True
                      ).then_inc(rank_mm, 1)
            pe.matmul(ps_total[:, 0:n_all * E], c.ones_bf[:, :], both[:, :, :], start=True, stop=True
                      ).then_inc(rank_mm, 1)

        @block.gpsimd
        def _(pool):
            pool.wait_ge(c.xs_clear, 16 * len(c.xs))
            pool.wait_ge(row_ok, 3)
            used = pool.value_load(c.used[0:1, 0:1], min_val=0, max_val=TILES)
            with pool.If(used > 0):
                for n in range(n_all):
                    for k in range(2):
                        pool.indirect_dma_start(
                            out=c.xs[tag][:, :], out_offset=bass.IndirectOffsetOnAxis(ap=c.row[:, k, n:n + 1], axis=0),
                            in_=xn[:, n, :], in_offset=None, bounds_check=TILES * P - 1, oob_is_err=False
                        ).then_inc(sent, 16)
                pool.wait_ge(sent, 16 * 2 * n_all)


def run_gated_experts(c, tag, w_in_dram, w_out_dram, hidden):
    nc = c.nc
    wide = 2 * hidden
    HC = hidden // P
    with c.stage() as st:
        w1 = c.sbuf(st, f"{tag}_w1", [P, DC, E, wide], F32)
        w2 = c.sbuf(st, f"{tag}_w2", [P, HC, E, D], F32)
        rows = c.sbuf(st, f"{tag}_rows", [P, 2, D], F32)
        rows_t = c.sbuf(st, f"{tag}_rows_t", [P, 2, DC, P], F32)
        hid = c.sbuf(st, f"{tag}_hid", [P, 2, hidden], F32)
        hid_t = c.sbuf(st, f"{tag}_hid_t", [P, 2, HC, P], F32)
        y = c.sbuf(st, f"{tag}_y", [P, 2, D], F32)
        act_gate = c.sbuf(st, f"{tag}_act_gate", [P, 2, hidden], F32)
        ps_x = c.psum(st, f"{tag}_ps_x", [P, S])
        ps_h = c.psum(st, f"{tag}_ps_h", [P, 2, 2, S])
        ps_ht = c.psum(st, f"{tag}_ps_ht", [P, S])
        ps_y = c.psum(st, f"{tag}_ps_y", [P, S])
        w_in = c.sem(st, f"{tag}_ew_in")
        rows_in = [c.sem(st, f"{tag}_rows_in{i}") for i in range(2)]
        x_mm = c.sem(st, f"{tag}_x_mm")
        x_out = c.sem(st, f"{tag}_x_out")
        h_mm = c.sem(st, f"{tag}_h_mm")
        gate_ok = c.sem(st, f"{tag}_gate_ok")
        hid_ok = c.sem(st, f"{tag}_hid_ok")
        ht_mm = c.sem(st, f"{tag}_ht_mm")
        ht_out = c.sem(st, f"{tag}_ht_out")
        y_mm = c.sem(st, f"{tag}_y_mm")
        y_ok = c.sem(st, f"{tag}_y_ok")
        y_sent = [c.sem(st, f"{tag}_y_sent{i}") for i in range(2)]
        block = st.enter_context(nc.Block())

        def used_tiles(eng):
            return eng.value_load(c.used[0:1, 0:1], min_val=0, max_val=TILES)

        @block.sync
        def _(sp):
            def load_rows(i):
                sp.dma_start(rows[:, i % 2, :], c.xs[tag][i * P:(i + 1) * P, :]).then_inc(rows_in[i % 2], 16)

            used = used_tiles(sp)
            for i in range(2):
                sp.sem_inc(y_sent[i], 16)
                load_rows(i)
            sp.dma_start(w1[:, :, :, :], w_in_dram).then_inc(w_in, 16)
            sp.dma_start(w2[:, :, :, :], w_out_dram).then_inc(w_in, 16)
            lag = 3
            for i in range(TILES + lag):
                if 2 <= i < TILES:
                    with sp.If(used > i - 2):
                        sp.wait_ge(x_mm, i - 1)
                        load_rows(i)
                j = i - lag
                if j >= 0:
                    with sp.If(used > j):
                        sp.wait_ge(y_ok, j + 2)
                        sp.dma_start(c.ys[tag][j * P:(j + 1) * P, :], y[:, j % 2, :]).then_inc(y_sent[j % 2], 16)
                    with sp.Else():
                        sp.dma_start(c.ys[tag][j * P:(j + 1) * P, :], c.zeros[:, 0, :]).then_inc(y_sent[j % 2], 16)
            for i in range(2):
                sp.wait_ge(y_sent[i], 16 + 16 * (TILES // 2))

        @block.tensor
        def _(pe):
            def turn_rows(it, k):
                pe.wait_ge(rows_in[k % 2], it * 16 + 16 * (k // 2 + 1))
                pe.wait_ge(x_out, it * 2 + (k + 1))
                for ch in range(DC):
                    mm = pe.transpose(ps_x[:, ch * P:ch * P + P], rows[:, k % 2, ch * P:ch * P + P], c.ident[:, :])
                mm.then_inc(x_mm, 1)

            def first(it, k):
                e = pe.value_load(c.owner[0:1, bass.ds(it * 2 + k, 1)], min_val=0, max_val=E - 1)
                pe.wait_ge(x_out, it * 2 + (k + 2))
                pe.wait_ge(hid_ok, it * 2 + (k + 1))
                for half in range(2):
                    for ch in range(DC):
                        mm = pe.matmul(ps_h[:, k % 2, half, :], rows_t[:, k % 2, ch, :],
                                       w1[:, ch, bass.ds(e, 1), half * S:half * S + S].rearrange("p a n -> p (a n)"),
                                       start=ch == 0, stop=ch == DC - 1)
                mm.then_inc(h_mm, 1)

            def turn_hidden(it, k):
                pe.wait_ge(hid_ok, it * 2 + (k + 3))
                for j in range(HC):
                    mm = pe.transpose(ps_ht[:, j * P:j * P + P], hid[:, k % 2, j * P:(j + 1) * P], c.ident[:, :])
                mm.then_inc(ht_mm, 1)

            def second(it, k, e):
                pe.wait_ge(ht_out, it * 2 + (k + 1))
                pe.wait_ge(y_ok, it * 2 + (k + 1))
                for j in range(HC):
                    mm = pe.matmul(ps_y[:, 0:D], hid_t[:, k % 2, j, :],
                                   w2[:, j, bass.ds(e, 1), :].rearrange("p a n -> p (a n)"),
                                   start=j == 0, stop=j == HC - 1)
                mm.then_inc(y_mm, 1)

            def slot(it, k, more, more2):
                e = pe.value_load(c.owner[0:1, bass.ds(it * 2 + k, 1)], min_val=0, max_val=E - 1)
                if more:
                    first(it, k + 1)
                turn_hidden(it, k)
                if more2:
                    turn_rows(it, k + 2)
                second(it, k, e)

            used = used_tiles(pe)
            turn_rows(0, 0)
            turn_rows(0, 1)
            pe.wait_ge(w_in, 32)
            first(0, 0)
            with pe.Fori(0, TILES // 2 - 1) as it:
                for k in range(2):
                    with pe.If(used > it * 2 + k):
                        slot(it, k, True, True)
            for k in range(2):
                with pe.If(used > TILES - 2 + k):
                    slot(TILES // 2 - 1, k, k == 0, False)

        @block.scalar
        def _(act):
            def rows_copy(it, k):
                act.wait_ge(x_mm, it * 2 + (k + 1))
                if not (isinstance(it, int) and it * 2 + k < 2):
                    act.wait_ge(h_mm, it * 2 + (k - 1))
                act.activation(rows_t[:, k % 2, :, :], ps_x[:, 0:DC * P].rearrange("p (c t) -> p c t", c=DC),
                               ACT.Copy).then_inc(x_out, 1)

            def gate(it, k):
                act.wait_ge(h_mm, it * 2 + (k + 1))
                act.wait_ge(hid_ok, it * 2 + (k + 1))
                act.activation(act_gate[:, k % 2, :], ps_h[:, k % 2, 0, :], ACT.Silu).then_inc(gate_ok, 1)

            def hidden_copy(it, k):
                act.wait_ge(ht_mm, it * 2 + (k + 1))
                act.wait_ge(y_mm, it * 2 + (k + 1))
                act.activation(hid_t[:, k % 2, :, :], ps_ht[:, :].rearrange("p (c t) -> p c t", c=HC),
                               ACT.Copy).then_inc(ht_out, 1)

            def slot(it, k, more, more2):
                if more:
                    gate(it, k + 1)
                hidden_copy(it, k)
                if more2:
                    rows_copy(it, k + 2)

            act.sem_inc(x_out, 1)
            act.sem_inc(y_mm, 2)
            used = used_tiles(act)
            rows_copy(0, 0)
            rows_copy(0, 1)
            gate(0, 0)
            with act.Fori(0, TILES // 2 - 1) as it:
                for k in range(2):
                    with act.If(used > it * 2 + k):
                        slot(it, k, True, True)
            for k in range(2):
                with act.If(used > TILES - 2 + k):
                    slot(TILES // 2 - 1, k, k == 0, False)

        @block.vector
        def _(dve):
            def combine(it, k):
                dve.wait_ge(h_mm, it * 2 + (k + 1))
                dve.wait_ge(gate_ok, it * 2 + (k + 1))
                if not (isinstance(it, int) and it * 2 + k < 2):
                    dve.wait_ge(ht_mm, it * 2 + (k - 1))
                dve.tensor_tensor(hid[:, k % 2, :], act_gate[:, k % 2, :], ps_h[:, k % 2, 1, :], ALU.mult
                                  ).then_inc(hid_ok, 1)

            def y_copy(it, k):
                dve.wait_ge(y_mm, it * 2 + (k + 3))
                dve.wait_ge(y_sent[k % 2], it * 16 + 16 * (k // 2 + 1))
                dve.tensor_copy(y[:, k % 2, :], ps_y[:, 0:D]).then_inc(y_ok, 1)

            def slot(it, k, more):
                if more:
                    combine(it, k + 1)
                y_copy(it, k)

            used = used_tiles(dve)
            dve.sem_inc(hid_ok, 2)
            dve.sem_inc(y_ok, 1)
            combine(0, 0)
            with dve.Fori(0, TILES // 2 - 1) as it:
                for k in range(2):
                    with dve.If(used > it * 2 + k):
                        slot(it, k, True)
            for k in range(2):
                with dve.If(used > TILES - 2 + k):
                    slot(TILES // 2 - 1, k, k == 0)


def run_selu_experts(c, tag, w_in_dram, b_in_dram, w_out_dram, b_out_dram):
    nc = c.nc
    HC = HIDDEN // P
    with c.stage() as st:
        w1 = c.sbuf(st, f"{tag}_w1", [P, DC, E, HIDDEN], F32)
        w2 = c.sbuf(st, f"{tag}_w2", [P, HC, E, D], F32)
        b1 = c.sbuf(st, f"{tag}_b1", [P, HC, E], F32)
        b2 = c.sbuf(st, f"{tag}_b2", [P, E, D], F32)
        shift = c.sbuf(st, f"{tag}_shift", [P, 1], F32)
        rows = c.sbuf(st, f"{tag}_rows", [P, 2, D], F32)
        rows_t = c.sbuf(st, f"{tag}_rows_t", [P, 2, DC, P], F32)
        hid = c.sbuf(st, f"{tag}_hid", [P, 2, S], F32)
        pre = c.sbuf(st, f"{tag}_pre", [P, 2, S], F32)
        low = c.sbuf(st, f"{tag}_low", [P, 2, S], F32)
        grown = c.sbuf(st, f"{tag}_grown", [P, 2, S], F32)
        high = c.sbuf(st, f"{tag}_high", [P, 2, S], F32)
        hid_t = c.sbuf(st, f"{tag}_hid_t", [P, 2, S], F32)
        y = c.sbuf(st, f"{tag}_y", [P, 2, D], F32)
        ps_x = c.psum(st, f"{tag}_ps_x", [P, S])
        ps_h = c.psum(st, f"{tag}_ps_h", [P, 2, S])
        ps_ht = c.psum(st, f"{tag}_ps_ht", [P, 2, S])
        ps_y = c.psum(st, f"{tag}_ps_y", [P, S])
        w_in = c.sem(st, f"{tag}_ew_in")
        rows_in = [c.sem(st, f"{tag}_rows_in{i}") for i in range(2)]
        x_mm = c.sem(st, f"{tag}_x_mm")
        x_out = c.sem(st, f"{tag}_x_out")
        h_mm = c.sem(st, f"{tag}_h_mm")
        hid_ok = c.sem(st, f"{tag}_hid_ok")
        ht_mm = c.sem(st, f"{tag}_ht_mm")
        pre_ok = c.sem(st, f"{tag}_pre_ok")
        low_ok = c.sem(st, f"{tag}_low_ok")
        grown_ok = c.sem(st, f"{tag}_grown_ok")
        high_ok = c.sem(st, f"{tag}_high_ok")
        shift_ok = c.sem(st, f"{tag}_shift_ok")
        selu_ok = c.sem(st, f"{tag}_selu_ok")
        y_mm = c.sem(st, f"{tag}_y_mm")
        y_ok = c.sem(st, f"{tag}_y_ok")
        y_sent = [c.sem(st, f"{tag}_y_sent{i}") for i in range(2)]
        block = st.enter_context(nc.Block())

        def parts(it, k, part, more):
            return it * 4 + (2 * k + part + more)

        def used_tiles(eng):
            return eng.value_load(c.used[0:1, 0:1], min_val=0, max_val=TILES)

        @block.sync
        def _(sp):
            def load_rows(i):
                sp.dma_start(rows[:, i % 2, :], c.xs[tag][i * P:(i + 1) * P, :]).then_inc(rows_in[i % 2], 16)

            used = used_tiles(sp)
            with sp.If(used > 0):
                for i in range(2):
                    sp.sem_inc(y_sent[i], 16)
                    load_rows(i)
                for ch in range(DC):
                    sp.dma_start(w1[:, ch, :, :], w_in_dram[:, ch]).then_inc(w_in, 16)
                sp.dma_start(w2[:, :, :, :], w_out_dram).then_inc(w_in, 16)
                sp.dma_start(b1[:, :, :], b_in_dram).then_inc(w_in, 16)
                sp.dma_start(b2[:, :, :], b_out_dram.partition_broadcast(P)).then_inc(w_in, 16)
                lag = 3
                for i in range(TILES + lag):
                    if 2 <= i < TILES:
                        with sp.If(used > i - 2):
                            sp.wait_ge(x_mm, i - 1)
                            load_rows(i)
                    j = i - lag
                    if j >= 0:
                        with sp.If(used > j):
                            sp.wait_ge(y_ok, j + 2)
                            sp.dma_start(c.ys[tag][j * P:(j + 1) * P, :], y[:, j % 2, :]).then_inc(y_sent[j % 2], 16)
                        with sp.Else():
                            sp.dma_start(c.ys[tag][j * P:(j + 1) * P, :], c.zeros[:, 0, :]).then_inc(y_sent[j % 2], 16)
                for i in range(2):
                    sp.wait_ge(y_sent[i], 16 + 16 * (TILES // 2))

        @block.tensor
        def _(pe):
            def turn_rows(it, k):
                pe.wait_ge(rows_in[k % 2], it * 16 + 16 * (k // 2 + 1))
                pe.wait_ge(x_out, it * 2 + (k + 1))
                for ch in range(DC):
                    mm = pe.transpose(ps_x[:, ch * P:ch * P + P], rows[:, k % 2, ch * P:ch * P + P], c.ident[:, :])
                mm.then_inc(x_mm, 1)

            def first(it, k):
                e = pe.value_load(c.owner[0:1, bass.ds(it * 2 + k, 1)], min_val=0, max_val=E - 1)
                pe.wait_ge(x_out, it * 2 + (k + 2))
                for part in range(2):
                    pe.wait_ge(hid_ok, parts(it, k, part, 1))
                    for ch in range(DC):
                        mm = pe.matmul(ps_h[:, part, :], rows_t[:, k % 2, ch, :],
                                       w1[:, ch, bass.ds(e, 1), part * S:part * S + S].rearrange("p a n -> p (a n)"),
                                       start=ch == 0, stop=ch == DC - 1)
                    mm.then_inc(h_mm, 1)

            def turn_hidden(it, k):
                for part in range(2):
                    pe.wait_ge(hid_ok, parts(it, k, part, 3))
                    pe.wait_ge(pre_ok, parts(it, k, part, 1))
                    for j in range(S // P):
                        mm = pe.transpose(ps_ht[:, part, j * P:j * P + P], hid[:, part, j * P:j * P + P],
                                          c.ident[:, :])
                    mm.then_inc(ht_mm, 1)

            def second(it, k):
                e = pe.value_load(c.owner[0:1, bass.ds(it * 2 + k, 1)], min_val=0, max_val=E - 1)
                pe.wait_ge(y_ok, it * 2 + (k + 1))
                for part in range(2):
                    pe.wait_ge(selu_ok, parts(it, k, part, 3))
                    for j in range(S // P):
                        kk = part * (S // P) + j
                        mm = pe.matmul(ps_y[:, 0:D], hid_t[:, part, j * P:j * P + P],
                                       w2[:, kk, bass.ds(e, 1), :].rearrange("p a n -> p (a n)"),
                                       start=kk == 0, stop=kk == HC - 1)
                mm.then_inc(y_mm, 1)

            def slot(it, k, more, more2):
                turn_hidden(it, k)
                if more:
                    first(it, k + 1)
                if more2:
                    turn_rows(it, k + 2)
                second(it, k)

            used = used_tiles(pe)
            with pe.If(used > 0):
                turn_rows(0, 0)
                turn_rows(0, 1)
                pe.wait_ge(w_in, 16 * (DC + 3))
                first(0, 0)
                with pe.Fori(0, TILES // 2 - 1) as it:
                    for k in range(2):
                        with pe.If(used > it * 2 + k):
                            slot(it, k, True, True)
                for k in range(2):
                    with pe.If(used > TILES - 2 + k):
                        slot(TILES // 2 - 1, k, k == 0, False)

        @block.scalar
        def _(act):
            def rows_copy(it, k):
                act.wait_ge(x_mm, it * 2 + (k + 1))
                if not (isinstance(it, int) and it * 2 + k < 2):
                    act.wait_ge(h_mm, it * 4 + (2 * k - 2))
                act.activation(rows_t[:, k % 2, :, :], ps_x[:, 0:DC * P].rearrange("p (c t) -> p c t", c=DC),
                               ACT.Copy).then_inc(x_out, 1)

            def hidden_copy(it, k):
                for part in range(2):
                    act.wait_ge(h_mm, parts(it, k, part, 1))
                    act.wait_ge(ht_mm, parts(it, k, part, 1))
                    act.activation(hid[:, part, :], ps_h[:, part, :], ACT.Copy).then_inc(hid_ok, 1)

            def grow(it, k):
                for part in range(2):
                    act.wait_ge(low_ok, parts(it, k, part, 3))
                    act.wait_ge(selu_ok, parts(it, k, part, 1))
                    act.activation(grown[:, part, :], low[:, part, :], ACT.Exp, bias=shift[:, 0:1]
                                   ).then_inc(grown_ok, 1)

            def slot(it, k, more, more2):
                grow(it, k)
                if more:
                    hidden_copy(it, k + 1)
                if more2:
                    rows_copy(it, k + 2)

            used = used_tiles(act)
            with act.If(used > 0):
                act.sem_inc(x_out, 1)
                act.sem_inc(hid_ok, 2)
                act.sem_inc(grown_ok, 2)
                rows_copy(0, 0)
                rows_copy(0, 1)
                hidden_copy(0, 0)
                with act.Fori(0, TILES // 2 - 1) as it:
                    for k in range(2):
                        with act.If(used > it * 2 + k):
                            slot(it, k, True, True)
                for k in range(2):
                    with act.If(used > TILES - 2 + k):
                        slot(TILES // 2 - 1, k, k == 0, False)

        @block.gpsimd
        def _(pool):
            used = used_tiles(pool)
            with pool.If(used > 0):
                pool.sem_inc(low_ok, 2)
                with pool.Fori(0, TILES // 2) as it:
                    for k in range(2):
                        with pool.If(used > it * 2 + k):
                            for part in range(2):
                                pool.wait_ge(pre_ok, parts(it, k, part, 3))
                                pool.wait_ge(grown_ok, parts(it, k, part, 1))
                                pool.nop(nofuse=True)
                                pool.tensor_scalar(low[:, part, :], pre[:, part, :], 0.0, None, ALU.min
                                                   ).then_inc(low_ok, 1)

        @block.vector
        def _(dve):
            S_P = S // P

            def before_second(it, k):
                e = dve.value_load(c.owner[0:1, bass.ds(it * 2 + k, 1)], min_val=0, max_val=E - 1)
                for part in range(2):
                    dve.wait_ge(ht_mm, parts(it, k, part, 3))
                    dve.wait_ge(low_ok, parts(it, k, part, 1))
                    dve.wait_ge(high_ok, parts(it, k, part, 1))
                    dve.tensor_tensor(
                        pre[:, part, :].rearrange("p (j t) -> p j t", t=P),
                        ps_ht[:, part, :].rearrange("p (j t) -> p j t", t=P),
                        b1[:, part * S_P:part * S_P + S_P, bass.ds(e, 1)].broadcast_to([P, S_P, P]),
                        ALU.add).then_inc(pre_ok, 1)
                for part in range(2):
                    dve.wait_ge(pre_ok, parts(it, k, part, 3))
                    dve.wait_ge(selu_ok, parts(it, k, part, 1))
                    dve.tensor_scalar(high[:, part, :], pre[:, part, :], 0.0, -SELU_ALPHA, ALU.max, ALU.add
                                      ).then_inc(high_ok, 1)
                for part in range(2):
                    dve.wait_ge(grown_ok, parts(it, k, part, 3))
                    dve.wait_ge(high_ok, parts(it, k, part, 3))
                    dve.wait_ge(y_mm, it * 2 + (k + 1))
                    dve.tensor_tensor(hid_t[:, part, :], high[:, part, :], grown[:, part, :], ALU.add
                                      ).then_inc(selu_ok, 1)

            def y_copy(it, k):
                e = dve.value_load(c.owner[0:1, bass.ds(it * 2 + k, 1)], min_val=0, max_val=E - 1)
                dve.wait_ge(y_mm, it * 2 + (k + 2))
                dve.wait_ge(y_sent[k % 2], it * 16 + 16 * (k // 2 + 1))
                dve.scalar_tensor_tensor(out=y[:, k % 2, :], in0=ps_y[:, 0:D], scalar=SELU_SCALE,
                                         in1=b2[:, bass.ds(e, 1), :].rearrange("p a n -> p (a n)"),
                                         op0=ALU.mult, op1=ALU.add).then_inc(y_ok, 1)

            used = used_tiles(dve)
            with dve.If(used > 0):
                dve.sem_inc(ht_mm, 2)
                dve.sem_inc(pre_ok, 2)
                dve.sem_inc(high_ok, 2)
                dve.sem_inc(selu_ok, 2)
                dve.sem_inc(y_mm, 1)
                dve.sem_inc(y_ok, 1)
                dve.memset(shift[:, :], float(np.log(SELU_ALPHA))).then_inc(shift_ok, 1)
                dve.wait_ge(shift_ok, 1)
                dve.wait_ge(w_in, 16 * (DC + 3))
                with dve.Fori(0, TILES // 2) as it:
                    for k in range(2):
                        with dve.If(used > it * 2 + k):
                            before_second(it, k)
                            y_copy(it, k)


def gather_experts(c, tag, weight):
    nc = c.nc
    n_all = NT + 1
    with c.stage() as st:
        got = c.sbuf(st, f"{tag}_got", [P, n_all, 2, D], F32)
        clear = c.sem(st, f"{tag}_clear")
        got_in = c.sem(st, f"{tag}_got_in")
        all_got = c.sem(st, f"{tag}_all_got")
        added = c.sem(st, f"{tag}_added")
        block = st.enter_context(nc.Block())

        @block.gpsimd
        def _(pool):
            used = pool.value_load(c.used[0:1, 0:1], min_val=0, max_val=TILES)
            pool.wait_ge(clear, 1)
            with pool.If(used > 0):
                for n in range(n_all):
                    for k in range(2):
                        pool.indirect_dma_start(
                            out=got[:, n, k, :], out_offset=None, in_=c.ys[tag][:, :],
                            in_offset=bass.IndirectOffsetOnAxis(ap=c.row[:, k, n:n + 1], axis=0),
                            bounds_check=TILES * P - 1, oob_is_err=False).then_inc(got_in, 16)
                pool.wait_ge(got_in, 16 * 2 * n_all)
            pool.sem_inc(all_got, 1)

        @block.vector
        def _(dve):
            dve.memset(got[:, :, :, :], 0.0).then_inc(clear, 1)
            dve.wait_ge(all_got, 1)
            for k in range(2):
                if k:
                    dve.wait_ge(added, n_all)
                for n in range(n_all):
                    dve.scalar_tensor_tensor(out=c.h[:, n, :], in0=got[:, n, k, :], scalar=weight[:, k, n:n + 1],
                                             in1=c.h[:, n, :], op0=ALU.mult, op1=ALU.add).then_inc(added, 1)


def route_moe(c, tag, router_dram, idx, weight):
    nc = c.nc
    n_all = NT + 1
    with c.stage() as st:
        router = c.sbuf(st, f"{tag}_router", [P, DC, E], F32)
        logits = c.sbuf(st, f"{tag}_logits", [P, n_all, E], F32)
        top = c.sbuf(st, f"{tag}_top8", [P, n_all, 8], F32)
        top_at = c.sbuf(st, f"{tag}_top8_at", [P, n_all, 8], U32)
        gap = c.sbuf(st, f"{tag}_gap", [P, n_all], F32)
        ratio = c.sbuf(st, f"{tag}_ratio", [P, n_all], F32)
        one_more = c.sbuf(st, f"{tag}_one_more", [P, n_all], F32)
        ps_l = c.psum(st, f"{tag}_ps_l", [P, S])
        r_in = c.sem(st, f"{tag}_r_in")
        l_mm = c.sem(st, f"{tag}_l_mm")
        l_ok = c.sem(st, f"{tag}_l_ok")
        top_ok = c.sem(st, f"{tag}_top_ok")
        at_ok = c.sem(st, f"{tag}_at_ok")
        gap_ok = c.sem(st, f"{tag}_gap_ok")
        ratio_ok = c.sem(st, f"{tag}_ratio_ok")
        chain = c.sem(st, f"{tag}_r_chain")
        block = st.enter_context(nc.Block())

        @block.sync
        def _(sp):
            sp.dma_start(router[:, :, :], router_dram).then_inc(r_in, 16)

        @block.tensor
        def _(pe):
            pe.wait_ge(r_in, 16)
            for n in range(n_all):
                r = P if n < NT else B
                for ch in range(DC):
                    lhs = (c.xt[:, ch, n // NQ, 1 + n % NQ * P:1 + n % NQ * P + P] if n < NT else c.xt[:, ch, :, 0])
                    mm = pe.matmul(ps_l[0:r, n * E:n * E + E], lhs, router[:, ch, :], start=ch == 0, stop=ch == DC - 1)
            mm.then_inc(l_mm, 1)

        @block.vector
        def _(dve):
            dve.memset(logits[:, NT, :], 0.0).then_inc(l_ok, 1)
            dve.wait_ge(l_mm, 1)
            dve.wait_ge(l_ok, 1)
            dve.tensor_copy(logits[:, 0:NT, :], ps_l[:, 0:NT * E].rearrange("p (n e) -> p n e", e=E)).then_inc(l_ok, 1)
            dve.tensor_copy(logits[0:B, NT, :], ps_l[0:B, NT * E:n_all * E]).then_inc(l_ok, 1)
            dve.wait_ge(l_ok, 3)
            for n in range(n_all):
                dve.max(top[:, n, :], logits[:, n, :]).then_inc(top_ok, 1)
            for n in range(n_all):
                dve.wait_ge(top_ok, n + 1)
                dve.max_index(top_at[:, n, :], top[:, n, :], logits[:, n, :]).then_inc(at_ok, 1)
            dve.tensor_tensor(gap[:, :], top[:, :, 1], top[:, :, 0], ALU.subtract).then_inc(gap_ok, 1)
            dve.wait_ge(at_ok, n_all)
            dve.tensor_copy(idx[:, :, :], top_at[:, :, 0:2]).then_inc(chain, 1)
            dve.wait_ge(ratio_ok, 1)
            dve.tensor_scalar(one_more[:, :], ratio[:, :], 1.0, None, ALU.add).then_inc(chain, 1)
            dve.wait_ge(chain, 2)
            dve.reciprocal(weight[:, 0, :], one_more[:, :]).then_inc(chain, 1)
            dve.wait_ge(chain, 3)
            dve.tensor_tensor(weight[:, 1, :], ratio[:, :], weight[:, 0, :], ALU.mult).then_inc(chain, 1)

        @block.scalar
        def _(act):
            act.wait_ge(gap_ok, 1)
            act.activation(ratio[:, :], gap[:, :], ACT.Exp).then_inc(ratio_ok, 1)


def route_last(c, tag, wi_dram, bi_dram, wo_dram, bo_dram, idx, weight):
    nc = c.nc
    HC = HIDDEN // P
    n_all = NT + 1
    with c.stage() as st:
        wi = c.sbuf(st, f"{tag}_gwi", [P, DC, HIDDEN], F32)
        wo = c.sbuf(st, f"{tag}_gwo", [P, HC, D], F32)
        bi = c.sbuf(st, f"{tag}_gbi", [P, HC], F32)
        bo = c.sbuf(st, f"{tag}_gbo", [P, D], F32)
        shift = c.sbuf(st, f"{tag}_gshift", [P, 1], F32)
        low = c.sbuf(st, f"{tag}_glow", [P, 2, S], F32)
        grown = c.sbuf(st, f"{tag}_ggrown", [P, 2, S], F32)
        high = c.sbuf(st, f"{tag}_ghigh", [P, 2, S], F32)
        hid = c.sbuf(st, f"{tag}_ghid", [P, 2, S], F32)
        logits = c.sbuf(st, f"{tag}_glogits", [P, NQ, D], F32)
        top = c.sbuf(st, f"{tag}_gtop", [P, NQ, 8], F32)
        top_at = c.sbuf(st, f"{tag}_gtop_at", [P, NQ, 8], U32)
        two = c.sbuf(st, f"{tag}_gtwo", [P, 2, n_all], F32)
        sums = c.sbuf(st, f"{tag}_gsums", [P, n_all], F32)
        ps_h = c.psum(st, f"{tag}_gps_h", [P, 2, S])
        ps_l = c.psum(st, f"{tag}_gps_l", [P, NQ, S])
        w_in = c.sem(st, f"{tag}_gw_in")
        ready = c.sem(st, f"{tag}_gready")
        h_mm = c.sem(st, f"{tag}_gh_mm")
        low_ok = c.sem(st, f"{tag}_glow_ok")
        high_ok = c.sem(st, f"{tag}_ghigh_ok")
        grown_ok = c.sem(st, f"{tag}_ggrown_ok")
        hid_ok = c.sem(st, f"{tag}_ghid_ok")
        l_mm = c.sem(st, f"{tag}_gl_mm")
        l_ok = c.sem(st, f"{tag}_gl_ok")
        top_ok = c.sem(st, f"{tag}_gtop_ok")
        at_ok = c.sem(st, f"{tag}_gat_ok")
        kept = c.sem(st, f"{tag}_gkept")
        block = st.enter_context(nc.Block())

        @block.sync
        def _(sp):
            sp.dma_start(wi[:, :, :], wi_dram).then_inc(w_in, 16)
            sp.dma_start(bi[:, :], bi_dram).then_inc(w_in, 16)
            sp.dma_start(wo[:, :, :], wo_dram).then_inc(w_in, 16)
            sp.dma_start(bo[:, :], bo_dram.partition_broadcast(P)).then_inc(w_in, 16)

        @block.tensor
        def _(pe):
            def hidden(b, f, wide):
                pe.wait_ge(high_ok, b * HC + (f + 1))
                for ch in range(DC):
                    src = (c.xt[:, ch, bass.ds(b, 1), 1:].rearrange("p a t -> p (a t)") if wide == S
                           else c.xt[:, ch, :, 0])
                    mm = pe.matmul(ps_h[:, f % 2, 0:wide], wi[:, ch, f * P:f * P + P], src,
                                   start=ch == 0, stop=ch == DC - 1)
                mm.then_inc(h_mm, 1)

            def add_logits(b, f, wide):
                pe.wait_ge(hid_ok, b * HC + (f + 3))
                for n in range(NQ if wide == S else 1):
                    if f == 0:
                        pe.wait_ge(l_ok, b * NQ + (n + 1))
                    r = min(wide, P)
                    mm = pe.matmul(ps_l[0:r, n, 0:D], hid[:, f % 2, n * P:n * P + r], wo[:, f, :],
                                   start=f == 0, stop=f == HC - 1)
                mm.then_inc(l_mm, 1)

            def image(b, wide):
                hidden(b, 0, wide)
                for f in range(HC):
                    if f + 1 < HC:
                        hidden(b, f + 1, wide)
                    add_logits(b, f, wide)

            pe.wait_ge(w_in, 16 * 4)
            with pe.Fori(0, B) as b:
                image(b, S)
            image(B, B)

        @block.scalar
        def _(act):
            def image(b, wide):
                for f in range(HC):
                    act.wait_ge(low_ok, b * HC + (f + 1))
                    act.wait_ge(hid_ok, b * HC + (f + 1))
                    act.activation(high[:, f % 2, 0:wide], ps_h[:, f % 2, 0:wide], ACT.Relu, bias=bi[:, f:f + 1]
                                   ).then_inc(high_ok, 1)
                    act.activation(grown[:, f % 2, 0:wide], low[:, f % 2, 0:wide], ACT.Exp, bias=shift[:, 0:1]
                                   ).then_inc(grown_ok, 1)

            act.sem_inc(high_ok, 2)
            act.sem_inc(grown_ok, 2)
            with act.Fori(0, B) as b:
                image(b, S)
            image(B, B)

        @block.vector
        def _(dve):
            def image(b, wide):
                for f in range(HC):
                    dve.wait_ge(h_mm, b * HC + (f + 1))
                    dve.wait_ge(grown_ok, b * HC + (f + 1))
                    dve.tensor_scalar(low[:, f % 2, 0:wide], ps_h[:, f % 2, 0:wide], bi[:, f:f + 1], 0.0,
                                      ALU.add, ALU.min).then_inc(low_ok, 1)
                    dve.wait_ge(high_ok, b * HC + (f + 3))
                    dve.wait_ge(grown_ok, b * HC + (f + 3))
                    dve.wait_ge(l_mm, b * HC + (f + 1))
                    dve.scalar_tensor_tensor(out=hid[:, f % 2, 0:wide], in0=grown[:, f % 2, 0:wide],
                                             scalar=-SELU_ALPHA, in1=high[:, f % 2, 0:wide],
                                             op0=ALU.add, op1=ALU.add).then_inc(hid_ok, 1)
                tiles = NQ if wide == S else 1
                r = min(wide, P)
                dve.wait_ge(l_mm, b * HC + (HC + 2))
                dve.wait_ge(at_ok, b * NQ + NQ)
                for n in range(tiles):
                    dve.scalar_tensor_tensor(out=logits[0:r, n, :], in0=ps_l[0:r, n, 0:D], scalar=SELU_SCALE,
                                             in1=bo[0:r, :], op0=ALU.mult, op1=ALU.add).then_inc(l_ok, 1)
                dve.wait_ge(kept, 2 * b + 2)
                for n in range(tiles):
                    dve.wait_ge(l_ok, b * NQ + (NQ + n + 1))
                    dve.nop(nofuse=True)
                    dve.max(top[:, n, :], logits[:, n, :]).then_inc(top_ok, 1)
                for n in range(tiles):
                    dve.wait_ge(top_ok, b * NQ + (n + 1))
                    dve.nop(nofuse=True)
                    dve.max_index(top_at[:, n, :], top[:, n, :], logits[:, n, :]).then_inc(at_ok, 1)
                dve.wait_ge(at_ok, b * NQ + (NQ + tiles))
                where = bass.ds(b * NQ, tiles)
                dve.tensor_copy(two[:, :, where].rearrange("p k n -> p n k"), top[:, 0:tiles, 0:2]).then_inc(kept, 1)
                dve.tensor_copy(idx[:, where, :], top_at[:, 0:tiles, 0:2]).then_inc(kept, 1)

            dve.sem_inc(hid_ok, 2)
            dve.sem_inc(l_mm, 2)
            dve.sem_inc(l_ok, NQ)
            dve.sem_inc(at_ok, NQ)
            dve.sem_inc(kept, 2)
            dve.memset(shift[:, :], float(np.log(SELU_ALPHA))).then_inc(ready, 1)
            dve.wait_ge(ready, 1)
            dve.wait_ge(w_in, 16 * 4)
            with dve.Fori(0, B) as b:
                image(b, S)
            dve.wait_ge(at_ok, (B + 1) * NQ)
            dve.memset(logits[:, 0, :], 1.0).then_inc(ready, 1)
            dve.wait_ge(ready, 2)
            image(B, B)
            dve.wait_ge(kept, 2 * B + 4)
            dve.tensor_tensor(sums[:, :], two[:, 0, :], two[:, 1, :], ALU.add).then_inc(ready, 1)
            dve.wait_ge(ready, 3)
            dve.reciprocal(sums[:, :], sums[:, :]).then_inc(ready, 1)
            dve.wait_ge(ready, 4)
            dve.tensor_tensor(weight[:, :, :], two[:, :, :],
                              sums[:, :].rearrange("p (a n) -> p a n", a=1).broadcast_to([P, 2, n_all]), ALU.mult
                              ).then_inc(ready, 1)


def load_patches(c, x_t, cls):
    with c.stage() as st:
        x_in = c.sem(st, "x_in")
        cleared = c.sem(st, "cleared")
        with c.nc.Block() as block:
            @block.sync
            def _(sp):
                for ch in range(DC):
                    sp.dma_start(c.xt[:, ch, :, 1:], x_t[:, ch]).then_inc(x_in, 16)
                sp.wait_ge(cleared, 1)
                sp.dma_start(c.h[0:B, NT, :], cls.partition_broadcast(B)).then_inc(x_in, 16)
                sp.wait_ge(x_in, 16 * (DC + 1))

            @block.gpsimd
            def _(pool):
                pool.memset(c.h[:, NT, :], 0.0).then_inc(cleared, 1)


def norm(c, tag, keep=None):
    nc = c.nc
    with c.stage() as st:
        stats = c.sbuf(st, f"{tag}_stats", [P, NT + 1, 6], F32)
        mv = c.sbuf(st, f"{tag}_mv", [P, NT + 1, 2], F32)
        rstd = c.sbuf(st, f"{tag}_rstd", [P, NT + 1], F32)
        eps = c.sbuf(st, f"{tag}_eps", [P, 1], F32)
        xn = keep if keep is not None else c.sbuf(st, f"{tag}_xn", [P, NT + 1, D], F32)
        ps_t = c.psum(st, f"{tag}_ps_xt", [P, 2, S])
        stat_ok = c.sem(st, f"{tag}_stat_ok")
        aggr_ok = c.sem(st, f"{tag}_aggr_ok")
        eps_ok = c.sem(st, f"{tag}_eps_ok")
        std_ok = c.sem(st, f"{tag}_std_ok")
        rstd_ok = c.sem(st, f"{tag}_rstd_ok")
        xn_ok = c.sem(st, f"{tag}_xn_ok")
        t_mm = c.sem(st, f"{tag}_xt_mm")
        t_out = c.sem(st, f"{tag}_xt_out")
        block = st.enter_context(nc.Block())

        @block.vector
        def _(dve):
            dve.memset(eps[:, :], EPS).then_inc(eps_ok, 1)
            for n in range(NT + 1):
                dve.bn_stats(stats[:, n, :], c.h[:, n, :]).then_inc(stat_ok, 1)
            for n in range(NT + 1):
                dve.wait_ge(stat_ok, n + 1)
                dve.bn_aggr(mv[:, n, :], stats[:, n, :]).then_inc(aggr_ok, 1)
            dve.wait_ge(std_ok, 1)
            dve.reciprocal(rstd[:, :], rstd[:, :]).then_inc(rstd_ok, 1)
            dve.wait_ge(rstd_ok, 1)
            dve.wait_ge(aggr_ok, NT + 1)
            for n in range(NT + 1):
                dve.tensor_scalar(xn[:, n, :], c.h[:, n, :], mv[:, n, 0:1], rstd[:, n:n + 1],
                                  ALU.subtract, ALU.mult).then_inc(xn_ok, 1)

        @block.tensor
        def _(pe):
            for n in range(NT + 1):
                pe.wait_ge(xn_ok, n + 1)
                if n >= 2:
                    pe.wait_ge(t_out, n - 1)
                r = P if n < NT else B
                for ch in range(DC):
                    mm = pe.transpose(ps_t[:, n % 2, ch * P:ch * P + r], xn[0:r, n, ch * P:ch * P + P],
                                      c.ident[0:r, 0:r])
                mm.then_inc(t_mm, 1)

        @block.scalar
        def _(act):
            act.wait_ge(aggr_ok, NT + 1)
            act.wait_ge(eps_ok, 1)
            act.activation(rstd[:, :], mv[:, :, 1], ACT.Sqrt, bias=eps[:, 0:1]).then_inc(std_ok, 1)
            for n in range(NT + 1):
                act.wait_ge(t_mm, n + 1)
                src = ps_t[:, n % 2, 0:DC * P].rearrange("p (c t) -> p c t", c=DC)
                if n < NT:
                    at = 1 + (n % NQ) * P
                    act.activation(c.xt[:, :, n // NQ, at:at + P], src, ACT.Copy).then_inc(t_out, 1)
                else:
                    act.activation(c.xt[:, :, :, 0], src[:, :, 0:B], ACT.Copy).then_inc(t_out, 1)


def store_output(c, ap):
    with c.stage() as st:
        out_ok = c.sem(st, "out_ok")
        with c.nc.Block() as block:
            @block.sync
            def _(sp):
                for b in range(B):
                    sp.dma_start(ap[b, 1:, :].rearrange("(n p) d -> p n d", p=P),
                                 c.h[:, b * NQ:b * NQ + NQ, :]).then_inc(out_ok, 16)
                sp.dma_start(ap[:, 0, :], c.h[0:B, NT, :]).then_inc(out_ok, 16)
                sp.wait_ge(out_ok, 16 * (B + 1))


def program(nc, a, out, stop=9):
    with ExitStack() as stack:
        c = Chip(nc, stack)
        c.qd = nc.dram_tensor("q_parts", [B, SPLIT, HD, NH, S], BF16, kind="Internal").ap()
        c.kd = {w: nc.dram_tensor(f"k{w}_parts", [B, SPLIT, HD, NH, w], BF16, kind="Internal").ap()
                for w in (S, S + 1)}
        c.vd = nc.dram_tensor("v_rows", [B, G, P, NQ, P], F32, kind="Internal").ap()
        c.xs = {t: nc.dram_tensor(f"{t}_xs", [TILES * P, D], F32, kind="Internal").ap() for t in ("moe", "last")}
        c.ys = {t: nc.dram_tensor(f"{t}_ys", [TILES * P, D], F32, kind="Internal").ap() for t in ("moe", "last")}
        constants(c)
        c.h = c.sbuf(stack, "h", [P, NT + 1, D], F32)
        c.vcls = c.sbuf(stack, "vcls", [B, D], F32)
        c.row = c.sbuf(stack, "row", [P, 2, NT + 1], U32)
        c.owner = c.sbuf(stack, "owner", [P, TILES], I32)
        c.used = c.sbuf(stack, "used", [P, 1], I32)
        idx = c.sbuf(stack, "idx", [P, NT + 1, 2], F32)
        weight = c.sbuf(stack, "weight", [P, 2, NT + 1], F32)
        c.ctx = c.sbuf(stack, "ctx", [P, NT + 1, D], F32)
        with ExitStack() as wide:
            c.xt = c.sbuf(wide, "xt", [P, DC, B, S + 1], F32)
            load_patches(c, a["x_t"], a["cls"])
            project(c, "tok", a["tok_w"], a["tok_qkb"], a["tok_vb"], cls=False)
            attend(c, "tok", causal=False, clear=True)
            attend_out(c, "tok", a["tok_wo"], a["tok_bo"], residual=False, cls=False)
            if stop == 0: return store_output(c, out)
            norm(c, "rot")
            project(c, "rot", a["rot_w"], a["rot_qkb"], a["rot_vb"], cls=True, rope=(a["cos"], a["sin"]))
            attend(c, "rot", causal=True)
            attend_out(c, "rot", a["rot_wo"], a["rot_bo"], residual=True, cls=True)
            if stop == 1: return store_output(c, out)
            norm(c, "moe", keep=c.ctx)
            route_moe(c, "moe", a["router"], idx, weight)
        dispatch(c, "moe", c.ctx, idx)
        run_gated_experts(c, "moe", a["moe_w13"], a["moe_w2"], S)
        gather_experts(c, "moe", weight)
        if stop == 2: return store_output(c, out)
        with ExitStack() as wide:
            c.xt = c.sbuf(wide, "xt2", [P, DC, B, S + 1], F32)
            norm(c, "top")
            project(c, "top", a["top_w"], a["top_qkb"], a["top_vb"], cls=True)
            attend_top(c, "top")
            attend_out(c, "top", a["top_wo"], a["top_bo"], residual=True, cls=True)
            if stop == 3: return store_output(c, out)
            norm(c, "last", keep=c.ctx)
            route_last(c, "last", a["gate_wi"], a["gate_bi"], a["gate_wo"], a["gate_bo"], idx, weight)
        dispatch(c, "last", c.ctx, idx)
        run_selu_experts(c, "last", a["exp_wi"], a["exp_bi"], a["exp_wo"], a["exp_bo"])
        gather_experts(c, "last", weight)
        store_output(c, out)


_OUT = (B, S + 1, D)


def _split_rows(w):
    return np.ascontiguousarray(w.reshape(DC, P, -1).transpose(1, 0, 2))


def _columns(*vectors):
    return _split_rows(np.stack(vectors, axis=1))


def _swap_halves(w):
    return w.reshape(-1, NH, 2, HD // 2)[:, :, ::-1].reshape(w.shape)


def layout(inputs):
    i = {k: np.asarray(v) for k, v in inputs.items()}
    a = {}
    a["x_t"] = np.ascontiguousarray(i["x"].reshape(B, S, DC, P).transpose(3, 2, 0, 1))
    a["cls"] = i["cls_tok"].reshape(D)
    wt = i["L0_tok_w_qkv"].T.reshape(D, NH, 3, HD).transpose(0, 2, 1, 3).reshape(D, 3 * D)
    bt = i["L0_tok_b_qkv"].reshape(NH, 3, HD).transpose(1, 0, 2).reshape(3, D)
    a["tok_w"] = _split_rows(wt)
    a["tok_qkb"] = _columns(bt[0], bt[1])
    a["tok_vb"] = np.ascontiguousarray(bt[2])
    a["tok_wo"] = _split_rows(i["L0_tok_w_out"].T)
    a["tok_bo"] = i["L0_tok_b_out"]
    wq, wk, wv = (i[f"L0_attn_w{x}_w"] for x in "qkv")
    bq, bk = i["L0_attn_wq_b"], i["L0_attn_wk_b"]
    a["rot_w"] = _split_rows(np.concatenate([wq, wk, wv, _swap_halves(wq), _swap_halves(wk)], axis=1))
    a["rot_qkb"] = _columns(bq, bk, _swap_halves(bq[None])[0], _swap_halves(bk[None])[0])
    a["rot_vb"] = i["L0_attn_wv_b"]
    a["rot_wo"] = _split_rows(i["L0_attn_wo_w"])
    a["rot_bo"] = i["L0_attn_wo_b"]
    half = HD // 2
    scale = np.float32(2500.0) ** (np.float32(2.0) * np.arange(half, dtype=np.float32) / np.float32(HD))
    angle = np.arange(1, S + 1, dtype=np.float32)[None, :] / scale[:, None].astype(np.float32)
    cos, sin = np.cos(angle).astype(np.float32), np.sin(angle).astype(np.float32)
    a["cos"] = np.tile(np.concatenate([cos, cos]), (P // HD, 1))
    a["sin"] = np.tile(np.concatenate([-sin, sin]), (P // HD, 1))
    a["top_w"] = _split_rows(np.concatenate([i[f"L1_attn_W{x}"].T for x in "qkv"], axis=1))
    a["top_qkb"] = _columns(i["L1_attn_bq"], i["L1_attn_bk"])
    a["top_vb"] = i["L1_attn_bv"]
    a["top_wo"] = _split_rows(i["L1_attn_Wo"].T)
    a["top_bo"] = i["L1_attn_bo"]
    a["router"] = _split_rows(i["L0_ffn_moe_router"])
    a["moe_w13"] = i["L0_ffn_moe_w13"].reshape(E, DC, P, -1).transpose(2, 1, 0, 3)
    a["moe_w2"] = i["L0_ffn_moe_w2"].reshape(E, -1, P, D).transpose(2, 1, 0, 3)
    a["gate_wi"] = _split_rows(i["L1_ffn_gate_wi"])
    a["gate_bi"] = i["L1_ffn_gate_bi"].reshape(-1, P).T
    a["gate_wo"] = i["L1_ffn_gate_wo"].reshape(-1, P, D).transpose(1, 0, 2)
    a["gate_bo"] = i["L1_ffn_gate_bo"]
    a["exp_wi"] = i["L1_ffn_exp_wi"].reshape(E, DC, P, -1).transpose(2, 1, 0, 3)
    a["exp_bi"] = i["L1_ffn_exp_bi"].reshape(E, -1, P).transpose(2, 1, 0)
    a["exp_wo"] = i["L1_ffn_exp_wo"].reshape(E, -1, P, D).transpose(2, 1, 0, 3)
    a["exp_bo"] = i["L1_ffn_exp_bo"]
    return {k: np.ascontiguousarray(v) for k, v in a.items()}


def kernel(**inputs):
    import concourse.bacc as bacc
    from concourse.bass_utils import run_bass_kernel_spmd

    nc = bacc.Bacc("TRN2", target_bir_lowering=False, num_devices=1)
    arrays = layout(inputs)
    aps = {k: nc.dram_tensor(f"in_{k}", list(v.shape), mybir.dt.from_np(v.dtype), kind="ExternalInput").ap()
           for k, v in arrays.items()}
    out = nc.dram_tensor("out", list(_OUT), F32, kind="ExternalOutput").ap()
    program(nc, aps, out)
    r = run_bass_kernel_spmd(nc, [{f"in_{k}": v for k, v in arrays.items()}], core_ids=[0])
    return r.results[0]["out"]
```

```python
from contextlib import ExitStack, contextmanager
from itertools import groupby

import numpy as np

import concourse.bass as bass
from concourse import mybir

F32 = mybir.dt.float32
BF16 = mybir.dt.bfloat16
U32 = mybir.dt.uint32
I32 = mybir.dt.int32
ALU = mybir.AluOpType
ACT = mybir.ActivationFunctionType
AX_X = mybir.AxisListType.X

P = 128
B = 4
S = 512
D = 256
DC = D // P
NH = 16
HD = D // NH
NQ = S // P
NT = B * NQ
G = 4
HG = NH // G
STRIP = 32
SPLIT = 3
Q_ORDER = (2, 1, 0, 0, 0, 1)
K_ORDER = (0, 0, 0, 1, 2, 1)
PARTS = len(Q_ORDER)
NLOADS = len(list(groupby(Q_ORDER))) + len(list(groupby(K_ORDER))) + 1
E = 8
EPS = 1e-5
MASKED = -1e30
TAKEN = -3e38
K_TOP = 32
TILES = (2 * (NT * P + B) - E) // P + E
UNROLL = 4
SURE_TILES = 2 * (NT * P + B) // P // UNROLL * UNROLL
NOWHERE = 1 << 16
MOE_HIDDEN = 512
HIDDEN = 1024
SELU_ALPHA = 1.6732632423543772
SELU_SCALE = 1.0507009873554805
QSCALE = 1.0 / float(np.sqrt(HD))


FIRST_PASS = {False: ((1, 1, 1), (1, 1, 1, 0), (1, 1, 1, 0), (1, 1, 1, 1)),
              True: ((1, 2, 1), (1, 2, 1, 1), (1, 1, 1, 0), (1, 0, 0, 0))}
EARLY = 3
FINISH_AFTER = 4


class Chip:

    def __init__(self, nc, stack):
        self.nc, self.stack = nc, stack
        self.stage_sems = []
        self.fetched = self.sem(stack, "fetched")
        self.fetches = 0

    @contextmanager
    def stage(self):
        with ExitStack() as st:
            yield st
        sems, self.stage_sems = self.stage_sems, []
        self.nc.clear_and_free_semaphores(sems)
        self.nc.all_engine_barrier()

    def fetch(self, eng, pairs):
        for dst, src in pairs:
            eng.dma_start(dst, src).then_inc(self.fetched, 16)
        self.fetches += len(pairs)

    def sbuf(self, stack, name, shape, dt):
        return stack.enter_context(self.nc.sbuf_tensor(name, shape, dt))

    def psum(self, stack, name, shape, dt=F32):
        return stack.enter_context(self.nc.psum_tensor(name, shape, dt))

    def sem(self, stack, name):
        sem = self.nc.alloc_semaphore(name)
        if stack is not self.stack:
            self.stage_sems.append(sem)
        return sem


def constants(c):
    nc = c.nc
    c.ident = c.sbuf(c.stack, "ident", [P, P], F32)
    c.ident_bf = c.sbuf(c.stack, "ident_bf", [P, P], BF16)
    c.mask_qk = c.sbuf(c.stack, "mask_qk", [P, P], BF16)
    c.mask_kq = c.sbuf(c.stack, "mask_kq", [P, P], BF16)
    c.pick_cls = c.sbuf(c.stack, "pick_cls", [B, B, P], F32)
    c.before = c.sbuf(c.stack, "before", [P, P], BF16)
    c.ones_bf = c.sbuf(c.stack, "ones_bf", [P, P], BF16)
    c.iota_e = c.sbuf(c.stack, "iota_e", [P, E], F32)
    c.iota_t = c.sbuf(c.stack, "iota_t", [P, TILES], F32)
    c.steps = c.sbuf(c.stack, "steps", [P, NT + 1], F32)
    c.valid = c.sbuf(c.stack, "valid", [P, NT + 1], F32)
    c.zeros = zeros = c.sbuf(c.stack, "zeros", [P, 1, D], F32)
    c.xs_clear = c.sem(c.stack, "xs_clear")
    with c.stage() as st:
        filled = c.sem(st, "const_filled")
        with nc.Block() as block:
            @block.gpsimd
            def _(pool):
                pool.memset(c.ident[:, :], 0.0).then_inc(filled, 1)
                pool.memset(c.ident_bf[:, :], 0.0).then_inc(filled, 1)
                pool.memset(c.mask_qk[:, :], 0.0).then_inc(filled, 1)
                pool.memset(c.mask_kq[:, :], 0.0).then_inc(filled, 1)
                pool.memset(c.pick_cls[:, :, :], 0.0).then_inc(filled, 1)
                pool.wait_ge(filled, 5)
                for ident in (c.ident, c.ident_bf):
                    pool.affine_select(out=ident[:, :], in_=ident[:, :], compare_op=ALU.not_equal, fill=1.0,
                                       base=0, pattern=[[-1, P]], channel_multiplier=1).then_inc(filled, 1)
                pool.affine_select(out=c.mask_qk[:, :], in_=c.mask_qk[:, :], compare_op=ALU.is_ge, fill=MASKED,
                                   base=0, pattern=[[-1, P]], channel_multiplier=1).then_inc(filled, 1)
                pool.affine_select(out=c.mask_kq[:, :], in_=c.mask_kq[:, :], compare_op=ALU.is_ge, fill=MASKED,
                                   base=0, pattern=[[1, P]], channel_multiplier=-1).then_inc(filled, 1)
                pool.affine_select(out=c.pick_cls[:, :, :], in_=c.pick_cls[:, :, :], compare_op=ALU.not_equal,
                                   fill=1.0, base=0, pattern=[[-1, B], [0, P]],
                                   channel_multiplier=1).then_inc(filled, 1)
                pool.wait_ge(filled, 10)
                pool.memset(zeros[:, :, :], 0.0).then_inc(filled, 1)
                pool.memset(c.before[:, :], 1.0).then_inc(filled, 1)
                pool.memset(c.ones_bf[:, :], 1.0).then_inc(filled, 1)
                pool.memset(c.valid[:, :], 1.0).then_inc(filled, 1)
                pool.iota(c.iota_e[:, :], pattern=[[1, E]], base=0, channel_multiplier=0,
                          allow_small_or_imprecise_dtypes=True).then_inc(filled, 1)
                pool.iota(c.iota_t[:, :], pattern=[[1, TILES]], base=0, channel_multiplier=0,
                          allow_small_or_imprecise_dtypes=True).then_inc(filled, 1)
                pool.iota(c.steps[:, :], pattern=[[P, NT + 1]], base=0, channel_multiplier=0,
                          allow_small_or_imprecise_dtypes=True).then_inc(filled, 1)
                pool.wait_ge(filled, 17)
                pool.affine_select(out=c.before[:, :], in_=c.before[:, :], compare_op=ALU.is_gt, fill=0.0,
                                   base=0, pattern=[[1, P]], channel_multiplier=-1).then_inc(filled, 1)
                pool.affine_select(out=c.valid[:, NT:NT + 1], in_=c.valid[:, NT:NT + 1], compare_op=ALU.is_ge,
                                   fill=0.0, base=B - 1, pattern=[[0, 1]], channel_multiplier=-1).then_inc(filled, 1)
                pool.wait_ge(filled, 19)


def load_step(sp, c, b, g, q, k, v, loaded):
    heads = slice(g * HG, g * HG + HG)
    for dst, parts, order in ((q, c.qd[b], Q_ORDER), (k, c.kd[k.shape[2]][b], K_ORDER)):
        at = 0
        for part, run in groupby(order):
            n = len(list(run))
            src = parts[part:part + 1, :, heads, :]
            if n > 1:
                src = src.broadcast_to([n, HD, HG, dst.shape[2]])
            sp.dma_start(dst[at * HD:(at + n) * HD, :, :], src.rearrange("i d h t -> (i d) h t") if n == 1 else src
                         ).then_inc(loaded, 16)
            at += n
    sp.dma_start(v[:, :, :], c.vd[b, g]).then_inc(loaded, 16)


def project(c, tag, w, qkb, vb, cls, rope=None):
    nc = c.nc
    turns = 2 if rope else 0
    with c.stage() as st:
        full = c.sbuf(st, f"{tag}_full", [P, 2, S + 1], F32)
        rest = c.sbuf(st, f"{tag}_rest", [P, 2, S + 1], F32)
        hi = c.sbuf(st, f"{tag}_hi", [P, 4, S + 1], BF16)
        mid = c.sbuf(st, f"{tag}_mid", [P, 4, S + 1], BF16)
        lo = c.sbuf(st, f"{tag}_lo", [P, 4, S + 1], BF16)
        kcls = c.sbuf(st, f"{tag}_kcls", [P, DC, B], F32)
        va = c.sbuf(st, f"{tag}_va", [P, NT, NH, STRIP], F32)
        if rope:
            cos, sin = rope
            turned = c.sbuf(st, f"{tag}_turned", [P, 2, S], F32)
            plain = c.sbuf(st, f"{tag}_plain", [P, 2, S], F32)
        ps = c.psum(st, f"{tag}_ps", [P, 2, S])
        ps_rot = c.psum(st, f"{tag}_ps_rot", [P, 2, S])
        ps_v = c.psum(st, f"{tag}_ps_v", [P, 2, S])
        ps_c = c.psum(st, f"{tag}_ps_c", [P, 2, S])
        cls_mm = c.sem(st, f"{tag}_cls_mm")
        cls_done = c.sem(st, f"{tag}_cls_done")
        tables = c.sem(st, f"{tag}_tables")
        qk_mm = c.sem(st, f"{tag}_qk_mm")
        full_ok = c.sem(st, f"{tag}_full_ok")
        turn_ok = c.sem(st, f"{tag}_turn_ok")
        hi_ok = c.sem(st, f"{tag}_hi_ok")
        rest_ok = c.sem(st, f"{tag}_rest_ok")
        mid_ok = c.sem(st, f"{tag}_mid_ok")
        lo_ok = c.sem(st, f"{tag}_lo_ok")
        stored = [c.sem(st, f"{tag}_stored{i}") for i in range(4)]
        v_mm = c.sem(st, f"{tag}_v_mm")
        v_ok = c.sem(st, f"{tag}_v_ok")
        v_ones = c.sem(st, f"{tag}_v_ones")
        v_out = c.sem(st, f"{tag}_v_out")
        step_stores = 16 * SPLIT
        fetched = 16 * c.fetches
        block = st.enter_context(nc.Block())

        def span(k):
            return slice(0 if cls and k // 2 == 1 else 1, S + 1)

        @block.sync
        def _(sp):
            for i in range(4):
                sp.sem_inc(stored[i], 16)
            for b in range(B):
                for k in range(4):
                    which, gg = k // 2, k % 2
                    dst = (c.qd, c.kd[S + 1 if cls else S])[which]
                    for part, (tile, ok, free) in enumerate(((hi, hi_ok, 0), (mid, mid_ok, 0), (lo, lo_ok, 2))):
                        sp.wait_ge(ok, b * 4 + (k + 1 + free))
                        sp.dma_start(dst[b, part, :, gg * 8:gg * 8 + 8, :].rearrange("d h t -> h d t"),
                                     tile[:, k, span(k)]).then_inc(stored[k], 16)
                sp.wait_ge(v_ok, 2 + (b + 1) * NQ)
                for g in range(G):
                    sp.dma_start(c.vd[b, g], va[:, b * NQ:b * NQ + NQ, g * HG:g * HG + HG, :].rearrange(
                        "p n h s -> p n (h s)")).then_inc(v_out, 16)
            sp.wait_ge(v_out, 16 * G * B)
            for i in range(4):
                sp.wait_ge(stored[i], 16 + B * step_stores)

        @block.tensor
        def _(pe):
            pe.wait_ge(c.fetched, fetched)
            if cls:
                for gg in range(DC):
                    for ch in range(DC):
                        pe.matmul(ps_c[:, 0, gg * B:gg * B + B], w[:, ch, D + gg * P:D + gg * P + P],
                                  c.xt[:, ch, :, 0], start=ch == 0, stop=ch == DC - 1)
                for ch in range(DC):
                    mm = pe.matmul(ps_c[0:B, 1, 0:D], c.xt[:, ch, :, 0], w[:, ch, 2 * D:3 * D],
                                   start=ch == 0, stop=ch == DC - 1)
                mm.then_inc(cls_mm, 1)
            for b in range(B):
                for k in range(4):
                    which, gg = k // 2, k % 2
                    pe.wait_ge(full_ok, b * 4 + (k + 1))
                    for ch in range(DC):
                        mm = pe.matmul(ps[:, k % 2, :], w[:, ch, which * D + gg * P:which * D + gg * P + P],
                                       c.xt[:, ch, b, 1:S + 1], start=ch == 0, stop=ch == DC - 1)
                    if rope:
                        at = (3 + which) * D + gg * P
                        for ch in range(DC):
                            mm = pe.matmul(ps_rot[:, k % 2, :], w[:, ch, at:at + P],
                                           c.xt[:, ch, b, 1:S + 1], start=ch == 0, stop=ch == DC - 1)
                    mm.then_inc(qk_mm, 1)
                    pe.wait_ge(v_ok, b * NQ + (k + 1))
                    for ch in range(DC):
                        mm = pe.matmul(ps_v[:, k % 2, 0:D], c.xt[:, ch, b, 1 + k * P:1 + k * P + P],
                                       w[:, ch, 2 * D:3 * D], start=ch == 0, stop=ch == DC - 1)
                    mm.then_inc(v_mm, 1)

        @block.vector
        def _(dve):
            dve.sem_inc(full_ok, 2)
            dve.sem_inc(rest_ok, 2)
            dve.sem_inc(lo_ok, 2)
            dve.sem_inc(v_ok, 2)
            dve.wait_ge(v_ones, 2)
            dve.wait_ge(c.fetched, fetched)
            if cls:
                dve.wait_ge(cls_mm, 1)
                for gg in range(DC):
                    dve.tensor_scalar(kcls[:, gg, :], ps_c[:, 0, gg * B:gg * B + B], qkb[:, gg, 1:2], None,
                                      ALU.add).then_inc(cls_done, 1)
                dve.tensor_tensor(c.vcls[:, :], ps_c[0:B, 1, 0:D], vb[0:B, :], ALU.add).then_inc(cls_done, 1)
                dve.wait_ge(cls_done, DC + 1)
            if rope:
                dve.tensor_scalar(cos[:, 0, :], cos[:, 0, :], QSCALE, None, ALU.mult).then_inc(tables, 1)
                dve.tensor_scalar(sin[:, 0, :], sin[:, 0, :], QSCALE, None, ALU.mult).then_inc(tables, 1)
                dve.wait_ge(tables, 2)
            per_image = 4 * turns + (2 if cls else 0)
            def split(b, k):
                dve.wait_ge(full_ok, b * 4 + (k + 3))
                dve.wait_ge(hi_ok, b * 4 + (k + 1))
                dve.wait_ge(lo_ok, b * 4 + (k + 1))
                dve.tensor_tensor(rest[:, k % 2, span(k)], full[:, k % 2, span(k)], hi[:, k, span(k)],
                                  ALU.subtract).then_inc(rest_ok, 1)
                n = b * NQ + k
                dve.wait_ge(v_mm, n + 1)
                dve.tensor_tensor(va[:, bass.ds(n, 1), :, 0:HD].rearrange("p a h d -> p (a h) d"),
                                  ps_v[:, k % 2, 0:D].rearrange("p (h d) -> p h d", d=HD),
                                  vb[:, :].rearrange("p (h d) -> p h d", d=HD), ALU.add).then_inc(v_ok, 1)

            def image(b, before):
                done = 0
                for k in range(4):
                    which, gg = k // 2, k % 2
                    dve.wait_ge(qk_mm, b * 4 + (k + 1))
                    dve.wait_ge(rest_ok, b * 4 + (k + 1))
                    dve.wait_ge(full_ok, b * 4 + (k + 1))
                    if cls and which == 1:
                        dve.tensor_copy(full[:, k % 2, 0:1], kcls[:, gg, bass.ds(b, 1)]).then_inc(turn_ok, 1)
                        done += 1
                    if rope:
                        dve.scalar_tensor_tensor(out=plain[:, k % 2, :], in0=ps[:, k % 2, :],
                                                 scalar=qkb[:, gg, which:which + 1], in1=cos[:, which, :],
                                                 op0=ALU.add, op1=ALU.mult).then_inc(turn_ok, 1)
                        dve.scalar_tensor_tensor(out=turned[:, k % 2, :], in0=ps_rot[:, k % 2, :],
                                                 scalar=qkb[:, gg, 2 + which:3 + which], in1=sin[:, which, :],
                                                 op0=ALU.add, op1=ALU.mult).then_inc(turn_ok, 1)
                        done += turns
                        dve.wait_ge(turn_ok, b * per_image + done)
                        dve.tensor_tensor(full[:, k % 2, 1:], plain[:, k % 2, :], turned[:, k % 2, :],
                                          ALU.add).then_inc(full_ok, 1)
                    else:
                        if cls and which == 1:
                            dve.wait_ge(turn_ok, b * per_image + done)
                        dve.tensor_scalar(full[:, k % 2, 1:], ps[:, k % 2, :], qkb[:, gg, which:which + 1],
                                          QSCALE if which == 0 else 1.0, ALU.add, ALU.mult).then_inc(full_ok, 1)
                    if k:
                        split(b, k - 1)
                    elif before:
                        split(b - 1, 3)

            image(0, False)
            with dve.Fori(1, B) as b:
                image(b, True)
            split(B - 1, 3)

        @block.scalar
        def _(act):
            def second_part(b, k):
                act.wait_ge(rest_ok, b * 4 + (k + 3))
                act.activation(mid[:, k, span(k)], rest[:, k % 2, span(k)], ACT.Copy).then_inc(mid_ok, 1)

            def image(b, before):
                for k in range(4):
                    act.wait_ge(full_ok, b * 4 + (k + 3))
                    act.wait_ge(stored[k], b * step_stores + 16)
                    act.activation(hi[:, k, span(k)], full[:, k % 2, span(k)], ACT.Copy).then_inc(hi_ok, 1)
                    if k:
                        second_part(b, k - 1)
                    elif before:
                        second_part(b - 1, 3)

            image(0, False)
            with act.Fori(1, B) as b:
                image(b, True)
            second_part(B - 1, 3)

        @block.gpsimd
        def _(pool):
            pool.memset(va[:, :, :, :], 0.0).then_inc(v_ones, 1)
            pool.wait_ge(v_ones, 1)
            pool.memset(va[:, :, :, HD:HD + 1], 1.0).then_inc(v_ones, 1)
            with pool.Fori(0, B) as b:
                for k in range(4):
                    pool.wait_ge(mid_ok, b * 4 + (k + 1))
                    pool.tensor_tensor(lo[:, k, span(k)], rest[:, k % 2, span(k)], mid[:, k, span(k)],
                                       ALU.subtract).then_inc(lo_ok, 1)


def attend(c, tag, causal, clear=False, fetch=()):
    nc = c.nc
    k0 = 1 if causal else 0
    units = NQ * HG
    plan = FIRST_PASS[causal]
    with c.stage() as st:
        qs = [c.sbuf(st, f"{tag}_qs{i}", [P, HG, S], BF16) for i in range(G)]
        ks = [c.sbuf(st, f"{tag}_ks{i}", [P, HG, S + k0], BF16) for i in range(G)]
        vs = [c.sbuf(st, f"{tag}_vs{i}", [P, NQ, P], F32) for i in range(G)]
        et = c.sbuf(st, f"{tag}_et", [P, 2, HG, S], F32)
        pv_rows = c.sbuf(st, f"{tag}_pv_rows", [P, S], F32)
        rowmax = c.sbuf(st, f"{tag}_rowmax", [P, 2, units], F32)
        top = c.sbuf(st, f"{tag}_top", [P, units], F32)
        cls_raw = c.sbuf(st, f"{tag}_cls_raw", [P, units], F32)
        neg = c.sbuf(st, f"{tag}_neg", [P, units, STRIP], BF16)
        neg_sum = c.sbuf(st, f"{tag}_neg_sum", [P, units], F32)
        cls_score = c.sbuf(st, f"{tag}_cls_score", [P, units], F32)
        p_cls = c.sbuf(st, f"{tag}_p_cls", [P, 2, units], F32)
        v_cls = c.sbuf(st, f"{tag}_v_cls", [P, B, D], F32)
        cls_part = c.sbuf(st, f"{tag}_cls_part", [P, NQ, HG, HD], F32)
        raw = c.sbuf(st, f"{tag}_raw", [P, NQ, HG, HD], F32)
        den = c.sbuf(st, f"{tag}_den", [P, units], F32)
        rden = c.sbuf(st, f"{tag}_rden", [P, units], F32)
        ps_st = c.psum(st, f"{tag}_ps_st", [P, HG, S])
        ps_s = c.psum(st, f"{tag}_ps_s", [P, 2, S])
        ps_pv = c.psum(st, f"{tag}_ps_pv", [P, S])
        ps_cls = c.psum(st, f"{tag}_ps_cls", [P, S])
        neg_t = ps_cls[:, :].bitcast(BF16)[:, S:]
        ctx_t = ps_pv[:, :].rearrange("p (n h s) -> p n h s", h=HG, s=STRIP)

        loaded = [c.sem(st, f"{tag}_loaded{i}") for i in range(G)]
        ready = c.sem(st, f"{tag}_ready")
        vcls_mm = c.sem(st, f"{tag}_vcls_mm")
        cls_row = c.sem(st, f"{tag}_cls_row")
        s_mm = c.sem(st, f"{tag}_s_mm")
        max_ok = c.sem(st, f"{tag}_max_ok")
        neg_chain = c.sem(st, f"{tag}_neg_chain")
        fin_chain = c.sem(st, f"{tag}_fin_chain")
        vcls_ok = c.sem(st, f"{tag}_vcls_ok")
        neg_ok = c.sem(st, f"{tag}_neg_ok")
        cls_mm = c.sem(st, f"{tag}_cls_score_mm")
        sc_ok = c.sem(st, f"{tag}_sc_ok")
        nt_mm = c.sem(st, f"{tag}_nt_mm")
        nt_out = c.sem(st, f"{tag}_nt_out")
        pcls_ok = c.sem(st, f"{tag}_pcls_ok")
        st_mm = c.sem(st, f"{tag}_st_mm")
        exp_ok = c.sem(st, f"{tag}_exp_ok")
        pv_mm = c.sem(st, f"{tag}_pv_mm")
        pv_out = c.sem(st, f"{tag}_pv_out")
        bt_mm = c.sem(st, f"{tag}_bt_mm")
        fin_ok = c.sem(st, f"{tag}_fin_ok")
        block = st.enter_context(nc.Block())

        def keys(qt):
            return (qt + 1) * P if causal else S

        def q_from(kt):
            return kt * P if causal else 0

        def over_steps(eng, step):
            step(0, 0, False, True, True)
            with eng.Fori(0, B - 1) as b:
                for g in range(1, G + 1):
                    step(b, g, True, True, True)
            for g in range(1, G):
                step(B - 1, g, True, g + 1 < G, g + 2 < G)

        @block.sync
        def _(sp):
            for s in range(B * G):
                b, g = s // G, s % G
                if s >= G:
                    sp.wait_ge(pv_mm, 2 + NQ * (s - G + 1))
                load_step(sp, c, b, g, qs[g], ks[g], vs[g], loaded[g])
                if clear and s == G:
                    for xs in c.xs.values():
                        sp.dma_start(xs.rearrange("(p r) d -> p (r d)", p=P).rearrange("p (n w) -> p n w", w=D),
                                     c.zeros[:, :, :].broadcast_to([P, TILES, D])).then_inc(c.xs_clear, 16)
            c.fetch(sp, fetch)

        @block.gpsimd
        def _(pool):
            for i in range(2, G):
                pool.memset(ks[i][PARTS * HD:P, :, :], 1.0).then_inc(ready, 1)

        @block.tensor
        def _(pe):
            def score_units(b, g, units_now):
                q, k = qs[g % G], ks[g % G]
                for u in units_now:
                    qt, h = u // HG, u % HG
                    if u == 0:
                        pe.wait_ge(loaded[g % G], b * (16 * NLOADS) + 16 * NLOADS * (g // G + 1))
                    pe.wait_ge(max_ok, b * (G * units) + (g * units + u + 1))
                    lhs = q[0:PARTS * HD, h, qt * P:qt * P + P]
                    mm = pe.matmul(ps_s[:, u % 2, 0:keys(qt)], lhs, k[0:PARTS * HD, h, k0:k0 + keys(qt)],
                                   start=True, stop=not causal)
                    if causal:
                        mm = pe.matmul(ps_s[:, u % 2, qt * P:qt * P + P], c.ident_bf[:, :], c.mask_qk[:, :],
                                       start=False, stop=True)
                    mm.then_inc(s_mm, 1)

            def score_cls(b, g):
                q, k = qs[g % G], ks[g % G]
                pe.wait_ge(loaded[g % G], b * (16 * NLOADS) + 16 * NLOADS * (g // G + 1))
                for u in range(units):
                    qt, h = u // HG, u % HG
                    mm = pe.matmul(ps_cls[:, u:u + 1], q[0:PARTS * HD, h, qt * P:qt * P + P],
                                   k[0:PARTS * HD, h, 0:1], start=True, stop=True)
                mm.then_inc(cls_mm, 1)

            def turn_neg(b, g):
                pe.wait_ge(neg_ok, b * G + (g + 2))
                if not (isinstance(b, int) and b == 0 and g == 0):
                    pe.wait_ge(nt_out, b * (G * HG) + g * HG)
                for qt in range(NQ):
                    mm = pe.transpose(neg_t[:, qt * P:qt * P + P],
                                      neg[:, qt * HG:qt * HG + HG, :].rearrange("p h s -> p (h s)"), c.ident_bf[:, :])
                mm.then_inc(nt_mm, 1)

            def second(b, g, kt, pr):
                q, k = qs[g % G], ks[g % G]
                if kt == 0 and pr == 0:
                    pe.wait_ge(nt_out, b * (G * HG) + (g + 1) * HG)
                pe.wait_ge(exp_ok, b * (G * 8) + (g * 8 + 2 * kt + pr + 1))
                for h in (2 * pr, 2 * pr + 1):
                    mm = pe.matmul(ps_st[:, h, q_from(kt):], k[:, h, k0 + kt * P:k0 + kt * P + P],
                                   q[:, h, q_from(kt):], start=True, stop=not causal)
                    if causal:
                        mm = pe.matmul(ps_st[:, h, kt * P:kt * P + P], c.ident_bf[:, :], c.mask_kq[:, :],
                                       start=False, stop=True)
                mm.then_inc(st_mm, 1)

            def values(b, g, kt):
                pe.wait_ge(exp_ok, b * (G * 8) + (g * 8 + 2 * kt + 4))
                if kt == 0:
                    pe.wait_ge(fin_ok, b * G + (g + 1))
                for h in range(HG):
                    mm = pe.matmul(ps_pv[h * STRIP:h * STRIP + STRIP, q_from(kt):],
                                   vs[g % G][:, kt, h * STRIP:h * STRIP + STRIP],
                                   et[:, kt % 2, h, q_from(kt):], start=kt == 0, stop=kt == NQ - 1)
                mm.then_inc(pv_mm, 1)

            def turn_back(b, g):
                pe.wait_ge(pv_out, b * G + (g + 1))
                for qt in range(NQ):
                    mm = pe.transpose(ps_pv[:, qt * P:qt * P + P], pv_rows[:, qt * P:qt * P + P], c.ident[:, :])
                mm.then_inc(bt_mm, 1)

            def step(b, g, before, more, more2):
                ahead = [EARLY]

                def scores(n):
                    if more:
                        score_units(b, g + 1, range(ahead[0], ahead[0] + n))
                    ahead[0] += n

                scores(plan[0][0])
                second(b, g, 0, 0)
                if causal and more:
                    score_cls(b, g + 1)
                scores(plan[0][1])
                second(b, g, 0, 1)
                scores(plan[0][2])
                if before:
                    turn_back(b, g - 1)
                for kt, (n0, n1, n2, n3) in enumerate(plan[1:]):
                    scores(n0)
                    second(b, g, kt + 1, 0)
                    scores(n1)
                    second(b, g, kt + 1, 1)
                    scores(n2)
                    values(b, g, kt)
                    scores(n3)
                values(b, g, NQ - 1)
                if more2:
                    score_units(b, g + 2, range(EARLY - 1))
                if more:
                    turn_neg(b, g + 1)
                if more2:
                    score_units(b, g + 2, range(EARLY - 1, EARLY))

            pe.wait_ge(ready, G + 1)
            if causal:
                for b in range(B):
                    mm = pe.matmul(ps_st[:, b, 0:D], c.pick_cls[:, b, :], c.vcls[:, :], start=True, stop=True)
                mm.then_inc(vcls_mm, 1)
                pe.wait_ge(vcls_ok, 1)
            if causal:
                score_cls(0, 0)
            score_units(0, 0, range(units))
            score_units(0, 1, range(EARLY - 1))
            turn_neg(0, 0)
            score_units(0, 1, range(EARLY - 1, EARLY))
            over_steps(pe, step)
            turn_back(B - 1, G - 1)

        @block.scalar
        def _(act):
            def cls_exp(b, g):
                act.wait_ge(sc_ok, b * G + (g + 1))
                if not (isinstance(b, int) and b == 0 and g == 0):
                    act.wait_ge(fin_ok, b * G + g)
                act.activation(p_cls[:, g % 2, :], cls_score[:, :], ACT.Exp).then_inc(pcls_ok, 1)

            def neg_copy(b, g):
                act.wait_ge(nt_mm, b * G + (g + 1))
                for h in range(HG // 2):
                    act.activation(qs[g % G][PARTS * HD:P, h, :], neg_t[h * STRIP:h * STRIP + STRIP, :], ACT.Copy
                                   ).then_inc(nt_out, 1)

            def step(b, g, before, more, more2):
                for kt in range(NQ):
                    act.wait_ge(pv_mm, b * (G * NQ) + (g * NQ + kt + 1))
                    for pr in range(2):
                        act.wait_ge(st_mm, b * (G * 8) + (g * 8 + 2 * kt + pr + 1))
                        act.activation(et[:, kt % 2, 2 * pr:2 * pr + 2, q_from(kt):],
                                       ps_st[:, 2 * pr:2 * pr + 2, q_from(kt):], ACT.Exp).then_inc(exp_ok, 1)
                act.wait_ge(pv_mm, b * (G * NQ) + (g * NQ + NQ + 2))
                act.activation(pv_rows[:, :], ps_pv[:, :], ACT.Copy).then_inc(pv_out, 1)
                if more:
                    neg_copy(b, g + 1)
                if more and causal:
                    cls_exp(b, g + 1)

            act.sem_inc(exp_ok, 2)
            neg_copy(0, 0)
            if causal:
                cls_exp(0, 0)
            over_steps(act, step)

        n_neg = 4 if causal else 1
        n_fin = 4 if causal else 1

        @block.vector
        def _(dve):
            def maxima(b, g, units_now):
                for u in units_now:
                    qt = u // HG
                    if u == 0 and not (isinstance(b, int) and b == 0 and g == 0):
                        dve.wait_ge(neg_ok, b * G + g)
                    dve.wait_ge(s_mm, b * (G * units) + (g * units + u + 1))
                    dve.tensor_reduce(rowmax[:, g % 2, u:u + 1], ps_s[:, u % 2, 0:keys(qt)], AX_X, ALU.max
                                      ).then_inc(max_ok, 1)

            def negate(b, g):
                base = b * (G * n_neg) + g * n_neg
                dve.wait_ge(max_ok, b * (G * units) + (g * units + units + 2))
                src = rowmax[:, g % 2, :]
                if causal:
                    dve.wait_ge(cls_mm, b * G + (g + 1))
                    dve.tensor_copy(cls_raw[:, :], ps_cls[:, 0:units]).then_inc(neg_chain, 1)
                    dve.wait_ge(neg_chain, base + 1)
                    dve.tensor_tensor(top[:, :], src, cls_raw[:, :], ALU.max).then_inc(neg_chain, 1)
                    dve.wait_ge(neg_chain, base + 2)
                    src = top[:, :]
                dve.tensor_scalar(neg[:, :, 0], src, -1.0, None, ALU.mult).then_inc(neg_chain, 1)
                dve.wait_ge(neg_chain, base + (3 if causal else 1))
                dve.scalar_tensor_tensor(out=neg[:, :, 1], in0=src, scalar=-1.0, in1=neg[:, :, 0],
                                         op0=ALU.mult, op1=ALU.subtract).then_inc(neg_ok, 1)
                if causal:
                    dve.wait_ge(neg_ok, b * G + (g + 2))
                    dve.tensor_tensor(neg_sum[:, :], neg[:, :, 0], neg[:, :, 1], ALU.add).then_inc(neg_chain, 1)
                    dve.wait_ge(neg_chain, base + 4)
                    dve.wait_ge(pcls_ok, b * G + (g + 1))
                    dve.tensor_tensor(cls_score[:, :], cls_raw[:, :], neg_sum[:, :], ALU.add
                                      ).then_inc(sc_ok, 1)

            def neg_copy(b, g):
                dve.wait_ge(nt_mm, b * G + (g + 1))
                for h in range(HG // 2, HG):
                    dve.tensor_copy(qs[g % G][PARTS * HD:P, h, :], neg_t[h * STRIP:h * STRIP + STRIP, :]
                                    ).then_inc(nt_out, 1)

            def finish(b, g):
                base = b * (G * n_fin) + g * n_fin
                image, columns = b + g // G, slice(g % G * HG * HD, (g % G + 1) * HG * HD)
                dve.wait_ge(bt_mm, b * G + (g + 1))
                dve.wait_ge(fin_ok, b * G + (g + 1))
                pc = p_cls[:, g % 2, :]
                if causal:
                    dve.wait_ge(pcls_ok, b * G + (g + 2))
                    dve.tensor_tensor(cls_part[:, :, :, :],
                                      pc.rearrange("p (n h a) -> p n h a", n=NQ, a=1).broadcast_to([P, NQ, HG, HD]),
                                      v_cls[:, bass.ds(image, 1), columns].rearrange(
                                          "p a (h d) -> p a h d", d=HD).broadcast_to([P, NQ, HG, HD]),
                                      ALU.mult).then_inc(fin_chain, 1)
                    dve.tensor_tensor(den[:, :].rearrange("p (n h) -> p n h", n=NQ), ctx_t[:, :, :, HD],
                                      pc.rearrange("p (n h) -> p n h", n=NQ), ALU.add).then_inc(fin_chain, 1)
                    dve.wait_ge(fin_chain, base + 2)
                    dve.reciprocal(rden[:, :], den[:, :]).then_inc(fin_chain, 1)
                    dve.tensor_tensor(raw[:, :, :, :], ctx_t[:, :, :, 0:HD], cls_part[:, :, :, :], ALU.add
                                      ).then_inc(fin_chain, 1)
                    dve.wait_ge(fin_chain, base + 4)
                    src = raw[:, :, :, :]
                else:
                    dve.reciprocal(rden[:, :].rearrange("p (n h) -> p n h", n=NQ), ctx_t[:, :, :, HD]
                                   ).then_inc(fin_chain, 1)
                    dve.wait_ge(fin_chain, base + 1)
                    src = ctx_t[:, :, :, 0:HD]
                dve.tensor_tensor(
                    c.ctx[:, bass.ds(image * NQ, NQ), columns].rearrange("p n (h d) -> p n h d", d=HD),
                    src, rden[:, :].rearrange("p (n h a) -> p n h a", n=NQ, a=1).broadcast_to([P, NQ, HG, HD]),
                    ALU.mult).then_inc(fin_ok, 1)

            def step(b, g, before, more, more2):
                if more:
                    maxima(b, g + 1, range(EARLY, EARLY + FINISH_AFTER))
                if before:
                    finish(b, g - 1)
                if more:
                    maxima(b, g + 1, range(EARLY + FINISH_AFTER, units))
                    negate(b, g + 1)
                if more2:
                    maxima(b, g + 2, range(EARLY - 1))
                if more:
                    neg_copy(b, g + 1)
                if more2:
                    maxima(b, g + 2, range(EARLY - 1, EARLY))

            dve.memset(neg[:, :, :], 0.0).then_inc(ready, 1)
            for i in range(2):
                dve.memset(ks[i][PARTS * HD:P, :, :], 1.0).then_inc(ready, 1)
            dve.wait_ge(ready, G + 1)
            dve.sem_inc(max_ok, 2)
            dve.sem_inc(pv_mm, 2)
            dve.sem_inc(fin_ok, 1)
            dve.sem_inc(neg_ok, 1)
            dve.sem_inc(pcls_ok, 1)
            if causal:
                dve.wait_ge(vcls_mm, 1)
                dve.tensor_copy(v_cls[:, :, :], ps_st[:, :, 0:D]).then_inc(vcls_ok, 1)
                dve.tensor_copy(c.ctx[0:B, NT, :], c.vcls[:, :]).then_inc(cls_row, 1)
            maxima(0, 0, range(units))
            negate(0, 0)
            maxima(0, 1, range(EARLY - 1))
            neg_copy(0, 0)
            maxima(0, 1, range(EARLY - 1, EARLY))
            over_steps(dve, step)
            finish(B - 1, G - 1)


def attend_top(c, tag):
    nc = c.nc
    units = NQ * HG
    pairs = units // 2
    rounds = K_TOP // 8
    ops = 2 * rounds
    WIDE = S + 1
    with c.stage() as st:
        qs = [c.sbuf(st, f"{tag}_qs{i}", [P, HG, S], BF16) for i in range(2)]
        ks = [c.sbuf(st, f"{tag}_ks{i}", [P, HG, WIDE], BF16) for i in range(2)]
        vs = [c.sbuf(st, f"{tag}_vs{i}", [P, NQ, P], F32) for i in range(2)]
        largest = c.sbuf(st, f"{tag}_largest", [P, 4, rounds, 8], F32)
        raw = c.sbuf(st, f"{tag}_raw", [P, 4, WIDE], F32)
        left = c.sbuf(st, f"{tag}_left", [P, 4, WIDE], F32)
        neg_max = c.sbuf(st, f"{tag}_neg_max", [P, 4], F32)
        e_all = c.sbuf(st, f"{tag}_e_all", [P, 4, WIDE], F32)
        e_left = c.sbuf(st, f"{tag}_e_left", [P, 2, WIDE], F32)
        prob = c.sbuf(st, f"{tag}_prob", [P, 2, HG, WIDE], F32)
        prob_t = c.sbuf(st, f"{tag}_prob_t", [P, 2, HG, S], F32)
        pv_rows = c.sbuf(st, f"{tag}_pv_rows", [P, P], F32)
        back = c.sbuf(st, f"{tag}_back", [P, HG, STRIP], F32)
        v_cls = c.sbuf(st, f"{tag}_v_cls", [P, B, D], F32)
        cls_part = c.sbuf(st, f"{tag}_cls_part", [P, HG, HD], F32)
        den = c.sbuf(st, f"{tag}_den", [P, NT, NH], F32)
        rden = c.sbuf(st, f"{tag}_rden", [P, NT, NH], F32)
        ps_s = c.psum(st, f"{tag}_ps_s", [P, 2, 2 * S])
        ps_t = c.psum(st, f"{tag}_ps_pt", [P, 2, S])
        ps_pv = c.psum(st, f"{tag}_ps_pv", [P, S])
        ps_back = c.psum(st, f"{tag}_ps_back", [P, S])

        loaded = [c.sem(st, f"{tag}_loaded{i}") for i in range(2)]
        vcls_mm = c.sem(st, f"{tag}_vcls_mm")
        vcls_ok = c.sem(st, f"{tag}_vcls_ok")
        s_mm = c.sem(st, f"{tag}_s_mm")
        raw_ok = c.sem(st, f"{tag}_raw_ok")
        pick = c.sem(st, f"{tag}_pick")
        neg_ok = c.sem(st, f"{tag}_neg_ok")
        all_ok = c.sem(st, f"{tag}_all_ok")
        left_ok = c.sem(st, f"{tag}_left_ok")
        prob_ok = c.sem(st, f"{tag}_prob_ok")
        t_mm = c.sem(st, f"{tag}_pt_mm")
        t_out = c.sem(st, f"{tag}_pt_out")
        pv_mm = c.sem(st, f"{tag}_pv_mm")
        pv_out = c.sem(st, f"{tag}_pv_out")
        bt_mm = c.sem(st, f"{tag}_bt_mm")
        back_ok = c.sem(st, f"{tag}_back_ok")
        part_ok = c.sem(st, f"{tag}_part_ok")
        fin_ok = c.sem(st, f"{tag}_fin_ok")
        scale_ok = c.sem(st, f"{tag}_scale_ok")
        block = st.enter_context(nc.Block())

        def keys(qt):
            return (qt + 1) * P

        def row(i, qt):
            return ps_s[:, i, S - 1:S + keys(qt)]

        def unit(b, g, u):
            return b * (G * units) + (g * units + u)

        def group(b, g, qt):
            return b * (G * NQ) + (g * NQ + qt)

        def picked(b, g, k, j, i):
            return b * (G * pairs * 2 * ops) + ((g * pairs + k) * 2 * ops + 2 * j + i + 1 + 4 * ops)

        def ahead(do, b, g, k, more):
            if k + 2 < pairs:
                do(b, g, k + 2)
            elif more:
                do(b, g + 1, k + 2 - pairs)

        def with_before(b, g, before):
            for k in range(pairs):
                yield k, ((b, g, k - 1) if k else (b, g - 1, pairs - 1) if before else None)

        def over_steps(eng, step):
            step(0, 0, False, True)
            with eng.Fori(0, B - 1) as b:
                for g in range(1, G + 1):
                    step(b, g, True, True)
            for g in range(1, G):
                step(B - 1, g, True, g + 1 < G)

        @block.sync
        def _(sp):
            for s in range(B * G):
                b, g = s // G, s % G
                if s >= 2:
                    sp.wait_ge(pv_mm, 2 + NQ * (s - 1))
                load_step(sp, c, b, g, qs[s % 2], ks[s % 2], vs[s % 2], loaded[s % 2])

        @block.tensor
        def _(pe):
            def score_pair(b, g, k):
                q, kk = qs[g % 2], ks[g % 2]
                qt = 2 * k // HG
                if k == 0:
                    pe.wait_ge(loaded[g % 2], b * (32 * NLOADS) + 16 * NLOADS * (g // 2 + 1))
                for i in range(2):
                    h = (2 * k + i) % HG
                    pe.wait_ge(raw_ok, unit(b, g, 2 * k + i + 1))
                    lhs = q[0:PARTS * HD, h, qt * P:qt * P + P]
                    pe.matmul(ps_s[:, i, S - 1:S], lhs, kk[0:PARTS * HD, h, 0:1], start=True, stop=True)
                    pe.matmul(ps_s[:, i, S:S + keys(qt)], lhs, kk[0:PARTS * HD, h, 1:1 + keys(qt)],
                              start=True, stop=False)
                    pe.matmul(ps_s[:, i, S + qt * P:S + qt * P + P], c.ident_bf[:, :], c.mask_qk[:, :],
                              start=False, stop=True).then_inc(s_mm, 1)

            def turn_pair(b, g, k):
                qt = 2 * k // HG
                for i in range(2):
                    u = 2 * k + i
                    pe.wait_ge(prob_ok, unit(b, g, u + 5))
                    pe.wait_ge(t_out, unit(b, g, u + 1))
                    for ch in range(qt + 1):
                        mm = pe.transpose(ps_t[:, i, ch * P:ch * P + P],
                                          prob[:, qt % 2, u % HG, 1 + ch * P:1 + ch * P + P], c.ident[:, :])
                    mm.then_inc(t_mm, 1)

            def values(b, g, qt):
                pe.wait_ge(t_out, unit(b, g, qt * HG + HG + 2))
                for ch in range(qt + 1):
                    for h in range(HG):
                        mm = pe.matmul(ps_pv[h * STRIP:h * STRIP + STRIP, 0:P],
                                       vs[g % 2][:, ch, h * STRIP:h * STRIP + STRIP],
                                       prob_t[:, qt % 2, h, ch * P:ch * P + P], start=ch == 0, stop=ch == qt)
                mm.then_inc(pv_mm, 1)
                pe.wait_ge(pv_out, group(b, g, qt + 1))
                pe.transpose(ps_back[:, 0:P], pv_rows[:, :], c.ident[:, :]).then_inc(bt_mm, 1)

            def use(b, g, k):
                turn_pair(b, g, k)
                if 2 * k % HG == HG - 2:
                    values(b, g, 2 * k // HG)

            def step(b, g, before, more):
                for k, last in with_before(b, g, before):
                    ahead(score_pair, b, g, k, more)
                    if last:
                        use(*last)

            for b in range(B):
                mm = pe.matmul(ps_s[:, b // 2, b % 2 * S:b % 2 * S + D], c.pick_cls[:, b, :], c.vcls[:, :],
                               start=True, stop=True)
            mm.then_inc(vcls_mm, 1)
            pe.wait_ge(vcls_ok, 2)
            score_pair(0, 0, 0)
            score_pair(0, 0, 1)
            over_steps(pe, step)
            use(B - 1, G - 1, pairs - 1)

        @block.scalar
        def _(act):
            def copy_pair(b, g, k):
                qt = 2 * k // HG
                for i in range(2):
                    act.wait_ge(s_mm, unit(b, g, 2 * k + i + 1))
                    act.wait_ge(pick, picked(b, g, k, 1, i) - 4 * ops)
                    act.wait_ge(all_ok, unit(b, g, 2 * k + i + 1))
                    act.activation(raw[:, 2 * (k % 2) + i, 0:1 + keys(qt)], row(i, qt), ACT.Copy
                                   ).then_inc(raw_ok, 1)

            def use(b, g, k):
                qt = 2 * k // HG
                w = 1 + keys(qt)
                for i in range(2):
                    u = 2 * k + i
                    act.wait_ge(t_mm, unit(b, g, u + 9))
                    act.wait_ge(pv_mm, group(b, g, qt + 1))
                    act.activation(prob_t[:, qt % 2, u % HG, 0:w - 1], ps_t[:, i, 0:w - 1], ACT.Copy
                                   ).then_inc(t_out, 1)
                if 2 * k % HG == HG - 2:
                    act.wait_ge(pv_mm, group(b, g, qt + 3))
                    act.activation(pv_rows[:, :], ps_pv[:, 0:P], ACT.Copy).then_inc(pv_out, 1)
                    act.wait_ge(bt_mm, group(b, g, qt + 1))
                    act.wait_ge(fin_ok, group(b, g, qt + 1))
                    act.activation(back[:, :, :], ps_back[:, 0:P].rearrange("p (h s) -> p h s", s=STRIP),
                                   ACT.Copy).then_inc(back_ok, 1)

            def step(b, g, before, more):
                for k, last in with_before(b, g, before):
                    qt = 2 * k // HG
                    w = 1 + keys(qt)
                    for i in range(2):
                        u, j = 2 * k + i, 2 * (k % 2) + i
                        act.wait_ge(neg_ok, unit(b, g, u + 5))
                        act.wait_ge(prob_ok, unit(b, g, u + 1))
                        act.activation(e_all[:, j, 0:w], raw[:, j, 0:w], ACT.Exp, bias=neg_max[:, j:j + 1]
                                       ).then_inc(all_ok, 1)
                    ahead(copy_pair, b, g, k, more)
                    for i in range(2):
                        u, j = 2 * k + i, 2 * (k % 2) + i
                        act.wait_ge(pick, picked(b, g, k, ops - 1, i))
                        act.wait_ge(prob_ok, unit(b, g, u + 3))
                        act.activation(e_left[:, i, 0:w], left[:, j, 0:w], ACT.Exp, bias=neg_max[:, j:j + 1]
                                       ).then_inc(left_ok, 1)
                    if last:
                        use(*last)

            act.sem_inc(raw_ok, 2)
            act.sem_inc(all_ok, 4)
            act.sem_inc(left_ok, 4)
            act.sem_inc(t_out, 2)
            act.wait_ge(vcls_ok, 2)
            copy_pair(0, 0, 0)
            copy_pair(0, 0, 1)
            over_steps(act, step)
            use(B - 1, G - 1, pairs - 1)

        @block.gpsimd
        def _(pool):
            def use(b, g, k):
                qt = 2 * k // HG
                w = 1 + keys(qt)
                for i in range(2):
                    u = 2 * k + i
                    pool.wait_ge(left_ok, unit(b, g, u + 5))
                    pool.wait_ge(t_mm, unit(b, g, u + 1))
                    pool.wait_ge(fin_ok, group(b, g, qt + 1))
                    pool.tensor_tensor(prob[:, qt % 2, u % HG, 0:w], e_all[:, 2 * (k % 2) + i, 0:w],
                                       e_left[:, i, 0:w], ALU.subtract).then_inc(prob_ok, 1)

            def finish(b, g, qt):
                p_cls = prob[:, qt % 2, :, 0:1]
                image, columns = b + g // G, slice(g % G * HG * HD, (g % G + 1) * HG * HD)
                n = image * NQ + qt
                pool.wait_ge(prob_ok, unit(b, g, qt * HG + HG + 4))
                pool.nop(nofuse=True)
                pool.tensor_tensor(cls_part[:, :, :], p_cls.broadcast_to([P, HG, HD]),
                                   v_cls[:, bass.ds(image, 1), columns].rearrange("p a (h d) -> p (a h) d", d=HD),
                                   ALU.mult).then_inc(part_ok, 1)
                pool.wait_ge(back_ok, group(b, g, qt + 1))
                pool.wait_ge(part_ok, 2 * group(b, g, qt) + 1)
                pool.nop(nofuse=True)
                pool.tensor_tensor(den[:, bass.ds(n, 1), g % G * HG:g % G * HG + HG].rearrange("p a h -> p (a h)"),
                                   back[:, :, HD], prob[:, qt % 2, :, 0], ALU.add).then_inc(part_ok, 1)
                pool.wait_ge(part_ok, 2 * group(b, g, qt) + 2)
                pool.nop(nofuse=True)
                pool.tensor_tensor(c.ctx[:, bass.ds(n, 1), columns].rearrange("p a (h d) -> p (a h) d", d=HD),
                                   back[:, :, 0:HD], cls_part[:, :, :], ALU.add).then_inc(fin_ok, 1)

            def step(b, g, before, more):
                for k, last in with_before(b, g, before):
                    for i in range(2):
                        u, j = 2 * k + i, 2 * (k % 2) + i
                        pool.wait_ge(pick, picked(b, g, k, 0, i))
                        pool.wait_ge(left_ok, unit(b, g, u + 1))
                        pool.nop(nofuse=True)
                        pool.tensor_scalar(neg_max[:, j:j + 1], largest[:, j, 0, 0:1], -1.0, None, ALU.mult
                                           ).then_inc(neg_ok, 1)
                    if last:
                        if last[2] % 2 == 0 and (before or k > 1):
                            finish(*((last[0], last[1], last[2] // 2 - 1) if last[2] else
                                     (last[0], last[1] - 1, NQ - 1)))
                        use(*last)

            pool.sem_inc(prob_ok, 4)
            pool.sem_inc(fin_ok, 1)
            pool.wait_ge(vcls_ok, 2)
            over_steps(pool, step)
            use(B - 1, G - 1, pairs - 1)
            finish(B - 1, G - 1, NQ - 1)

        @block.vector
        def _(dve):
            def step(b, g):
                for k in range(pairs):
                    qt = 2 * k // HG
                    w = 1 + keys(qt)
                    for j in range(ops):
                        for i in range(2):
                            u, at = 2 * k + i, 2 * (k % 2) + i
                            src = raw[:, at, 0:w] if j < 2 else left[:, at, 0:w]
                            if j == 0:
                                dve.wait_ge(raw_ok, unit(b, g, u + 3))
                                dve.wait_ge(pick, picked(b, g, k, ops - 1, i) - 4 * ops)
                                dve.wait_ge(neg_ok, unit(b, g, u + 1))
                            else:
                                dve.wait_ge(pick, picked(b, g, k, j - 1, i))
                            if j == 1:
                                dve.wait_ge(left_ok, unit(b, g, u + 1))
                            dve.nop(nofuse=True)
                            if j % 2 == 0:
                                ins = dve.max(largest[:, at, j // 2, :], src)
                            else:
                                ins = dve.match_replace(left[:, at, 0:w], largest[:, at, j // 2, :], src, TAKEN)
                            ins.then_inc(pick, 1)

            dve.sem_inc(pick, 4 * ops)
            dve.sem_inc(neg_ok, 4)
            dve.sem_inc(t_mm, 8)
            dve.sem_inc(pv_mm, 2)
            dve.wait_ge(vcls_mm, 1)
            for i in range(2):
                dve.tensor_copy(v_cls[:, 2 * i:2 * i + 2, :], ps_s[:, i, :].rearrange("p (a n) -> p a n", a=2)[:, :, 0:D]
                                ).then_inc(vcls_ok, 1)
            dve.tensor_copy(c.ctx[0:B, NT, :], c.vcls[:, :]).then_inc(scale_ok, 1)
            with dve.Fori(0, B) as b:
                for g in range(G):
                    step(b, g)
            dve.wait_ge(fin_ok, 1 + B * G * NQ)
            dve.reciprocal(rden[:, :, :], den[:, :, :]).then_inc(scale_ok, 1)
            dve.wait_ge(scale_ok, 2)
            for n in range(NT):
                ctx_n = c.ctx[:, n, :].rearrange("p (h d) -> p h d", d=HD)
                dve.tensor_tensor(ctx_n, ctx_n,
                                  rden[:, n, :].rearrange("p (h a) -> p h a", a=1).broadcast_to([P, NH, HD]),
                                  ALU.mult).then_inc(scale_ok, 1)


def attend_out(c, tag, wo_dram, bo_dram, residual, cls, keep=None, fetch=()):
    nc = c.nc
    n_all = NT + 1
    tiles = NT + (1 if cls else 0)
    with c.stage() as st:
        wo = c.sbuf(st, f"{tag}_wo", [P, DC, D], F32)
        bo = c.sbuf(st, f"{tag}_bo", [P, D], F32)
        ctx_t = c.sbuf(st, f"{tag}_ctx_t", [P, 2, DC, P], F32)
        summed = c.sbuf(st, f"{tag}_summed", [P, 2, D], F32)
        stats = c.sbuf(st, f"{tag}_stats", [P, n_all, 6], F32)
        mv = c.sbuf(st, f"{tag}_mv", [P, n_all, 2], F32)
        std = c.sbuf(st, f"{tag}_std", [P, n_all], F32)
        rstd = c.sbuf(st, f"{tag}_rstd", [P, n_all], F32)
        eps = c.sbuf(st, f"{tag}_eps", [P, 1], F32)
        xn = keep if keep is not None else c.sbuf(st, f"{tag}_xn", [P, n_all, D], F32)
        ps_t = c.psum(st, f"{tag}_ps_t", [P, 2, S])
        ps_o = c.psum(st, f"{tag}_ps_o", [P, 2, S])
        ps_x = c.psum(st, f"{tag}_ps_x", [P, 2, S])
        w_in = c.sem(st, f"{tag}_wo_in")
        t_mm = c.sem(st, f"{tag}_t_mm")
        t_out = c.sem(st, f"{tag}_t_out")
        o_mm = c.sem(st, f"{tag}_o_mm")
        sum_ok = c.sem(st, f"{tag}_sum_ok")
        h_ok = c.sem(st, f"{tag}_h_ok")
        eps_ok = c.sem(st, f"{tag}_eps_ok")
        stat_ok = c.sem(st, f"{tag}_stat_ok")
        aggr_ok = c.sem(st, f"{tag}_aggr_ok")
        std_ok = c.sem(st, f"{tag}_std_ok")
        rstd_ok = c.sem(st, f"{tag}_rstd_ok")
        xn_ok = c.sem(st, f"{tag}_xn_ok")
        x_mm = c.sem(st, f"{tag}_x_mm")
        x_out = c.sem(st, f"{tag}_x_out")
        block = st.enter_context(nc.Block())

        def rows(n):
            return P if n < NT else B

        @block.sync
        def _(sp):
            sp.dma_start(wo[:, :, :], wo_dram).then_inc(w_in, 16)
            sp.dma_start(bo[:, :], bo_dram.partition_broadcast(P)).then_inc(w_in, 16)
            c.fetch(sp, fetch)

        @block.tensor
        def _(pe):
            def turn(n):
                r = rows(n)
                if n >= 2:
                    pe.wait_ge(t_out, n - 1)
                for ch in range(DC):
                    mm = pe.transpose(ps_t[:, n % 2, ch * P:ch * P + r], c.ctx[0:r, n, ch * P:ch * P + P],
                                      c.ident[0:r, 0:r])
                mm.then_inc(t_mm, 1)

            def project_tile(n):
                pe.wait_ge(t_out, n + 1)
                if n >= 2:
                    pe.wait_ge(sum_ok, n - 1)
                for ch in range(DC):
                    mm = pe.matmul(ps_o[0:rows(n), n % 2, 0:D], ctx_t[:, n % 2, ch, 0:rows(n)], wo[:, ch, :],
                                   start=ch == 0, stop=ch == DC - 1)
                mm.then_inc(o_mm, 1)

            def turn_normed(n):
                r = rows(n)
                pe.wait_ge(xn_ok, n + 1)
                if n >= 2:
                    pe.wait_ge(x_out, n - 1)
                for ch in range(DC):
                    mm = pe.transpose(ps_x[:, n % 2, ch * P:ch * P + r], xn[0:r, n, ch * P:ch * P + P],
                                      c.ident[0:r, 0:r])
                mm.then_inc(x_mm, 1)

            turn(0)
            pe.wait_ge(w_in, 32)
            for n in range(n_all + 2):
                if n + 1 < tiles:
                    turn(n + 1)
                if n < tiles:
                    project_tile(n)
                if n >= 2:
                    turn_normed(n - 2)

        @block.scalar
        def _(act):
            def ctx_copy(n):
                r = rows(n)
                act.wait_ge(t_mm, n + 1)
                if n >= 2:
                    act.wait_ge(o_mm, n - 1)
                act.activation(ctx_t[:, n % 2, :, 0:r],
                               ps_t[:, n % 2, 0:DC * P].rearrange("p (c t) -> p c t", c=DC)[:, :, 0:r],
                               ACT.Copy).then_inc(t_out, 1)

            def deviation(n):
                act.wait_ge(aggr_ok, n + 1)
                act.activation(std[:, n:n + 1], mv[:, n, 1:2], ACT.Sqrt, bias=eps[:, 0:1]).then_inc(std_ok, 1)

            def x_copy(n):
                act.wait_ge(x_mm, n + 1)
                src = ps_x[:, n % 2, 0:DC * P].rearrange("p (c t) -> p c t", c=DC)
                if n < NT:
                    at = 1 + (n % NQ) * P
                    act.activation(c.xt[:, :, n // NQ, at:at + P], src, ACT.Copy).then_inc(x_out, 1)
                else:
                    act.activation(c.xt[:, :, :, 0], src[:, :, 0:B], ACT.Copy).then_inc(x_out, 1)

            act.wait_ge(eps_ok, 1)
            for n in range(n_all + 3):
                if n < tiles:
                    ctx_copy(n)
                if 1 <= n <= n_all:
                    deviation(n - 1)
                if n >= 3:
                    x_copy(n - 3)

        @block.vector
        def _(dve):
            def sums(n):
                r = rows(n)
                dve.wait_ge(o_mm, n + 1)
                if residual:
                    if n >= 2:
                        dve.wait_ge(h_ok, n - 1)
                    dve.tensor_tensor(summed[0:r, n % 2, :], ps_o[0:r, n % 2, 0:D], bo[0:r, :], ALU.add
                                      ).then_inc(sum_ok, 1)
                    dve.wait_ge(sum_ok, n + 1)
                    dve.tensor_tensor(c.h[0:r, n, :], c.h[0:r, n, :], summed[0:r, n % 2, :], ALU.add
                                      ).then_inc(h_ok, 1)
                    dve.wait_ge(h_ok, n + 1)
                else:
                    dve.tensor_tensor(c.h[0:r, n, :], ps_o[0:r, n % 2, 0:D], bo[0:r, :], ALU.add
                                      ).then_inc(sum_ok, 1)
                    dve.wait_ge(sum_ok, n + 1)

            def moments(n):
                dve.bn_stats(stats[:, n, :], c.h[:, n, :]).then_inc(stat_ok, 1)
                dve.wait_ge(stat_ok, n + 1)
                dve.bn_aggr(mv[:, n, :], stats[:, n, :]).then_inc(aggr_ok, 1)

            def normalise(n):
                dve.wait_ge(std_ok, n + 1)
                dve.reciprocal(rstd[:, n:n + 1], std[:, n:n + 1]).then_inc(rstd_ok, 1)
                dve.wait_ge(rstd_ok, n + 1)
                dve.wait_ge(aggr_ok, n + 1)
                dve.tensor_scalar(xn[:, n, :], c.h[:, n, :], mv[:, n, 0:1], rstd[:, n:n + 1],
                                  ALU.subtract, ALU.mult).then_inc(xn_ok, 1)

            dve.memset(eps[:, :], EPS).then_inc(eps_ok, 1)
            dve.wait_ge(w_in, 32)
            for n in range(n_all + 1):
                if n < tiles:
                    sums(n)
                if n < n_all:
                    moments(n)
                if n >= 1:
                    normalise(n - 1)


def dispatch(c, tag, xn, idx):
    nc = c.nc
    n_all = NT + 1
    with c.stage() as st:
        chosen = c.sbuf(st, f"{tag}_chosen", [P, 2, n_all, E], F32)
        both = c.sbuf(st, f"{tag}_both", [P, n_all, E], BF16)
        base = c.sbuf(st, f"{tag}_base", [P, n_all + 1, E], F32)
        begin = c.sbuf(st, f"{tag}_begin", [P, E + 1], F32)
        tiles = c.sbuf(st, f"{tag}_tiles", [P, E], F32)
        over = c.sbuf(st, f"{tag}_over", [P, E, n_all], F32)
        slot = c.sbuf(st, f"{tag}_slot", [P, n_all, E], F32)
        slot_in = c.sbuf(st, f"{tag}_slot_in", [P, n_all, E], F32)
        mine = c.sbuf(st, f"{tag}_mine", [P, 2, n_all, E], F32)
        at = c.sbuf(st, f"{tag}_at", [P, 2, n_all], F32)
        has = c.sbuf(st, f"{tag}_has", [P, 2, n_all], F32)
        past = c.sbuf(st, f"{tag}_past", [P, TILES, E - 1], F32)
        owner_f = c.sbuf(st, f"{tag}_owner_f", [P, TILES], F32)
        ps_rank = c.psum(st, f"{tag}_ps_rank", [P, S])
        ps_total = c.psum(st, f"{tag}_ps_total", [P, S])
        both_ok = c.sem(st, f"{tag}_both_ok")
        rank_mm = c.sem(st, f"{tag}_rank_mm")
        chain = c.sem(st, f"{tag}_d_chain")
        row_ok = c.sem(st, f"{tag}_row_ok")
        sent = c.sem(st, f"{tag}_sent")
        block = st.enter_context(nc.Block())
        rank = ps_rank[:, 0:n_all * E].rearrange("p (n e) -> p n e", e=E)
        total = ps_total[:, 0:n_all * E].rearrange("p (n e) -> p n e", e=E)

        @block.vector
        def _(dve):
            done = [0]

            def then(ins):
                done[0] += 1
                ins.then_inc(chain, 1)
                dve.wait_ge(chain, done[0])

            for k in range(2):
                then(dve.tensor_tensor(chosen[:, k, :, :],
                                       c.iota_e[:, :].rearrange("p (a e) -> p a e", a=1).broadcast_to([P, n_all, E]),
                                       idx[:, :, k:k + 1].broadcast_to([P, n_all, E]), ALU.is_equal))
                then(dve.tensor_tensor(chosen[:, k, :, :], chosen[:, k, :, :],
                                       c.valid[:, :].rearrange("p (n a) -> p n a", a=1).broadcast_to([P, n_all, E]),
                                       ALU.mult))
            dve.tensor_tensor(both[:, :, :], chosen[:, 0, :, :], chosen[:, 1, :, :], ALU.add).then_inc(both_ok, 1)
            then(dve.memset(base[:, 0, :], 0.0))
            dve.wait_ge(rank_mm, 2)
            for n in range(n_all):
                then(dve.tensor_tensor(base[:, n + 1, :], base[:, n, :], total[:, n, :], ALU.add))
            then(dve.tensor_tensor(over[:, :, :],
                                   base[:, n_all, :].rearrange("p (e a) -> p e a", a=1).broadcast_to([P, E, n_all]),
                                   c.steps[:, :].rearrange("p (a n) -> p a n", a=1).broadcast_to([P, E, n_all]),
                                   ALU.is_gt))
            then(dve.tensor_reduce(tiles[:, :], over[:, :, :], AX_X, ALU.add))
            then(dve.memset(begin[:, 0:1], 0.0))
            for e in range(E):
                then(dve.tensor_tensor(begin[:, e + 1:e + 2], begin[:, e:e + 1], tiles[:, e:e + 1], ALU.add))
            then(dve.scalar_tensor_tensor(
                out=slot_in[:, :, :], in0=begin[:, 0:E].rearrange("p (a e) -> p a e", a=1).broadcast_to([P, n_all, E]),
                scalar=float(P), in1=base[:, 0:n_all, :], op0=ALU.mult, op1=ALU.add))
            then(dve.tensor_tensor(slot[:, :, :], slot_in[:, :, :], rank, ALU.add))
            for k in range(2):
                then(dve.tensor_tensor(mine[:, k, :, :], chosen[:, k, :, :], slot[:, :, :], ALU.mult))
            then(dve.tensor_reduce(at[:, :, :], mine[:, :, :, :], AX_X, ALU.add))
            then(dve.tensor_reduce(has[:, :, :], chosen[:, :, :, :], AX_X, ALU.add))
            then(dve.scalar_tensor_tensor(out=at[:, :, :], in0=has[:, :, :], scalar=-float(NOWHERE),
                                          in1=at[:, :, :], op0=ALU.mult, op1=ALU.add))
            dve.tensor_scalar(c.row[:, :, :], at[:, :, :], float(NOWHERE), None, ALU.add).then_inc(row_ok, 1)
            then(dve.tensor_tensor(past[:, :, :],
                                   c.iota_t[:, :].rearrange("p (t a) -> p t a", a=1).broadcast_to([P, TILES, E - 1]),
                                   begin[:, 1:E].rearrange("p (a e) -> p a e", a=1).broadcast_to([P, TILES, E - 1]),
                                   ALU.is_ge))
            then(dve.tensor_reduce(owner_f[:, :], past[:, :, :], AX_X, ALU.add))
            dve.tensor_copy(c.owner[:, :], owner_f[:, :]).then_inc(row_ok, 1)
            dve.tensor_copy(c.used[:, :], begin[:, E:E + 1]).then_inc(row_ok, 1)

        @block.tensor
        def _(pe):
            pe.wait_ge(both_ok, 1)
            pe.matmul(ps_rank[:, 0:n_all * E], c.before[:, :], both[:, :, :], start=True, stop=True
                      ).then_inc(rank_mm, 1)
            pe.matmul(ps_total[:, 0:n_all * E], c.ones_bf[:, :], both[:, :, :], start=True, stop=True
                      ).then_inc(rank_mm, 1)

        @block.gpsimd
        def _(pool):
            pool.wait_ge(c.xs_clear, 16 * len(c.xs))
            pool.wait_ge(row_ok, 3)
            used = pool.value_load(c.used[0:1, 0:1], min_val=0, max_val=TILES)
            with pool.If(used > 0):
                for n in range(n_all):
                    for k in range(2):
                        pool.indirect_dma_start(
                            out=c.xs[tag][:, :], out_offset=bass.IndirectOffsetOnAxis(ap=c.row[:, k, n:n + 1], axis=0),
                            in_=xn[:, n, :], in_offset=None, bounds_check=TILES * P - 1, oob_is_err=False
                        ).then_inc(sent, 16)
                pool.wait_ge(sent, 16 * 2 * n_all)


def run_gated_experts(c, tag, w1, w2, hidden):
    nc = c.nc
    HC = hidden // P
    with c.stage() as st:
        rows = c.sbuf(st, f"{tag}_rows", [P, 2, D], F32)
        rows_t = c.sbuf(st, f"{tag}_rows_t", [P, 2, DC, P], F32)
        hid = c.sbuf(st, f"{tag}_hid", [P, 2, hidden], F32)
        hid_t = c.sbuf(st, f"{tag}_hid_t", [P, 2, HC, P], F32)
        y = c.sbuf(st, f"{tag}_y", [P, 2, D], F32)
        act_gate = c.sbuf(st, f"{tag}_act_gate", [P, 2, hidden], F32)
        ps_x = c.psum(st, f"{tag}_ps_x", [P, S])
        ps_h = c.psum(st, f"{tag}_ps_h", [P, 2, 2, S])
        ps_ht = c.psum(st, f"{tag}_ps_ht", [P, S])
        ps_y = c.psum(st, f"{tag}_ps_y", [P, S])
        rows_in = [c.sem(st, f"{tag}_rows_in{i}") for i in range(2)]
        x_mm = c.sem(st, f"{tag}_x_mm")
        x_out = c.sem(st, f"{tag}_x_out")
        h_mm = c.sem(st, f"{tag}_h_mm")
        gate_ok = c.sem(st, f"{tag}_gate_ok")
        hid_ok = c.sem(st, f"{tag}_hid_ok")
        ht_mm = c.sem(st, f"{tag}_ht_mm")
        ht_out = c.sem(st, f"{tag}_ht_out")
        y_mm = c.sem(st, f"{tag}_y_mm")
        y_ok = c.sem(st, f"{tag}_y_ok")
        y_sent = [c.sem(st, f"{tag}_y_sent{i}") for i in range(2)]
        block = st.enter_context(nc.Block())

        def used_tiles(eng):
            return eng.value_load(c.used[0:1, 0:1], min_val=0, max_val=TILES)

        @block.sync
        def _(sp):
            def load_rows(i):
                sp.dma_start(rows[:, i % 2, :], c.xs[tag][i * P:(i + 1) * P, :]).then_inc(rows_in[i % 2], 16)

            used = used_tiles(sp)
            for i in range(2):
                sp.sem_inc(y_sent[i], 16)
                load_rows(i)
            lag = 3
            def reload_rows(i):
                sp.wait_ge(x_mm, i - 1)
                load_rows(i)

            def store_y(j):
                sp.wait_ge(y_ok, j + 2)
                sp.dma_start(c.ys[tag][j * P:(j + 1) * P, :], y[:, j % 2, :]).then_inc(y_sent[j % 2], 16)

            for i in range(2, TILES + lag):
                if i < SURE_TILES + 2:
                    reload_rows(i)
                elif i < TILES:
                    with sp.If(used > i - 2):
                        reload_rows(i)
                j = i - lag
                if 0 <= j < SURE_TILES:
                    store_y(j)
                elif j >= 0:
                    with sp.If(used > j):
                        store_y(j)
                    with sp.Else():
                        sp.dma_start(c.ys[tag][j * P:(j + 1) * P, :], c.zeros[:, 0, :]).then_inc(y_sent[j % 2], 16)
            for i in range(2):
                sp.wait_ge(y_sent[i], 16 + 16 * (TILES // 2))

        @block.tensor
        def _(pe):
            def turn_rows(it, k):
                pe.wait_ge(rows_in[k % 2], it * 16 + 16 * (k // 2 + 1))
                pe.wait_ge(x_out, it * 2 + (k + 1))
                for ch in range(DC):
                    mm = pe.transpose(ps_x[:, ch * P:ch * P + P], rows[:, k % 2, ch * P:ch * P + P], c.ident[:, :])
                mm.then_inc(x_mm, 1)

            def owner(it, k):
                return pe.value_load(c.owner[0:1, bass.ds(it * 2 + k, 1)], min_val=0, max_val=E - 1)

            def first(it, k, e):
                pe.wait_ge(x_out, it * 2 + (k + 2))
                pe.wait_ge(hid_ok, it * 2 + (k + 1))
                for half in range(2):
                    for ch in range(DC):
                        mm = pe.matmul(ps_h[:, k % 2, half, :], rows_t[:, k % 2, ch, :],
                                       w1[:, ch, bass.ds(e, 1), half * S:half * S + S].rearrange("p a n -> p (a n)"),
                                       start=ch == 0, stop=ch == DC - 1)
                mm.then_inc(h_mm, 1)

            def turn_hidden(it, k):
                pe.wait_ge(hid_ok, it * 2 + (k + 3))
                for j in range(HC):
                    mm = pe.transpose(ps_ht[:, j * P:j * P + P], hid[:, k % 2, j * P:(j + 1) * P], c.ident[:, :])
                mm.then_inc(ht_mm, 1)

            def second(it, k, e):
                pe.wait_ge(ht_out, it * 2 + (k + 1))
                pe.wait_ge(y_ok, it * 2 + (k + 1))
                for j in range(HC):
                    mm = pe.matmul(ps_y[:, 0:D], hid_t[:, k % 2, j, :],
                                   w2[:, j, bass.ds(e, 1), :].rearrange("p a n -> p (a n)"),
                                   start=j == 0, stop=j == HC - 1)
                mm.then_inc(y_mm, 1)

            def slot(it, k, e, more, more2):
                turn_hidden(it, k)
                if more:
                    first(it, k + 1, e[k + 1])
                if more2:
                    turn_rows(it, k + 2)
                second(it, k, e[k])

            used = used_tiles(pe)
            turn_rows(0, 0)
            turn_rows(0, 1)
            pe.wait_ge(c.fetched, 16 * c.fetches)
            first(0, 0, owner(0, 0))
            with pe.Fori(0, SURE_TILES // 2, UNROLL // 2) as it:
                e = [owner(it, k) for k in range(UNROLL + 1)]
                for k in range(UNROLL):
                    slot(it, k, e, True, True)
            with pe.Fori(SURE_TILES // 2, TILES // 2 - 1) as it:
                e = [owner(it, k) for k in range(3)]
                for k in range(2):
                    with pe.If(used > it * 2 + k):
                        slot(it, k, e, True, True)
            e = [owner(TILES // 2 - 1, k) for k in range(2)]
            for k in range(2):
                with pe.If(used > TILES - 2 + k):
                    slot(TILES // 2 - 1, k, e, k == 0, False)

        @block.scalar
        def _(act):
            def rows_copy(it, k):
                act.wait_ge(x_mm, it * 2 + (k + 1))
                if not (isinstance(it, int) and it * 2 + k < 2):
                    act.wait_ge(h_mm, it * 2 + (k - 1))
                act.activation(rows_t[:, k % 2, :, :], ps_x[:, 0:DC * P].rearrange("p (c t) -> p c t", c=DC),
                               ACT.Copy).then_inc(x_out, 1)

            def gate(it, k):
                act.wait_ge(h_mm, it * 2 + (k + 1))
                act.wait_ge(hid_ok, it * 2 + (k + 1))
                act.activation(act_gate[:, k % 2, :], ps_h[:, k % 2, 0, :], ACT.Silu).then_inc(gate_ok, 1)

            def hidden_copy(it, k):
                act.wait_ge(ht_mm, it * 2 + (k + 1))
                act.wait_ge(y_mm, it * 2 + (k + 1))
                act.activation(hid_t[:, k % 2, :, :], ps_ht[:, :].rearrange("p (c t) -> p c t", c=HC),
                               ACT.Copy).then_inc(ht_out, 1)

            def slot(it, k, more, more2):
                hidden_copy(it, k)
                if more:
                    gate(it, k + 1)
                if more2:
                    rows_copy(it, k + 2)

            act.sem_inc(x_out, 1)
            act.sem_inc(y_mm, 2)
            used = used_tiles(act)
            rows_copy(0, 0)
            rows_copy(0, 1)
            gate(0, 0)
            with act.Fori(0, SURE_TILES // 2, UNROLL // 2) as it:
                for k in range(UNROLL):
                    slot(it, k, True, True)
            with act.Fori(SURE_TILES // 2, TILES // 2 - 1) as it:
                for k in range(2):
                    with act.If(used > it * 2 + k):
                        slot(it, k, True, True)
            for k in range(2):
                with act.If(used > TILES - 2 + k):
                    slot(TILES // 2 - 1, k, k == 0, False)

        @block.vector
        def _(dve):
            def combine(it, k):
                dve.wait_ge(h_mm, it * 2 + (k + 1))
                dve.wait_ge(gate_ok, it * 2 + (k + 1))
                if not (isinstance(it, int) and it * 2 + k < 2):
                    dve.wait_ge(ht_mm, it * 2 + (k - 1))
                dve.tensor_tensor(hid[:, k % 2, :], act_gate[:, k % 2, :], ps_h[:, k % 2, 1, :], ALU.mult
                                  ).then_inc(hid_ok, 1)

            def y_copy(it, k):
                dve.wait_ge(y_mm, it * 2 + (k + 3))
                dve.wait_ge(y_sent[k % 2], it * 16 + 16 * (k // 2 + 1))
                dve.tensor_copy(y[:, k % 2, :], ps_y[:, 0:D]).then_inc(y_ok, 1)

            def slot(it, k, more):
                if more:
                    combine(it, k + 1)
                y_copy(it, k)

            used = used_tiles(dve)
            dve.sem_inc(hid_ok, 2)
            dve.sem_inc(y_ok, 1)
            combine(0, 0)
            with dve.Fori(0, SURE_TILES // 2, UNROLL // 2) as it:
                for k in range(UNROLL):
                    slot(it, k, True)
            with dve.Fori(SURE_TILES // 2, TILES // 2 - 1) as it:
                for k in range(2):
                    with dve.If(used > it * 2 + k):
                        slot(it, k, True)
            for k in range(2):
                with dve.If(used > TILES - 2 + k):
                    slot(TILES // 2 - 1, k, k == 0)


def run_selu_experts(c, tag, w_in_dram, b_in_dram, w_out_dram, b_out_dram):
    nc = c.nc
    HC = HIDDEN // P
    with c.stage() as st:
        w1 = c.sbuf(st, f"{tag}_w1", [P, DC, E, HIDDEN], F32)
        w2 = c.sbuf(st, f"{tag}_w2", [P, HC, E, D], F32)
        b1 = c.sbuf(st, f"{tag}_b1", [P, HC, E], F32)
        b2 = c.sbuf(st, f"{tag}_b2", [P, E, D], F32)
        shift = c.sbuf(st, f"{tag}_shift", [P, 1], F32)
        rows = c.sbuf(st, f"{tag}_rows", [P, 2, D], F32)
        rows_t = c.sbuf(st, f"{tag}_rows_t", [P, 2, DC, P], F32)
        hid = c.sbuf(st, f"{tag}_hid", [P, 2, S], F32)
        pre = c.sbuf(st, f"{tag}_pre", [P, 2, S], F32)
        low = c.sbuf(st, f"{tag}_low", [P, 2, S], F32)
        grown = c.sbuf(st, f"{tag}_grown", [P, 2, S], F32)
        high = c.sbuf(st, f"{tag}_high", [P, 2, S], F32)
        hid_t = c.sbuf(st, f"{tag}_hid_t", [P, 2, S], F32)
        y = c.sbuf(st, f"{tag}_y", [P, 2, D], F32)
        ps_x = c.psum(st, f"{tag}_ps_x", [P, S])
        ps_h = c.psum(st, f"{tag}_ps_h", [P, 2, S])
        ps_ht = c.psum(st, f"{tag}_ps_ht", [P, 2, S])
        ps_y = c.psum(st, f"{tag}_ps_y", [P, S])
        w_in = c.sem(st, f"{tag}_ew_in")
        rows_in = [c.sem(st, f"{tag}_rows_in{i}") for i in range(2)]
        x_mm = c.sem(st, f"{tag}_x_mm")
        x_out = c.sem(st, f"{tag}_x_out")
        h_mm = c.sem(st, f"{tag}_h_mm")
        hid_ok = c.sem(st, f"{tag}_hid_ok")
        ht_mm = c.sem(st, f"{tag}_ht_mm")
        pre_ok = c.sem(st, f"{tag}_pre_ok")
        low_ok = c.sem(st, f"{tag}_low_ok")
        grown_ok = c.sem(st, f"{tag}_grown_ok")
        high_ok = c.sem(st, f"{tag}_high_ok")
        shift_ok = c.sem(st, f"{tag}_shift_ok")
        selu_ok = c.sem(st, f"{tag}_selu_ok")
        y_mm = c.sem(st, f"{tag}_y_mm")
        y_ok = c.sem(st, f"{tag}_y_ok")
        y_sent = [c.sem(st, f"{tag}_y_sent{i}") for i in range(2)]
        block = st.enter_context(nc.Block())

        def parts(it, k, part, more):
            return it * 4 + (2 * k + part + more)

        def used_tiles(eng):
            return eng.value_load(c.used[0:1, 0:1], min_val=0, max_val=TILES)

        @block.sync
        def _(sp):
            def load_rows(i):
                sp.dma_start(rows[:, i % 2, :], c.xs[tag][i * P:(i + 1) * P, :]).then_inc(rows_in[i % 2], 16)

            used = used_tiles(sp)
            with sp.If(used > 0):
                for i in range(2):
                    sp.sem_inc(y_sent[i], 16)
                    load_rows(i)
                for ch in range(DC):
                    sp.dma_start(w1[:, ch, :, :], w_in_dram[:, ch]).then_inc(w_in, 16)
                sp.dma_start(w2[:, :, :, :], w_out_dram).then_inc(w_in, 16)
                sp.dma_start(b1[:, :, :], b_in_dram).then_inc(w_in, 16)
                sp.dma_start(b2[:, :, :], b_out_dram.partition_broadcast(P)).then_inc(w_in, 16)
                lag = 3
                for i in range(TILES + lag):
                    if 2 <= i < TILES:
                        with sp.If(used > i - 2):
                            sp.wait_ge(x_mm, i - 1)
                            load_rows(i)
                    j = i - lag
                    if j >= 0:
                        with sp.If(used > j):
                            sp.wait_ge(y_ok, j + 2)
                            sp.dma_start(c.ys[tag][j * P:(j + 1) * P, :], y[:, j % 2, :]).then_inc(y_sent[j % 2], 16)
                        with sp.Else():
                            sp.dma_start(c.ys[tag][j * P:(j + 1) * P, :], c.zeros[:, 0, :]).then_inc(y_sent[j % 2], 16)
                for i in range(2):
                    sp.wait_ge(y_sent[i], 16 + 16 * (TILES // 2))

        @block.tensor
        def _(pe):
            def turn_rows(it, k):
                pe.wait_ge(rows_in[k % 2], it * 16 + 16 * (k // 2 + 1))
                pe.wait_ge(x_out, it * 2 + (k + 1))
                for ch in range(DC):
                    mm = pe.transpose(ps_x[:, ch * P:ch * P + P], rows[:, k % 2, ch * P:ch * P + P], c.ident[:, :])
                mm.then_inc(x_mm, 1)

            def first(it, k):
                e = pe.value_load(c.owner[0:1, bass.ds(it * 2 + k, 1)], min_val=0, max_val=E - 1)
                pe.wait_ge(x_out, it * 2 + (k + 2))
                for part in range(2):
                    pe.wait_ge(hid_ok, parts(it, k, part, 1))
                    for ch in range(DC):
                        mm = pe.matmul(ps_h[:, part, :], rows_t[:, k % 2, ch, :],
                                       w1[:, ch, bass.ds(e, 1), part * S:part * S + S].rearrange("p a n -> p (a n)"),
                                       start=ch == 0, stop=ch == DC - 1)
                    mm.then_inc(h_mm, 1)

            def turn_hidden(it, k):
                for part in range(2):
                    pe.wait_ge(hid_ok, parts(it, k, part, 3))
                    pe.wait_ge(pre_ok, parts(it, k, part, 1))
                    for j in range(S // P):
                        mm = pe.transpose(ps_ht[:, part, j * P:j * P + P], hid[:, part, j * P:j * P + P],
                                          c.ident[:, :])
                    mm.then_inc(ht_mm, 1)

            def second(it, k):
                e = pe.value_load(c.owner[0:1, bass.ds(it * 2 + k, 1)], min_val=0, max_val=E - 1)
                pe.wait_ge(y_ok, it * 2 + (k + 1))
                for part in range(2):
                    pe.wait_ge(selu_ok, parts(it, k, part, 3))
                    for j in range(S // P):
                        kk = part * (S // P) + j
                        mm = pe.matmul(ps_y[:, 0:D], hid_t[:, part, j * P:j * P + P],
                                       w2[:, kk, bass.ds(e, 1), :].rearrange("p a n -> p (a n)"),
                                       start=kk == 0, stop=kk == HC - 1)
                mm.then_inc(y_mm, 1)

            def slot(it, k, more, more2):
                turn_hidden(it, k)
                if more:
                    first(it, k + 1)
                if more2:
                    turn_rows(it, k + 2)
                second(it, k)

            used = used_tiles(pe)
            with pe.If(used > 0):
                turn_rows(0, 0)
                turn_rows(0, 1)
                pe.wait_ge(w_in, 16 * (DC + 3))
                first(0, 0)
                with pe.Fori(0, TILES // 2 - 1) as it:
                    for k in range(2):
                        with pe.If(used > it * 2 + k):
                            slot(it, k, True, True)
                for k in range(2):
                    with pe.If(used > TILES - 2 + k):
                        slot(TILES // 2 - 1, k, k == 0, False)

        @block.scalar
        def _(act):
            def rows_copy(it, k):
                act.wait_ge(x_mm, it * 2 + (k + 1))
                if not (isinstance(it, int) and it * 2 + k < 2):
                    act.wait_ge(h_mm, it * 4 + (2 * k - 2))
                act.activation(rows_t[:, k % 2, :, :], ps_x[:, 0:DC * P].rearrange("p (c t) -> p c t", c=DC),
                               ACT.Copy).then_inc(x_out, 1)

            def hidden_copy(it, k):
                for part in range(2):
                    act.wait_ge(h_mm, parts(it, k, part, 1))
                    act.wait_ge(ht_mm, parts(it, k, part, 1))
                    act.activation(hid[:, part, :], ps_h[:, part, :], ACT.Copy).then_inc(hid_ok, 1)

            def grow(it, k):
                for part in range(2):
                    act.wait_ge(low_ok, parts(it, k, part, 3))
                    act.wait_ge(selu_ok, parts(it, k, part, 1))
                    act.activation(grown[:, part, :], low[:, part, :], ACT.Exp, bias=shift[:, 0:1]
                                   ).then_inc(grown_ok, 1)

            def slot(it, k, more, more2):
                grow(it, k)
                if more:
                    hidden_copy(it, k + 1)
                if more2:
                    rows_copy(it, k + 2)

            used = used_tiles(act)
            with act.If(used > 0):
                act.sem_inc(x_out, 1)
                act.sem_inc(hid_ok, 2)
                act.sem_inc(grown_ok, 2)
                rows_copy(0, 0)
                rows_copy(0, 1)
                hidden_copy(0, 0)
                with act.Fori(0, TILES // 2 - 1) as it:
                    for k in range(2):
                        with act.If(used > it * 2 + k):
                            slot(it, k, True, True)
                for k in range(2):
                    with act.If(used > TILES - 2 + k):
                        slot(TILES // 2 - 1, k, k == 0, False)

        @block.gpsimd
        def _(pool):
            used = used_tiles(pool)
            with pool.If(used > 0):
                pool.sem_inc(low_ok, 2)
                with pool.Fori(0, TILES // 2) as it:
                    for k in range(2):
                        with pool.If(used > it * 2 + k):
                            for part in range(2):
                                pool.wait_ge(pre_ok, parts(it, k, part, 3))
                                pool.wait_ge(grown_ok, parts(it, k, part, 1))
                                pool.nop(nofuse=True)
                                pool.tensor_scalar(low[:, part, :], pre[:, part, :], 0.0, None, ALU.min
                                                   ).then_inc(low_ok, 1)

        @block.vector
        def _(dve):
            S_P = S // P

            def before_second(it, k):
                e = dve.value_load(c.owner[0:1, bass.ds(it * 2 + k, 1)], min_val=0, max_val=E - 1)
                for part in range(2):
                    dve.wait_ge(ht_mm, parts(it, k, part, 3))
                    dve.wait_ge(low_ok, parts(it, k, part, 1))
                    dve.wait_ge(high_ok, parts(it, k, part, 1))
                    dve.tensor_tensor(
                        pre[:, part, :].rearrange("p (j t) -> p j t", t=P),
                        ps_ht[:, part, :].rearrange("p (j t) -> p j t", t=P),
                        b1[:, part * S_P:part * S_P + S_P, bass.ds(e, 1)].broadcast_to([P, S_P, P]),
                        ALU.add).then_inc(pre_ok, 1)
                for part in range(2):
                    dve.wait_ge(pre_ok, parts(it, k, part, 3))
                    dve.wait_ge(selu_ok, parts(it, k, part, 1))
                    dve.tensor_scalar(high[:, part, :], pre[:, part, :], 0.0, -SELU_ALPHA, ALU.max, ALU.add
                                      ).then_inc(high_ok, 1)
                for part in range(2):
                    dve.wait_ge(grown_ok, parts(it, k, part, 3))
                    dve.wait_ge(high_ok, parts(it, k, part, 3))
                    dve.wait_ge(y_mm, it * 2 + (k + 1))
                    dve.tensor_tensor(hid_t[:, part, :], high[:, part, :], grown[:, part, :], ALU.add
                                      ).then_inc(selu_ok, 1)

            def y_copy(it, k):
                e = dve.value_load(c.owner[0:1, bass.ds(it * 2 + k, 1)], min_val=0, max_val=E - 1)
                dve.wait_ge(y_mm, it * 2 + (k + 2))
                dve.wait_ge(y_sent[k % 2], it * 16 + 16 * (k // 2 + 1))
                dve.scalar_tensor_tensor(out=y[:, k % 2, :], in0=ps_y[:, 0:D], scalar=SELU_SCALE,
                                         in1=b2[:, bass.ds(e, 1), :].rearrange("p a n -> p (a n)"),
                                         op0=ALU.mult, op1=ALU.add).then_inc(y_ok, 1)

            used = used_tiles(dve)
            with dve.If(used > 0):
                dve.sem_inc(ht_mm, 2)
                dve.sem_inc(pre_ok, 2)
                dve.sem_inc(high_ok, 2)
                dve.sem_inc(selu_ok, 2)
                dve.sem_inc(y_mm, 1)
                dve.sem_inc(y_ok, 1)
                dve.memset(shift[:, :], float(np.log(SELU_ALPHA))).then_inc(shift_ok, 1)
                dve.wait_ge(shift_ok, 1)
                dve.wait_ge(w_in, 16 * (DC + 3))
                with dve.Fori(0, TILES // 2) as it:
                    for k in range(2):
                        with dve.If(used > it * 2 + k):
                            before_second(it, k)
                            y_copy(it, k)


def gather_experts(c, tag, weight, all_have, out=None):
    nc = c.nc
    n_all = NT + 1
    groups = [range(b * NQ, b * NQ + NQ) for b in range(B)] + [range(NT, n_all)]
    with c.stage() as st:
        got = c.sbuf(st, f"{tag}_got", [P, 2, n_all, D], F32)
        clear = c.sem(st, f"{tag}_clear")
        got_in = [c.sem(st, f"{tag}_got_in{i}") for i in range(len(groups))]
        added = c.sem(st, f"{tag}_added")
        stored = c.sem(st, f"{tag}_stored")
        block = st.enter_context(nc.Block())
        cleared = slice(NT if all_have else 0, n_all)

        @block.gpsimd
        def _(pool):
            used = pool.value_load(c.used[0:1, 0:1], min_val=0, max_val=TILES)
            pool.memset(got[:, 1, cleared, :], 0.0).then_inc(clear, 1)
            pool.wait_ge(clear, 2)
            with pool.If(used > 0):
                for tiles, sem in zip(groups, got_in):
                    for n in tiles:
                        for k in range(2):
                            pool.indirect_dma_start(
                                out=got[:, k, n, :], out_offset=None, in_=c.ys[tag][:, :],
                                in_offset=bass.IndirectOffsetOnAxis(ap=c.row[:, k, n:n + 1], axis=0),
                                bounds_check=TILES * P - 1, oob_is_err=False).then_inc(sem, 16)
            with pool.Else():
                for tiles, sem in zip(groups, got_in):
                    pool.sem_inc(sem, 16 * 2 * len(tiles))

        @block.vector
        def _(dve):
            dve.memset(got[:, 0, cleared, :], 0.0).then_inc(clear, 1)
            dve.wait_ge(clear, 2)
            done = 0
            for tiles, sem in zip(groups, got_in):
                dve.wait_ge(sem, 16 * 2 * len(tiles))
                for k in range(2):
                    if k:
                        dve.wait_ge(added, done)
                    for n in tiles:
                        dve.scalar_tensor_tensor(out=c.h[:, n, :], in0=got[:, k, n, :], scalar=weight[:, k, n:n + 1],
                                                 in1=c.h[:, n, :], op0=ALU.mult, op1=ALU.add).then_inc(added, 1)
                        done += 1

        @block.sync
        def _(sp):
            if out is not None:
                for b in range(B):
                    sp.wait_ge(added, 2 * NQ * (b + 1))
                    sp.dma_start(out[b, 1:, :].rearrange("(n p) d -> p n d", p=P),
                                 c.h[:, b * NQ:b * NQ + NQ, :]).then_inc(stored, 16)
                sp.wait_ge(added, 2 * n_all)
                sp.dma_start(out[:, 0, :], c.h[0:B, NT, :]).then_inc(stored, 16)
                sp.wait_ge(stored, 16 * (B + 1))


def route_moe(c, tag, router_dram, idx, weight):
    nc = c.nc
    n_all = NT + 1
    with c.stage() as st:
        router = c.sbuf(st, f"{tag}_router", [P, DC, E], F32)
        logits = c.sbuf(st, f"{tag}_logits", [P, n_all, E], F32)
        top = c.sbuf(st, f"{tag}_top8", [P, n_all, 8], F32)
        top_at = c.sbuf(st, f"{tag}_top8_at", [P, n_all, 8], U32)
        gap = c.sbuf(st, f"{tag}_gap", [P, n_all], F32)
        ratio = c.sbuf(st, f"{tag}_ratio", [P, n_all], F32)
        one_more = c.sbuf(st, f"{tag}_one_more", [P, n_all], F32)
        ps_l = c.psum(st, f"{tag}_ps_l", [P, S])
        r_in = c.sem(st, f"{tag}_r_in")
        l_mm = c.sem(st, f"{tag}_l_mm")
        l_ok = c.sem(st, f"{tag}_l_ok")
        top_ok = c.sem(st, f"{tag}_top_ok")
        at_ok = c.sem(st, f"{tag}_at_ok")
        gap_ok = c.sem(st, f"{tag}_gap_ok")
        ratio_ok = c.sem(st, f"{tag}_ratio_ok")
        chain = c.sem(st, f"{tag}_r_chain")
        block = st.enter_context(nc.Block())

        @block.sync
        def _(sp):
            sp.dma_start(router[:, :, :], router_dram).then_inc(r_in, 16)

        @block.tensor
        def _(pe):
            pe.wait_ge(r_in, 16)
            for n in range(n_all):
                r = P if n < NT else B
                for ch in range(DC):
                    lhs = (c.xt[:, ch, n // NQ, 1 + n % NQ * P:1 + n % NQ * P + P] if n < NT else c.xt[:, ch, :, 0])
                    mm = pe.matmul(ps_l[0:r, n * E:n * E + E], lhs, router[:, ch, :], start=ch == 0, stop=ch == DC - 1)
            mm.then_inc(l_mm, 1)

        @block.vector
        def _(dve):
            dve.memset(logits[:, NT, :], 0.0).then_inc(l_ok, 1)
            dve.wait_ge(l_mm, 1)
            dve.wait_ge(l_ok, 1)
            dve.tensor_copy(logits[:, 0:NT, :], ps_l[:, 0:NT * E].rearrange("p (n e) -> p n e", e=E)).then_inc(l_ok, 1)
            dve.tensor_copy(logits[0:B, NT, :], ps_l[0:B, NT * E:n_all * E]).then_inc(l_ok, 1)
            dve.wait_ge(l_ok, 3)
            for n in range(n_all):
                dve.max(top[:, n, :], logits[:, n, :]).then_inc(top_ok, 1)
            for n in range(n_all):
                dve.wait_ge(top_ok, n + 1)
                dve.max_index(top_at[:, n, :], top[:, n, :], logits[:, n, :]).then_inc(at_ok, 1)
            dve.tensor_tensor(gap[:, :], top[:, :, 1], top[:, :, 0], ALU.subtract).then_inc(gap_ok, 1)
            dve.wait_ge(at_ok, n_all)
            dve.tensor_copy(idx[:, :, :], top_at[:, :, 0:2]).then_inc(chain, 1)
            dve.wait_ge(ratio_ok, 1)
            dve.tensor_scalar(one_more[:, :], ratio[:, :], 1.0, None, ALU.add).then_inc(chain, 1)
            dve.wait_ge(chain, 2)
            dve.reciprocal(weight[:, 0, :], one_more[:, :]).then_inc(chain, 1)
            dve.wait_ge(chain, 3)
            dve.tensor_tensor(weight[:, 1, :], ratio[:, :], weight[:, 0, :], ALU.mult).then_inc(chain, 1)

        @block.scalar
        def _(act):
            act.wait_ge(gap_ok, 1)
            act.activation(ratio[:, :], gap[:, :], ACT.Exp).then_inc(ratio_ok, 1)


def route_last(c, tag, wi, bi, wo, bo, idx, weight):
    nc = c.nc
    HC = HIDDEN // P
    n_all = NT + 1
    with c.stage() as st:
        shift = c.sbuf(st, f"{tag}_gshift", [P, 1], F32)
        low = c.sbuf(st, f"{tag}_glow", [P, 2, S], F32)
        grown = c.sbuf(st, f"{tag}_ggrown", [P, 2, S], F32)
        high = c.sbuf(st, f"{tag}_ghigh", [P, 2, S], F32)
        hid = c.sbuf(st, f"{tag}_ghid", [P, 2, S], F32)
        logits = c.sbuf(st, f"{tag}_glogits", [P, NQ, D], F32)
        top = c.sbuf(st, f"{tag}_gtop", [P, NQ, 8], F32)
        top_at = c.sbuf(st, f"{tag}_gtop_at", [P, NQ, 8], U32)
        two = c.sbuf(st, f"{tag}_gtwo", [P, 2, n_all], F32)
        sums = c.sbuf(st, f"{tag}_gsums", [P, n_all], F32)
        ps_h = c.psum(st, f"{tag}_gps_h", [P, 2, S])
        ps_l = c.psum(st, f"{tag}_gps_l", [P, NQ, S])
        ready = c.sem(st, f"{tag}_gready")
        h_mm = c.sem(st, f"{tag}_gh_mm")
        low_ok = c.sem(st, f"{tag}_glow_ok")
        high_ok = c.sem(st, f"{tag}_ghigh_ok")
        grown_ok = c.sem(st, f"{tag}_ggrown_ok")
        hid_ok = c.sem(st, f"{tag}_ghid_ok")
        l_mm = c.sem(st, f"{tag}_gl_mm")
        l_ok = c.sem(st, f"{tag}_gl_ok")
        top_ok = c.sem(st, f"{tag}_gtop_ok")
        at_ok = c.sem(st, f"{tag}_gat_ok")
        kept = c.sem(st, f"{tag}_gkept")
        block = st.enter_context(nc.Block())

        @block.tensor
        def _(pe):
            def hidden(b, f, wide):
                pe.wait_ge(high_ok, b * HC + (f + 1))
                for ch in range(DC):
                    src = (c.xt[:, ch, bass.ds(b, 1), 1:].rearrange("p a t -> p (a t)") if wide == S
                           else c.xt[:, ch, :, 0])
                    mm = pe.matmul(ps_h[:, f % 2, 0:wide], wi[:, ch, f * P:f * P + P], src,
                                   start=ch == 0, stop=ch == DC - 1)
                mm.then_inc(h_mm, 1)

            def add_logits(b, f, wide):
                pe.wait_ge(hid_ok, b * HC + (f + 3))
                for n in range(NQ if wide == S else 1):
                    if f == 0:
                        pe.wait_ge(l_ok, b * NQ + (n + 1))
                    r = min(wide, P)
                    mm = pe.matmul(ps_l[0:r, n, 0:D], hid[:, f % 2, n * P:n * P + r], wo[:, f, :],
                                   start=f == 0, stop=f == HC - 1)
                mm.then_inc(l_mm, 1)

            def image(b, wide, following):
                for f in range(HC):
                    if f + 1 < HC:
                        hidden(b, f + 1, wide)
                    elif following:
                        hidden(b + 1, 0, following)
                    add_logits(b, f, wide)

            pe.wait_ge(c.fetched, 16 * c.fetches)
            hidden(0, 0, S)
            with pe.Fori(0, B - 1) as b:
                image(b, S, S)
            image(B - 1, S, B)
            image(B, B, 0)

        @block.scalar
        def _(act):
            def image(b, wide):
                for f in range(HC):
                    act.wait_ge(low_ok, b * HC + (f + 1))
                    act.wait_ge(hid_ok, b * HC + (f + 1))
                    act.activation(high[:, f % 2, 0:wide], ps_h[:, f % 2, 0:wide], ACT.Relu, bias=bi[:, f:f + 1]
                                   ).then_inc(high_ok, 1)
                    act.activation(grown[:, f % 2, 0:wide], low[:, f % 2, 0:wide], ACT.Exp, bias=shift[:, 0:1]
                                   ).then_inc(grown_ok, 1)

            act.sem_inc(high_ok, 2)
            act.sem_inc(grown_ok, 2)
            with act.Fori(0, B) as b:
                image(b, S)
            image(B, B)

        @block.vector
        def _(dve):
            def search(b, f, tiles=NQ):
                n = f % NQ
                if n >= tiles:
                    return
                if f < NQ:
                    dve.wait_ge(l_ok, b * NQ + (NQ + n + 1))
                    dve.wait_ge(kept, 2 * b + 2)
                    dve.nop(nofuse=True)
                    dve.max(top[:, n, :], logits[:, n, :]).then_inc(top_ok, 1)
                else:
                    dve.wait_ge(top_ok, b * NQ + (n + 1))
                    dve.nop(nofuse=True)
                    dve.max_index(top_at[:, n, :], top[:, n, :], logits[:, n, :]).then_inc(at_ok, 1)

            def keep(b, tiles=NQ):
                dve.wait_ge(at_ok, b * NQ + (NQ + tiles))
                where = bass.ds(b * NQ, tiles)
                dve.tensor_copy(two[:, :, where].rearrange("p k n -> p n k"), top[:, 0:tiles, 0:2]).then_inc(kept, 1)
                dve.tensor_copy(idx[:, where, :], top_at[:, 0:tiles, 0:2]).then_inc(kept, 1)

            def image(b, wide, before):
                for f in range(HC):
                    dve.wait_ge(h_mm, b * HC + (f + 1))
                    dve.wait_ge(grown_ok, b * HC + (f + 1))
                    dve.tensor_scalar(low[:, f % 2, 0:wide], ps_h[:, f % 2, 0:wide], bi[:, f:f + 1], 0.0,
                                      ALU.add, ALU.min).then_inc(low_ok, 1)
                    if before:
                        search(b - 1, f)
                    dve.wait_ge(high_ok, b * HC + (f + 3))
                    dve.wait_ge(grown_ok, b * HC + (f + 3))
                    dve.wait_ge(l_mm, b * HC + (f + 1))
                    dve.scalar_tensor_tensor(out=hid[:, f % 2, 0:wide], in0=grown[:, f % 2, 0:wide],
                                             scalar=-SELU_ALPHA, in1=high[:, f % 2, 0:wide],
                                             op0=ALU.add, op1=ALU.add).then_inc(hid_ok, 1)
                if before:
                    keep(b - 1)
                tiles = NQ if wide == S else 1
                r = min(wide, P)
                if wide < S:
                    dve.memset(logits[:, 0, :], 1.0).then_inc(ready, 1)
                    dve.wait_ge(ready, 2)
                dve.wait_ge(l_mm, b * HC + (HC + 2))
                for n in range(tiles):
                    dve.scalar_tensor_tensor(out=logits[0:r, n, :], in0=ps_l[0:r, n, 0:D], scalar=SELU_SCALE,
                                             in1=bo[0:r, :], op0=ALU.mult, op1=ALU.add).then_inc(l_ok, 1)

            dve.sem_inc(hid_ok, 2)
            dve.sem_inc(l_mm, 2)
            dve.sem_inc(l_ok, NQ)
            dve.sem_inc(at_ok, NQ)
            dve.sem_inc(kept, 2)
            dve.memset(shift[:, :], float(np.log(SELU_ALPHA))).then_inc(ready, 1)
            dve.wait_ge(ready, 1)
            dve.wait_ge(c.fetched, 16 * c.fetches)
            image(0, S, False)
            with dve.Fori(1, B) as b:
                image(b, S, True)
            image(B, B, True)
            for f in (0, NQ):
                search(B, f, 1)
            keep(B, 1)
            dve.wait_ge(kept, 2 * B + 4)
            dve.tensor_tensor(sums[:, :], two[:, 0, :], two[:, 1, :], ALU.add).then_inc(ready, 1)
            dve.wait_ge(ready, 3)
            dve.reciprocal(sums[:, :], sums[:, :]).then_inc(ready, 1)
            dve.wait_ge(ready, 4)
            dve.tensor_tensor(weight[:, :, :], two[:, :, :],
                              sums[:, :].rearrange("p (a n) -> p a n", a=1).broadcast_to([P, 2, n_all]), ALU.mult
                              ).then_inc(ready, 1)


def load_patches(c, x_t, cls, fetch):
    with c.stage() as st:
        x_in = c.sem(st, "x_in")
        cleared = c.sem(st, "cleared")
        with c.nc.Block() as block:
            @block.sync
            def _(sp):
                for ch in range(DC):
                    sp.dma_start(c.xt[:, ch, :, 1:], x_t[:, ch]).then_inc(x_in, 16)
                c.fetch(sp, fetch)
                sp.wait_ge(cleared, 1)
                sp.dma_start(c.h[0:B, NT, :], cls.partition_broadcast(B)).then_inc(x_in, 16)
                sp.wait_ge(x_in, 16 * (DC + 1))

            @block.gpsimd
            def _(pool):
                pool.memset(c.h[:, NT, :], 0.0).then_inc(cleared, 1)


def norm(c, tag, fetch):
    nc = c.nc
    with c.stage() as st:
        stats = c.sbuf(st, f"{tag}_stats", [P, NT + 1, 6], F32)
        mv = c.sbuf(st, f"{tag}_mv", [P, NT + 1, 2], F32)
        rstd = c.sbuf(st, f"{tag}_rstd", [P, NT + 1], F32)
        eps = c.sbuf(st, f"{tag}_eps", [P, 1], F32)
        xn = c.sbuf(st, f"{tag}_xn", [P, NT + 1, D], F32)
        ps_t = c.psum(st, f"{tag}_ps_xt", [P, 2, S])
        stat_ok = c.sem(st, f"{tag}_stat_ok")
        aggr_ok = c.sem(st, f"{tag}_aggr_ok")
        eps_ok = c.sem(st, f"{tag}_eps_ok")
        std_ok = c.sem(st, f"{tag}_std_ok")
        rstd_ok = c.sem(st, f"{tag}_rstd_ok")
        xn_ok = c.sem(st, f"{tag}_xn_ok")
        t_mm = c.sem(st, f"{tag}_xt_mm")
        t_out = c.sem(st, f"{tag}_xt_out")
        block = st.enter_context(nc.Block())

        @block.sync
        def _(sp):
            c.fetch(sp, fetch)

        @block.vector
        def _(dve):
            dve.memset(eps[:, :], EPS).then_inc(eps_ok, 1)
            for n in range(NT + 1):
                dve.bn_stats(stats[:, n, :], c.h[:, n, :]).then_inc(stat_ok, 1)
            for n in range(NT + 1):
                dve.wait_ge(stat_ok, n + 1)
                dve.bn_aggr(mv[:, n, :], stats[:, n, :]).then_inc(aggr_ok, 1)
            dve.wait_ge(std_ok, 1)
            dve.reciprocal(rstd[:, :], rstd[:, :]).then_inc(rstd_ok, 1)
            dve.wait_ge(rstd_ok, 1)
            dve.wait_ge(aggr_ok, NT + 1)
            for n in range(NT + 1):
                dve.tensor_scalar(xn[:, n, :], c.h[:, n, :], mv[:, n, 0:1], rstd[:, n:n + 1],
                                  ALU.subtract, ALU.mult).then_inc(xn_ok, 1)

        @block.tensor
        def _(pe):
            for n in range(NT + 1):
                pe.wait_ge(xn_ok, n + 1)
                if n >= 2:
                    pe.wait_ge(t_out, n - 1)
                r = P if n < NT else B
                for ch in range(DC):
                    mm = pe.transpose(ps_t[:, n % 2, ch * P:ch * P + r], xn[0:r, n, ch * P:ch * P + P],
                                      c.ident[0:r, 0:r])
                mm.then_inc(t_mm, 1)

        @block.scalar
        def _(act):
            act.wait_ge(aggr_ok, NT + 1)
            act.wait_ge(eps_ok, 1)
            act.activation(rstd[:, :], mv[:, :, 1], ACT.Sqrt, bias=eps[:, 0:1]).then_inc(std_ok, 1)
            for n in range(NT + 1):
                act.wait_ge(t_mm, n + 1)
                src = ps_t[:, n % 2, 0:DC * P].rearrange("p (c t) -> p c t", c=DC)
                if n < NT:
                    at = 1 + (n % NQ) * P
                    act.activation(c.xt[:, :, n // NQ, at:at + P], src, ACT.Copy).then_inc(t_out, 1)
                else:
                    act.activation(c.xt[:, :, :, 0], src[:, :, 0:B], ACT.Copy).then_inc(t_out, 1)


def projection_buffers(c, stack, a, tag):
    w, qkb = a[f"{tag}_w"], a[f"{tag}_qkb"]
    buffers = (c.sbuf(stack, f"{tag}_w", list(w.shape), F32), c.sbuf(stack, f"{tag}_qkb", list(qkb.shape), F32),
               c.sbuf(stack, f"{tag}_vb", [P, D], F32))
    return buffers, [(buffers[0][:, :, :], w), (buffers[1][:, :, :], qkb),
                     (buffers[2][:, :], a[f"{tag}_vb"].partition_broadcast(P))]


def program(nc, a, out):
    with ExitStack() as stack:
        c = Chip(nc, stack)
        c.qd = nc.dram_tensor("q_parts", [B, SPLIT, HD, NH, S], BF16, kind="Internal").ap()
        c.kd = {w: nc.dram_tensor(f"k{w}_parts", [B, SPLIT, HD, NH, w], BF16, kind="Internal").ap()
                for w in (S, S + 1)}
        c.vd = nc.dram_tensor("v_rows", [B, G, P, NQ, P], F32, kind="Internal").ap()
        c.xs = {t: nc.dram_tensor(f"{t}_xs", [TILES * P, D], F32, kind="Internal").ap() for t in ("moe", "last")}
        c.ys = {t: nc.dram_tensor(f"{t}_ys", [TILES * P, D], F32, kind="Internal").ap() for t in ("moe", "last")}
        constants(c)
        c.h = c.sbuf(stack, "h", [P, NT + 1, D], F32)
        c.vcls = c.sbuf(stack, "vcls", [B, D], F32)
        c.row = c.sbuf(stack, "row", [P, 2, NT + 1], U32)
        c.owner = c.sbuf(stack, "owner", [P, TILES], I32)
        c.used = c.sbuf(stack, "used", [P, 1], I32)
        idx = c.sbuf(stack, "idx", [P, NT + 1, 2], F32)
        weight = c.sbuf(stack, "weight", [P, 2, NT + 1], F32)
        c.ctx = c.sbuf(stack, "ctx", [P, NT + 1, D], F32)
        with ExitStack() as wide:
            c.xt = c.sbuf(wide, "xt", [P, DC, B, S + 1], F32)
            w_tok, get_tok = projection_buffers(c, wide, a, "tok")
            w_rot, get_rot = projection_buffers(c, wide, a, "rot")
            tables = [c.sbuf(wide, f"rot_{name}", [P, 2, S], F32) for name in ("cos", "sin")]
            get_rot += [(t[:, h, :], a[name]) for t, name in zip(tables, ("cos", "sin")) for h in range(2)]
            load_patches(c, a["x_t"], a["cls"], get_tok)
            project(c, "tok", *w_tok, cls=False)
            attend(c, "tok", causal=False, clear=True, fetch=get_rot)
            attend_out(c, "tok", a["tok_wo"], a["tok_bo"], residual=False, cls=False)
            project(c, "rot", *w_rot, cls=True, rope=tables)
            attend(c, "rot", causal=True)
            w13 = c.sbuf(wide, "moe_w13", [P, DC, E, 2 * MOE_HIDDEN], F32)
            w2 = c.sbuf(wide, "moe_w2", [P, MOE_HIDDEN // P, E, D], F32)
            fetch = [(w13[:, ch], a["moe_w13"][:, ch]) for ch in range(DC)] + [(w2[:, :, :, :], a["moe_w2"])]
            attend_out(c, "rot", a["rot_wo"], a["rot_bo"], residual=True, cls=True, keep=c.ctx, fetch=fetch)
            route_moe(c, "moe", a["router"], idx, weight)
            dispatch(c, "moe", c.ctx, idx)
            run_gated_experts(c, "moe", w13, w2, MOE_HIDDEN)
        gather_experts(c, "moe", weight, all_have=True)
        with ExitStack() as wide:
            c.xt = c.sbuf(wide, "xt2", [P, DC, B, S + 1], F32)
            w_top, get_top = projection_buffers(c, wide, a, "top")
            norm(c, "mixed", get_top)
            project(c, "top", *w_top, cls=True)
            attend_top(c, "top")
            gate = (c.sbuf(wide, "gate_wi", [P, DC, HIDDEN], F32), c.sbuf(wide, "gate_bi", [P, HIDDEN // P], F32),
                    c.sbuf(wide, "gate_wo", [P, HIDDEN // P, D], F32), c.sbuf(wide, "gate_bo", [P, D], F32))
            fetch_gate = list(zip((t[:] for t in gate), (a["gate_wi"], a["gate_bi"], a["gate_wo"],
                                                         a["gate_bo"].partition_broadcast(P))))
            attend_out(c, "top", a["top_wo"], a["top_bo"], residual=True, cls=True, keep=c.ctx,
                       fetch=fetch_gate)
            route_last(c, "last", *gate, idx, weight)
        dispatch(c, "last", c.ctx, idx)
        run_selu_experts(c, "last", a["exp_wi"], a["exp_bi"], a["exp_wo"], a["exp_bo"])
        gather_experts(c, "last", weight, all_have=False, out=out)


_OUT = (B, S + 1, D)


def _split_rows(w):
    return np.ascontiguousarray(w.reshape(DC, P, -1).transpose(1, 0, 2))


def _columns(*vectors):
    return _split_rows(np.stack(vectors, axis=1))


def _swap_halves(w):
    return w.reshape(-1, NH, 2, HD // 2)[:, :, ::-1].reshape(w.shape)


def layout(inputs):
    i = {k: np.asarray(v) for k, v in inputs.items()}
    a = {}
    a["x_t"] = np.ascontiguousarray(i["x"].reshape(B, S, DC, P).transpose(3, 2, 0, 1))
    a["cls"] = i["cls_tok"].reshape(D)
    wt = i["L0_tok_w_qkv"].T.reshape(D, NH, 3, HD).transpose(0, 2, 1, 3).reshape(D, 3 * D)
    bt = i["L0_tok_b_qkv"].reshape(NH, 3, HD).transpose(1, 0, 2).reshape(3, D)
    a["tok_w"] = _split_rows(wt)
    a["tok_qkb"] = _columns(bt[0], bt[1])
    a["tok_vb"] = np.ascontiguousarray(bt[2])
    a["tok_wo"] = _split_rows(i["L0_tok_w_out"].T)
    a["tok_bo"] = i["L0_tok_b_out"]
    wq, wk, wv = (i[f"L0_attn_w{x}_w"] for x in "qkv")
    bq, bk = i["L0_attn_wq_b"], i["L0_attn_wk_b"]
    a["rot_w"] = _split_rows(np.concatenate([wq, wk, wv, _swap_halves(wq), _swap_halves(wk)], axis=1))
    a["rot_qkb"] = _columns(bq, bk, _swap_halves(bq[None])[0], _swap_halves(bk[None])[0])
    a["rot_vb"] = i["L0_attn_wv_b"]
    a["rot_wo"] = _split_rows(i["L0_attn_wo_w"])
    a["rot_bo"] = i["L0_attn_wo_b"]
    half = HD // 2
    scale = np.float32(2500.0) ** (np.float32(2.0) * np.arange(half, dtype=np.float32) / np.float32(HD))
    angle = np.arange(1, S + 1, dtype=np.float32)[None, :] / scale[:, None].astype(np.float32)
    cos, sin = np.cos(angle).astype(np.float32), np.sin(angle).astype(np.float32)
    a["cos"] = np.tile(np.concatenate([cos, cos]), (P // HD, 1))
    a["sin"] = np.tile(np.concatenate([-sin, sin]), (P // HD, 1))
    a["top_w"] = _split_rows(np.concatenate([i[f"L1_attn_W{x}"].T for x in "qkv"], axis=1))
    a["top_qkb"] = _columns(i["L1_attn_bq"], i["L1_attn_bk"])
    a["top_vb"] = i["L1_attn_bv"]
    a["top_wo"] = _split_rows(i["L1_attn_Wo"].T)
    a["top_bo"] = i["L1_attn_bo"]
    a["router"] = _split_rows(i["L0_ffn_moe_router"])
    a["moe_w13"] = i["L0_ffn_moe_w13"].reshape(E, DC, P, -1).transpose(2, 1, 0, 3)
    a["moe_w2"] = i["L0_ffn_moe_w2"].reshape(E, -1, P, D).transpose(2, 1, 0, 3)
    a["gate_wi"] = _split_rows(i["L1_ffn_gate_wi"])
    a["gate_bi"] = i["L1_ffn_gate_bi"].reshape(-1, P).T
    a["gate_wo"] = i["L1_ffn_gate_wo"].reshape(-1, P, D).transpose(1, 0, 2)
    a["gate_bo"] = i["L1_ffn_gate_bo"]
    a["exp_wi"] = i["L1_ffn_exp_wi"].reshape(E, DC, P, -1).transpose(2, 1, 0, 3)
    a["exp_bi"] = i["L1_ffn_exp_bi"].reshape(E, -1, P).transpose(2, 1, 0)
    a["exp_wo"] = i["L1_ffn_exp_wo"].reshape(E, -1, P, D).transpose(2, 1, 0, 3)
    a["exp_bo"] = i["L1_ffn_exp_bo"]
    return {k: np.ascontiguousarray(v) for k, v in a.items()}


def kernel(**inputs):
    import concourse.bacc as bacc
    from concourse.bass_utils import run_bass_kernel_spmd

    nc = bacc.Bacc("TRN2", target_bir_lowering=False, num_devices=1)
    arrays = layout(inputs)
    aps = {k: nc.dram_tensor(f"in_{k}", list(v.shape), mybir.dt.from_np(v.dtype), kind="ExternalInput").ap()
           for k, v in arrays.items()}
    out = nc.dram_tensor("out", list(_OUT), F32, kind="ExternalOutput").ap()
    program(nc, aps, out)
    r = run_bass_kernel_spmd(nc, [{f"in_{k}": v for k, v in arrays.items()}], core_ids=[0])
    return r.results[0]["out"]
```
